# Optimizing a Trainium2 kernel written in Bass

```python
import numpy as np
import jax
import jax.numpy as jnp

def _softmax(x, axis=-1):
    return jax.nn.softmax(x, axis=axis)

def _gelu(x):
    return jax.nn.gelu(x, approximate=True)

def _silu(x):
    return jax.nn.silu(x)

def _sigmoid(x):
    return jax.nn.sigmoid(x)

def _layernorm(x, axis=-1, eps=1e-05):
    m = jnp.mean(x, axis=axis, keepdims=True)
    v = jnp.var(x, axis=axis, keepdims=True)
    return (x - m) / jnp.sqrt(v + eps)

def _scatter_add(tgt, idx, src, axis=0):
    return tgt.at[idx].add(src)

def _segment_sum(src, seg, n):
    return jax.ops.segment_sum(src, seg, n)
kernel_name = 'mk_seq_preln_d2_jaxref_r8_88e21c'

def setup_inputs(seed: int=0):
    np.random.seed(seed)
    _w = jnp.asarray

    def _L0_attn_setup():
        import jax, jax.numpy as jnp
        import numpy as np
        BS, L, D, N = (4, 256, 128, 16)
        key = jax.random.key(seed)
        ks = jax.random.split(key, 8)
        s = 1.0 / np.sqrt(D)
        x = jax.random.normal(ks[0], (BS, L, D), dtype=jnp.float32)
        W1 = jax.random.uniform(ks[1], (D, D), jnp.float32, -s, s)
        b1 = jax.random.uniform(ks[2], (D,), jnp.float32, -s, s)
        W2 = jax.random.uniform(ks[3], (D, N), jnp.float32, -s, s)
        b2 = jax.random.uniform(ks[4], (N,), jnp.float32, -s, s)
        W3 = jax.random.uniform(ks[5], (D, N), jnp.float32, -s, s)
        b3 = jax.random.uniform(ks[6], (N,), jnp.float32, -s, s)
        A = jax.random.normal(ks[7], (D, N), jnp.float32) * np.sqrt(2.0 / (D + N))
        return {'x': x, 'W1': W1, 'b1': b1, 'W2': W2, 'b2': b2, 'W3': W3, 'b3': b3, 'A': A}
    _L0_attn_in = _L0_attn_setup()

    def _L0_ffn_setup():
        import jax, jax.numpy as jnp
        import numpy as np
        NUM_EXPERTS_TOTAL = 9
        TOP_K = 2
        key = jax.random.key(seed)
        k0, k1, k2, k3, k4 = jax.random.split(key, 5)
        B, S, H, I = (2, 256, 128, 352)
        E = NUM_EXPERTS_TOTAL
        x = jax.random.normal(k0, (B, S, H), dtype=jnp.float32)
        Wr = jax.random.normal(k1, (H, E), dtype=jnp.float32) * 0.02
        Wg = jax.random.normal(k2, (E, H, I), dtype=jnp.float32) * 0.02
        Wu = jax.random.normal(k3, (E, H, I), dtype=jnp.float32) * 0.02
        Wd = jax.random.normal(k4, (E, I, H), dtype=jnp.float32) * 0.02
        return {'x': x, 'Wr': Wr, 'Wg': Wg, 'Wu': Wu, 'Wd': Wd}
    _L0_ffn_in = _L0_ffn_setup()

    def _L1_attn_setup():
        import jax, jax.numpy as jnp
        import numpy as np
        HEADS = 16
        LN_EPS = 1e-05

        def _ln(v, w, b):
            mu = jnp.mean(v, axis=-1, keepdims=True)
            var = jnp.mean(jnp.square(v - mu), axis=-1, keepdims=True)
            return (v - mu) * jax.lax.rsqrt(var + LN_EPS) * w + b
        key = jax.random.key(seed)
        ks = jax.random.split(key, 5)
        b, t, e = (2, 256, 128)
        x = jax.random.normal(ks[0], (b, t, e), dtype=jnp.float32)
        scale = 0.02
        Wk = jax.random.normal(ks[1], (e, e), dtype=jnp.float32) * scale
        Wq = jax.random.normal(ks[2], (e, e), dtype=jnp.float32) * scale
        Wv = jax.random.normal(ks[3], (e, e), dtype=jnp.float32) * scale
        Wu = jax.random.normal(ks[4], (e, e), dtype=jnp.float32) * scale
        s = e // HEADS
        return {'x': x, 'Wk': Wk, 'Wq': Wq, 'Wv': Wv, 'Wu': Wu, 'kln_w': jnp.ones((s,), jnp.float32), 'kln_b': jnp.zeros((s,), jnp.float32), 'qln_w': jnp.ones((s,), jnp.float32), 'qln_b': jnp.zeros((s,), jnp.float32)}
    _L1_attn_in = _L1_attn_setup()

    def _L1_ffn_setup():
        import jax, jax.numpy as jnp
        import numpy as np
        TOP_K = 8
        key = jax.random.key(seed)
        ks = jax.random.split(key, 6)
        B, S, D, F, E = (2, 128, 128, 64, 64)
        x = jax.random.normal(ks[0], (B, S, D), dtype=jnp.float32)
        centroids = jax.random.normal(ks[1], (E, D), dtype=jnp.float32) * 0.05
        expert_biases = jnp.zeros((E,), dtype=jnp.float32)
        Ws_up = jax.random.normal(ks[2], (D, F), dtype=jnp.float32) / np.sqrt(D)
        Ws_down = jax.random.normal(ks[3], (F, D), dtype=jnp.float32) / np.sqrt(F)
        W_up = jax.random.normal(ks[4], (E, D, F), dtype=jnp.float32) / np.sqrt(D)
        W_down = jax.random.normal(ks[5], (E, F, D), dtype=jnp.float32) / np.sqrt(F)
        return {'x': x, 'centroids': centroids, 'expert_biases': expert_biases, 'Ws_up': Ws_up, 'Ws_down': Ws_down, 'W_up': W_up, 'W_down': W_down}
    _L1_ffn_in = _L1_ffn_setup()
    _d = {'L0_attn_x': _L0_attn_in['x'], 'L0_attn_W1': _L0_attn_in['W1'], 'L0_attn_b1': _L0_attn_in['b1'], 'L0_attn_W2': _L0_attn_in['W2'], 'L0_attn_b2': _L0_attn_in['b2'], 'L0_attn_W3': _L0_attn_in['W3'], 'L0_attn_b3': _L0_attn_in['b3'], 'L0_attn_A': _L0_attn_in['A'], 'L0_ffn_Wr': _L0_ffn_in['Wr'], 'L0_ffn_Wg': _L0_ffn_in['Wg'], 'L0_ffn_Wu': _L0_ffn_in['Wu'], 'L0_ffn_Wd': _L0_ffn_in['Wd'], 'L1_attn_Wk': _L1_attn_in['Wk'], 'L1_attn_Wq': _L1_attn_in['Wq'], 'L1_attn_Wv': _L1_attn_in['Wv'], 'L1_attn_Wu': _L1_attn_in['Wu'], 'L1_attn_kln_w': _L1_attn_in['kln_w'], 'L1_attn_kln_b': _L1_attn_in['kln_b'], 'L1_attn_qln_w': _L1_attn_in['qln_w'], 'L1_attn_qln_b': _L1_attn_in['qln_b'], 'L1_ffn_centroids': _L1_ffn_in['centroids'], 'L1_ffn_expert_biases': _L1_ffn_in['expert_biases'], 'L1_ffn_Ws_up': _L1_ffn_in['Ws_up'], 'L1_ffn_Ws_down': _L1_ffn_in['Ws_down'], 'L1_ffn_W_up': _L1_ffn_in['W_up'], 'L1_ffn_W_down': _L1_ffn_in['W_down']}
    _x0 = _d['L0_attn_x']
    _d['L0_attn_x'] = jax.random.normal(jax.random.fold_in(jax.random.key(seed), 1), (16, 256, 128), dtype=_x0.dtype)
    del _x0
    return _d

def reference(L0_attn_x, L0_attn_W1, L0_attn_b1, L0_attn_W2, L0_attn_b2, L0_attn_W3, L0_attn_b3, L0_attn_A, L0_ffn_Wr, L0_ffn_Wg, L0_ffn_Wu, L0_ffn_Wd, L1_attn_Wk, L1_attn_Wq, L1_attn_Wv, L1_attn_Wu, L1_attn_kln_w, L1_attn_kln_b, L1_attn_qln_w, L1_attn_qln_b, L1_ffn_centroids, L1_ffn_expert_biases, L1_ffn_Ws_up, L1_ffn_Ws_down, L1_ffn_W_up, L1_ffn_W_down):

    def _L0_attn_ref(x, W1, b1, W2, b2, W3, b3, A):
        import jax, jax.numpy as jnp
        import numpy as np
        BS, L, D, N = (4, 256, 128, 16)
        B = x @ W2 + b2
        C = x @ W3 + b3
        delta = jax.nn.softplus(x @ W1 + b1)
        dB = jnp.einsum('bld,bln->bldn', delta, B)
        h = x[..., None] * dB
        y = jnp.einsum('bln,bldn->bld', C, h)
        return y

    def _L0_ffn_ref(x, Wr, Wg, Wu, Wd):
        import jax, jax.numpy as jnp
        import numpy as np
        NUM_EXPERTS_TOTAL = 9
        TOP_K = 2
        B, S, H = x.shape
        E = NUM_EXPERTS_TOTAL
        T = B * S
        logits = jnp.einsum('bsh,he->bse', x, Wr)
        probs = jax.nn.softmax(logits, axis=-1)
        topk_w, topk_idx = jax.lax.top_k(probs, TOP_K)
        topk_w = topk_w / jnp.sum(topk_w, axis=-1, keepdims=True)
        xf = x.reshape(T, H)
        wf = topk_w.reshape(T, TOP_K)
        idxf = topk_idx.reshape(T, TOP_K)
        cw = jnp.zeros((T, E), dtype=x.dtype).at[jnp.arange(T)[:, None], idxf].add(wf)
        gate = jax.nn.silu(jnp.einsum('th,ehi->tei', xf, Wg))
        hidden = gate * jnp.einsum('th,ehi->tei', xf, Wu)
        out = jnp.einsum('tei,eih,te->th', hidden, Wd, cw)
        return out.reshape(B, S, H)

    def _L1_attn_ref(x, Wk, Wq, Wv, Wu, kln_w, kln_b, qln_w, qln_b):
        import jax, jax.numpy as jnp
        import numpy as np
        HEADS = 16
        LN_EPS = 1e-05

        def _ln(v, w, b):
            mu = jnp.mean(v, axis=-1, keepdims=True)
            var = jnp.mean(jnp.square(v - mu), axis=-1, keepdims=True)
            return (v - mu) * jax.lax.rsqrt(var + LN_EPS) * w + b
        b, t, e = x.shape
        h = HEADS
        s = e // h
        k = (x @ Wk.T).reshape(b, t, h, s)
        q = (x @ Wq.T).reshape(b, t, h, s)
        v = (x @ Wv.T).reshape(b, t, h, s)
        k = _ln(k, kln_w, kln_b)
        q = _ln(q, qln_w, qln_b)
        scalefactor = 1.0 / np.sqrt(s).astype(np.float32)
        dot = jnp.einsum('bqhs,bkhs->bhqk', q, k) * scalefactor
        causal = jnp.triu(jnp.ones((t, t), dtype=bool), k=1)
        dot = jnp.where(causal, -jnp.inf, dot)
        attn = jax.nn.softmax(dot, axis=-1)
        out = jnp.einsum('bhqk,bkhs->bqhs', attn, v).reshape(b, t, e)
        return out @ Wu.T

    def _L1_ffn_ref(x, centroids, expert_biases, Ws_up, Ws_down, W_up, W_down):
        import jax, jax.numpy as jnp
        import numpy as np
        TOP_K = 8
        B, S, D = x.shape
        E = centroids.shape[0]
        T = B * S
        xf = x.reshape(T, D)
        shared = jax.nn.silu(xf @ Ws_up) @ Ws_down
        aff = xf @ centroids.T
        biased = aff + expert_biases
        _, idx = jax.lax.top_k(biased, TOP_K)
        sel = jnp.take_along_axis(aff, idx, axis=1)
        w = jax.nn.sigmoid(sel)
        w = w / (jnp.sum(w, axis=-1, keepdims=True) + 1e-08)
        cw = jnp.zeros((T, E), dtype=x.dtype).at[jnp.arange(T)[:, None], idx].add(w)
        h = jax.nn.silu(jnp.einsum('td,edf->etf', xf, W_up))
        y = jnp.einsum('etf,efd->etd', h, W_down)
        routed = jnp.einsum('etd,te->td', y, cw)
        return (shared + routed).reshape(B, S, D)
    x = L0_attn_x
    x = x + _L0_attn_ref(_layernorm(x, axis=-1), L0_attn_W1, L0_attn_b1, L0_attn_W2, L0_attn_b2, L0_attn_W3, L0_attn_b3, L0_attn_A)
    x = x + _L0_ffn_ref(_layernorm(x, axis=-1), L0_ffn_Wr, L0_ffn_Wg, L0_ffn_Wu, L0_ffn_Wd)
    x = x + _L1_attn_ref(_layernorm(x, axis=-1), L1_attn_Wk, L1_attn_Wq, L1_attn_Wv, L1_attn_Wu, L1_attn_kln_w, L1_attn_kln_b, L1_attn_qln_w, L1_attn_qln_b)
    x = x + _L1_ffn_ref(_layernorm(x, axis=-1), L1_ffn_centroids, L1_ffn_expert_biases, L1_ffn_Ws_up, L1_ffn_Ws_down, L1_ffn_W_up, L1_ffn_W_down)
    return x

_drawn_inputs = setup_inputs


def setup_inputs(seed=0):
    import zlib

    import numpy as np

    out = dict(_drawn_inputs(seed))
    spreads = {'L1_attn_kln_w': (1.0, 0.6),
     'L1_attn_kln_b': (0.0, 0.8),
     'L1_attn_qln_w': (1.0, 0.6),
     'L1_attn_qln_b': (0.0, 0.8),
     'L1_ffn_expert_biases': (0.0, 0.1)}
    factors = {'L0_ffn_Wr': 4.292,
     'L0_ffn_Wg': 3.816,
     'L0_ffn_Wu': 3.814,
     'L0_ffn_Wd': 3.883,
     'L1_attn_Wk': 3.52,
     'L1_attn_Wq': 3.582,
     'L1_attn_Wv': 2.97,
     'L1_attn_Wu': 2.997}
    for name, (base, spread) in spreads.items():
        noise = np.random.default_rng([zlib.crc32(name.encode()), seed]).standard_normal(out[name].shape)
        drawn = base * np.exp(spread * noise) if base else spread * noise
        out[name] = jnp.asarray(drawn.astype(out[name].dtype))
    for name, factor in factors.items():
        out[name] = (out[name] * factor).astype(out[name].dtype)
    return out
```

```python
from contextlib import ExitStack

import concourse.bass as bass
from concourse import mybir

F32 = mybir.dt.float32
F32R = mybir.dt.float32r
BF16 = mybir.dt.bfloat16
I32 = mybir.dt.int32
ALU = mybir.AluOpType
ACT = mybir.ActivationFunctionType
AX = mybir.AxisListType
ds = bass.ds

P = 128
LN_EPS = 1e-5
BIG = 1.0e30


def apart(eng, passed):
    eng.sem_inc(passed, 1)


class Tickets:

    def __init__(self, eng, sem, base=0):
        self.eng, self.sem, self.base, self.n = eng, sem, base, 0

    def done(self, ins):
        ins.then_inc(self.sem, 1)
        self.n += 1
        return self.n

    def need(self, ticket):
        self.eng.wait_ge(self.sem, self.base + ticket)

    def link(self, ins):
        self.need(self.done(ins))


def bass_two_layers(nc, x, W1, b1, W2, b2, W3, b3, Wr, Wg, Wu, Wd, WkT, WqT, WvT, WuT, kln_w, kln_b, qln_w, qln_b,
                    cent, ebias, Ws_up, Ws_down, W_up, W_down, out):
    B, L, D = x.shape
    T = B * L
    NT = T // P
    N = W2.shape[1]
    M1 = D + 2 * N
    E1, _, I1 = Wg.shape
    JC = -(-I1 // P)
    IP = JC * P
    K1 = 2
    SUB = 4
    NPIECE = NT // SUB
    REG = T + P
    NBLK = T * K1 // P + E1 - 1
    NBLK = -(-NBLK // 4) * 4
    assert D == P and NPIECE % 2 == 0

    x_tok = x.rearrange("b (u p) d -> p (b u) d", p=P)
    out_tok = out.rearrange("b (u p) d -> p (b u) d", p=P)

    xs = nc.dram_tensor("xs", [E1 * REG, D], F32).ap()
    ys = nc.dram_tensor("ys", [NBLK * P, D], F32).ap()

    with ExitStack() as ctx:
        def sb(name, shape, dt):
            return ctx.enter_context(nc.sbuf_tensor(name, shape, dt))

        def sem(name):
            return ctx.enter_context(nc.semaphore(name))

        ps = ctx.enter_context(nc.psum_tensor("ps", [P, 8, 512], F32))
        bank = [ps[:, i, :] for i in range(8)]

        x_res = sb("x_res", [P, NT, D], F32)
        ident = sb("ident", [P, P], F32)
        eps_c = sb("eps_c", [P, 1], F32)
        st = sb("st", [P, 2, SUB, 6], F32)
        mv = sb("mv", [P, 2, SUB, 2], F32)
        lnv = sb("lnv", [P, 2, SUB], F32)
        rstd = sb("rstd", [P, 2, SUB], F32)
        xnT = sb("xnT", [P, 2, SUB, P], F32)
        wgt = sb("wgt", [P, NT, K1], F32)
        gpi = sb("gpi", [P, NT * K1], I32)
        gps = sb("gps", [P, 2, 2 * K1], I32)
        yg = sb("yg", [P, 4, K1, D], F32)
        first = ExitStack()

        def sb1(name, shape, dt):
            return first.enter_context(nc.sbuf_tensor(name, shape, dt))

        w123 = sb1("w123", [P, M1], F32)
        bias = sb1("bias", [P, 2, M1], F32)
        tri = sb1("tri", [P, P], BF16)
        ones = sb1("ones", [P, P], BF16)
        trif = sb1("trif", [P, P], F32)
        zrow = sb1("zrow", [P, P], F32)
        wr_s = sb1("wr_s", [P, E1], F32)
        rev9 = sb1("rev9", [P, SUB, E1], F32)
        off9 = sb1("off9", [P, E1], F32)
        prow = sb1("prow", [P, E1], F32)
        iblk = sb1("iblk", [P, NBLK], F32)
        xn = sb1("xn", [P, 2, SUB, D], F32)
        xm = sb1("xm", [P, 2, SUB, D], F32)
        z = sb1("z", [P, 2, SUB, M1], F32)
        sp = sb1("sp", [P, 2, 3, SUB, D], F32)
        bc = sb1("bc", [P, 2, SUB, N], F32)
        bcs = sb1("bcs", [P, 2, SUB], F32)
        lg = sb1("lg", [P, 2, SUB, E1], F32)
        r9 = sb1("r9", [P, 2, 5, SUB, E1], F32)
        r1 = sb1("r1", [P, 2, 8, SUB], F32)
        sel = sb1("sel", [P, 2, SUB, E1], BF16)
        pick = sb1("pick", [P, NT, K1, E1], F32)
        posf = sb1("posf", [P, NT, K1], F32)
        posi = sb1("posi", [P, 2, SUB, K1], I32)
        base = sb1("base", [P, E1], F32)
        stg = sb1("stg", [P, E1 * I1], F32)
        stu = sb1("stu", [P, E1 * I1], F32)
        std = sb1("std", [P, E1 * JC * D], F32)
        wgh = sb1("wgh", [P, E1 * I1], F32R)
        wgl = sb1("wgl", [P, E1 * I1], F32R)
        wuh = sb1("wuh", [P, E1 * I1], F32R)
        wul = sb1("wul", [P, E1 * I1], F32R)
        wdh = sb1("wdh", [P, E1 * JC * D], F32R)
        wdl = sb1("wdl", [P, E1 * JC * D], F32R)
        cnti = sb1("cnti", [P, E1], I32)
        nblk = sb1("nblk", [P, E1], F32)
        bend = sb1("bend", [P, E1], F32)
        bstart = sb1("bstart", [P, E1], F32)
        q9 = sb1("q9", [P, 3, E1], F32)
        tail = sb1("tail", [P, E1], I32)
        b9 = sb1("b9", [P, 3, NBLK, E1], F32)
        bf = sb1("bf", [P, 3, NBLK], F32)
        blk_src = sb1("blk_src", [P, NBLK], I32)
        blk_e = sb1("blk_e", [P, NBLK], I32)
        gp9 = sb1("gp9", [P, NT * K1, E1], F32)
        gpf = sb1("gpf", [P, NT * K1], F32)
        xb = sb1("xb", [P, 4, D], F32)
        xbh = sb1("xbh", [P, 2, D], F32R)
        xbl = sb1("xbl", [P, 2, D], F32R)
        sg = sb1("sg", [P, 2, I1], F32)
        hb = sb1("hb", [P, 2, IP], F32)
        hh = sb1("hh", [P, 2, IP], F32R)
        hl = sb1("hl", [P, 2, IP], F32R)
        yb = sb1("yb", [P, 4, D], F32)

        first.close()

        E2, F2 = cent.shape[1], W_up.shape[2]
        K2 = 8
        NP2 = E2 * F2 // P
        WC = 512
        TT = 4 * P
        NC = (E2 * F2 + NP2 * D) // WC
        assert NC == B and 2 * F2 == P
        wh = sb("wh", [P, E2 * F2 + NP2 * D], F32R)
        wl = sb("wl", [P, E2 * F2 + NP2 * D], F32R)
        wst = sb("wst", [P, 2, WC], F32)
        shf = sb("shf", [P, F2 + D], F32)
        shh = sb("shh", [P, F2 + D], F32R)
        shl = sb("shl", [P, F2 + D], F32R)
        cen_s = sb("cen_s", [P, E2], F32)
        ebi = sb("ebi", [P, E2], F32)
        attn = ExitStack()

        def sb2(name, shape, dt):
            return attn.enter_context(nc.sbuf_tensor(name, shape, dt))

        H = 16
        S = D // H
        HW = 32
        KS = 3 * S
        wqkv = sb2("wqkv", [P, 3 * D], F32)
        wqh = sb2("wqh", [P, 3 * D], F32R)
        wql = sb2("wql", [P, 3 * D], F32R)
        wuT = sb2("wuT", [P, D], F32)
        ln8 = sb2("ln8", [P, 4, S], F32)
        lnw = sb2("lnw", [P, 2, H, S], F32)
        lnb = sb2("lnb", [P, 2, H, S], F32)
        identb = sb2("identb", [P, P], BF16)
        mskf = sb2("mskf", [P, 2, 2, P], F32)
        msk = sb2("msk", [P, 2, 2, P], BF16)
        cst = sb2("cst", [P, 2, 6], F32)
        cmv = sb2("cmv", [P, 2, 2], F32)
        cln = sb2("cln", [P, 2], F32)
        crs = sb2("crs", [P, 2], F32)
        xc = sb2("xc", [P, 2, D], F32)
        xch = sb2("xch", [P, 2, P], F32R)
        xcl = sb2("xcl", [P, 2, P], F32R)
        zs = sb2("zs", [P, 2, 2, 3 * D], F32)
        ms = sb2("ms", [P, 2, 2 * H], F32)
        cen = sb2("cen", [P, 2, 2 * D], F32)
        csq = sb2("csq", [P, 2, 2 * D], F32)
        vsm = sb2("vsm", [P, 2, 2 * H], F32)
        rql = sb2("rql", [P, 2, 2 * H], F32)
        rq = sb2("rq", [P, 2, 2 * H], F32)
        nq = sb2("nq", [P, 3, 2, 2 * D], F32)
        nqh = sb2("nqh", [P, 2, 2 * D], F32R)
        qs = sb2("qs", [P, 2, 2, H, HW], F32)
        ks = sb2("ks", [P, 2, 2, H, HW], F32)
        vp = sb2("vp", [P, 2, 2, H, HW], F32)
        qT = sb2("qT", [P, 4, 2 * P], F32R)
        qT2 = sb2("qT2", [P, 2, 4, 2 * P], F32R)
        kT = sb2("kT", [P, 2, 4, 2 * P], F32R)
        nm = sb2("nm", [P, 2, H], F32)
        nmh = sb2("nmh", [P, 2, H], F32R)
        pt = sb2("pt", [P, 4, 3 * P], F32)
        ot = sb2("ot", [P, 2, 4, 2 * P], F32)
        rc = sb2("rc", [P, 2, H], F32)
        oo = sb2("oo", [P, 2, D], F32)
        ooT = sb2("ooT", [P, 2, P], F32)

        attn.close()

        xh4 = sb("xh4", [P, T], F32R)
        xl4 = sb("xl4", [P, T], F32R)
        cwT = sb("cwT", [P, T], F32R)
        selr = sb("selr", [P, E2 * F2], F32R)
        route = ExitStack()

        def sb3(name, shape, dt):
            return route.enter_context(nc.sbuf_tensor(name, shape, dt))

        selz = sb3("selz", [P, E2, F2], F32)
        xm4 = sb3("xm4", [P, 2, SUB, D], F32)
        af = sb3("af", [P, 2, SUB, E2], F32)
        bi = sb3("bi", [P, 2, SUB, E2], F32)
        m8 = sb3("m8", [P, 2, SUB, 8], F32)
        mr = sb3("mr", [P, 2, SUB, E2], F32)
        g4 = sb3("g4", [P, 2, 5, SUB, E2], F32)
        s4 = sb3("s4", [P, 2, 3, SUB], F32)
        cwh = sb3("cwh", [P, 2, SUB, E2], F32R)
        cs = sb3("cs", [P, 2, SUB, 2 * E2], F32)
        route.close()
        sg4 = sb("sg4", [P, 3, TT], F32)
        h4 = sb("h4", [P, 3, TT], F32)
        hh4 = sb("hh4", [P, 3, TT], F32R)
        hl4 = sb("hl4", [P, 3, TT], F32R)
        oT4 = sb("oT4", [P, TT], F32)
        y4 = sb("y4", [P, 2, SUB, D], F32)
        NU = NP2 + 1

        x_in = sem("x_in")
        small_in = sem("small_in")
        wg_in, wu_in, wd_in = sem("wg_in"), sem("wu_in"), sem("wd_in")
        w_hi, w_lo = sem("w_hi"), sem("w_lo")
        consts = sem("consts")
        pool_own, dve_own, act_own = sem("pool_own"), sem("dve_own"), sem("act_own")
        dve_passed, pool_passed = sem("dve_passed"), sem("pool_passed")
        mv1, rs1, xn1, tr1, tc1, zz1, zc1, sp1 = (sem(n) for n in (
            "ln1_stats", "ln1_rstd", "ln1_out", "ln1_T", "ln1_T_copied", "mix_z", "mix_z_copied", "mix_softplus"))
        mv2, rs2, xn2, tr2, tc2, lg2, df2, ex2, sl2, rk2, ps2 = (sem(n) for n in (
            "ln2_stats", "ln2_rstd", "ln2_out", "ln2_T", "ln2_T_copied", "r1_logits", "r1_diff", "r1_exp",
            "r1_sel", "r1_rank", "r1_pos"))
        scat = [sem("scat0"), sem("scat1")]
        scat_ok = [sem("scat_ok0"), sem("scat_ok1")]
        tails = sem("tails")
        tails_in = sem("tails_in")
        list_ready = sem("list_ready")
        xb_in = [sem(f"xb_in{u}") for u in range(4)]
        ys_out = [sem(f"ys_out{u}") for u in range(4)]
        xT_r, xh_r, xl_r, gu_r, sg_r, h_r, hT_r, hh_r, hl_r, y_r, yb_r = (sem(n) for n in (
            "blk_xT", "blk_xh", "blk_xl", "blk_gu", "blk_silu", "blk_h", "blk_hT", "blk_hh", "blk_hl", "blk_y", "blk_yb"))
        yg_in = [sem(f"yg_in{u}") for u in range(4)]
        x2_half, x2_r = sem("x2_first_row"), sem("x2_ready")
        gps_r = sem("batch_rows")
        gp_r = sem("gather_rows")
        o_out = [sem("o_out0"), sem("o_out1")]
        w_in = [sem("w_in0"), sem("w_in1")]
        wd_done, sh_in, sh_done, d_const, d_sel, act_passed = (sem(n) for n in (
            "w2_parts", "shared_in", "shared_parts", "d_const", "d_sel", "act_passed"))
        act_d, dve_d = sem("act_d"), sem("dve_d")
        d_mv, d_rs, d_xn, d_T, d_Tc, d_hl, d_af, d_afc, d_ex, d_cs, d_cT, d_cw = (sem(n) for n in (
            "ln4_stats", "ln4_rstd", "ln4_out", "ln4_T", "ln4_T_copied", "x4_parts", "r2_logits", "r2_copied", "r2_exp",
            "r2_weights", "r2_T", "r2_done"))
        u_up, u_cw, u_sg, u_h, u_hh, u_hl, u_dn, u_oT, u_y, u_T = (sem(n) for n in (
            "e_up", "e_weight", "e_silu", "e_h", "e_hh", "e_hl", "e_down", "e_outT", "e_y", "e_out_T"))
        c_in, c_const, c_w = sem("c_in"), sem("c_const"), sem("c_w")
        act_c, dve_c1, dve_cf, pool_c = sem("act_c"), sem("dve_c1"), sem("dve_cf"), sem("pool_c")
        c_mv, c_rs, c_xn, c_xT, c_xh, c_xl, c_z, c_zs, c_cen, c_sq, c_vs, c_rq, c_n, c_wb, c_nh, c_lo, c_dup, c_vp = (
            sem(n) for n in ("ln3_stats", "ln3_rstd", "ln3_out", "ln3_T", "ln3_T_hi", "ln3_T_lo", "qkv", "qkv_copied",
                             "qk_centred", "qk_squares", "qk_vars", "qk_rstd", "qk_scaled", "qk_affine", "qk_hi", "qk_lo",
                             "qk_spread", "v_spread"))
        c_T, c_qT, c_kT, c_S1, c_mx, c_nm, c_T2, c_q2, c_S2, c_P, c_PV, c_OT, c_F1, c_F2, c_F3, c_F4, c_F5, c_F6 = (
            sem(n) for n in ("qk_T", "q_T_copied", "k_T_copied", "scores_q", "row_max", "max_spread", "q2_T", "q2_T_copied",
                             "scores_k", "probs", "pv", "pv_copied", "att_T", "att_norm", "att_T2", "att_T2_copied",
                             "att_proj", "x3"))

        R1 = I1 - (JC - 1) * P
        stv, hv, lv = (w[:, 0:E1 * JC * D].rearrange("p (e j d) -> p e j d", e=E1, j=JC) for w in (std, wdh, wdl))
        ACT_A, DVE_A, DVE_D = 8, 78, 46

        pool_w, act_c2, dve_nm = sem("pool_w"), sem("act_c2"), sem("dve_nm")
        pool_h, u_sg0 = sem("pool_h"), sem("e_silu_shared")

        def both4(op, q, own):
            was = list(q)
            for s in range(2):
                own.need(was[s])
                q[s] = own.done(op(s))

        def tiles_of(eng, tile):
            tile(0, 0, None)
            tile(1, 1, (0, 0, 0))
            with eng.Fori(1, T // TT // 2) as it:
                tile(it * 2, 0, (it * 2 - 1, 1, it - 1))
                tile(it * 2 + 1, 1, (it * 2, 0, it))

        def rows(h, n):
            return slice((h % 4) * HW, (h % 4) * HW + n)

        def heads4(v, c):
            return v[:, :, c * D:(c + 1) * D].rearrange("p u (h s) -> p u h s", h=H)

        def over_tiles(w):
            return w[:, :, :, :].rearrange("p c h s -> p (c h s)").unsqueeze(1).broadcast_to([P, 2, 2 * D])

        def heads_of(w, c):
            return w[:, :, c * D:(c + 1) * D].rearrange("p u (h s) -> p u h s", h=H)

        def turns(turn, eng):
            turn(-2, -1, 0, False, False, False, True, True)
            turn(-1, -1, 1, False, False, True, True, True)
            turn(0, 0, 0, True, False, True, True, True)
            with eng.Fori(0, (B - 4) // 2) as it:
                turn(it * 2 + 1, it, 1, True, True, True, True, True)
                turn(it * 2 + 2, it + 1, 0, True, True, True, True, True)
            turn(B - 3, (B - 3) // 2, 1, True, True, True, True, False)
            turn(B - 2, (B - 2) // 2, 0, True, True, True, False, False)
            turn(B - 1, (B - 1) // 2, 1, True, True, False, False, False)
            turn(B, B // 2, 0, False, True, False, False, False)

        block = ctx.enter_context(nc.Block())

        @block.sync
        def _(sp_):
            for i in range(4):
                n = NT // 4
                sp_.dma_start(x_res[:, i * n:(i + 1) * n, :], x_tok[:, i * n:(i + 1) * n, :]).then_inc(x_in, 16)
            for o, src in ((0, W1), (D, W2), (D + N, W3)):
                sp_.dma_start(w123[:, o:o + src.shape[1]], src).then_inc(small_in, 16)
            for r in range(2):
                for o, src in ((0, b1), (D, b2), (D + N, b3)):
                    n = src.shape[0]
                    sp_.dma_start(bias[:, r, o:o + n],
                                  src.rearrange("(a n) -> a n", a=1).broadcast_to([P, n])).then_inc(small_in, 16)
            sp_.dma_start(wr_s[:, :], Wr).then_inc(small_in, 16)
            for dst, src, arrived in ((stg, Wg, wg_in), (stu, Wu, wu_in)):
                sp_.dma_start(dst[:, :].rearrange("p (e i) -> p e i", e=E1), src.rearrange("e d i -> d e i")).then_inc(arrived, 16)
            for j in range(JC - 1):
                sp_.dma_start(stv[:, :, j, :], Wd[:, j * P:(j + 1) * P, :].rearrange("e p d -> p e d")).then_inc(wd_in, 16)
            sp_.dma_start(stv[0:R1, :, JC - 1, :],
                          Wd[:, (JC - 1) * P:I1, :].rearrange("e p d -> p e d")).then_inc(wd_in, 16)

            def load_block(b, u):
                src = sp_.value_load(blk_src[0:1, ds(b, 1)], min_val=0, max_val=(E1 - 1) * REG + T)
                sp_.dma_start(xb[:, u, :], xs[ds(src, P), :]).then_inc(xb_in[u], 16)

            for u in range(4):
                sp_.sem_inc(ys_out[u], 16)

            def store_block(b, u):
                sp_.wait_ge(yb_r, b + 1)
                sp_.dma_start(ys[ds(b * P, P), :], yb[:, u, :]).then_inc(ys_out[u], 16)

            sp_.wait_ge(list_ready, 1)
            for s in range(2):
                sp_.wait_ge(scat[s], 16 * (SUB * K1 * NPIECE // 2))
            sp_.wait_ge(tails_in, 16 * E1)
            for b in range(4):
                load_block(b, b)
            for b in range(4):
                sp_.wait_ge(xT_r, b + 1)
                load_block(b + 4, b)
                if b >= 2:
                    store_block(b - 2, b - 2)
            with sp_.Fori(1, NBLK // 4 - 1) as it:
                for u in range(4):
                    b = it * 4 + u
                    sp_.wait_ge(xT_r, b + 1)
                    load_block(b + 4, u)
                    store_block(b - 2, (u - 2) % 4)
            for b in range(NBLK - 6, NBLK):
                store_block(b, b % 4)
            for u in range(4):
                sp_.wait_ge(ys_out[u], 16 * (NBLK // 4 + 1))
            for j, w in enumerate((WqT, WkT, WvT)):
                sp_.dma_start(wqkv[:, j * D:(j + 1) * D], w).then_inc(c_in, 16)
            sp_.dma_start(wuT[:, :], WuT).then_inc(c_in, 16)
            for j, w in enumerate((qln_w, kln_w, qln_b, kln_b)):
                sp_.dma_start(ln8[:, j, :], w.rearrange("(a n) -> a n", a=1).broadcast_to([P, S])).then_inc(c_in, 16)
            sp_.dma_start(shf[:, 0:F2], Ws_up).then_inc(sh_in, 16)
            sp_.dma_start(shf[0:F2, F2:F2 + D], Ws_down).then_inc(sh_in, 16)
            sp_.dma_start(cen_s[:, :], cent).then_inc(sh_in, 16)
            sp_.dma_start(ebi[:, :], ebias.rearrange("(a n) -> a n", a=1).broadcast_to([P, E2])).then_inc(sh_in, 16)
            PC = WC // D
            for c in range(NC):
                if c >= 2:
                    sp_.wait_ge(wd_done, c - 1)
                for q in range(PC):
                    pair = (c % (NC // 2)) * PC + q
                    dst = wst[:, c % 2, q * D:(q + 1) * D]
                    if c < NC // 2:
                        sp_.dma_start(dst.rearrange("p (two f) -> p two f", two=2),
                                      W_up[2 * pair:2 * pair + 2].rearrange("two d f -> d two f")).then_inc(w_in[c % 2], 16)
                    else:
                        sp_.dma_start(dst, W_down[2 * pair:2 * pair + 2].rearrange("two f d -> (two f) d")).then_inc(w_in[c % 2], 16)
            for p in range(2):
                sp_.sem_inc(o_out[p], 16)
            for t in range(T // TT):
                sp_.wait_ge(u_y, t + 1)
                sp_.dma_start(out_tok[:, t * SUB:(t + 1) * SUB, :], y4[:, t % 2, :, :]).then_inc(o_out[t % 2], 16)
            for p in range(2):
                sp_.wait_ge(o_out[p], 16 * ((T // TT) // 2 + 1))

        @block.gpsimd
        def _(pool):
            own = Tickets(pool, pool_own)
            own.done(pool.memset(ident[:, :], 0.0))
            own.done(pool.memset(trif[:, :], 1.0))
            own.done(pool.memset(eps_c[:, :], LN_EPS))
            own.done(pool.memset(zrow[:, :], 0.0))
            own.done(pool.memset(base[:, :], 0.0))
            own.done(pool.memset(ones[:, :], 1.0))
            own.done(pool.memset(hb[:, :, :], 0.0))
            for dst, pattern, cm, b0 in ((rev9[:, :, :], [[0, SUB], [-1, E1]], 0, E1), (off9[:, :], [[REG, E1]], 0, 0),
                                         (prow[:, :], [[0, E1]], 1, 0), (iblk[:, :], [[1, NBLK]], 0, 0)):
                own.done(pool.iota(dst, pattern=pattern, base=b0, channel_multiplier=cm,
                                   allow_small_or_imprecise_dtypes=True))
            own.need(own.n)
            own.done(pool.affine_select(out=ident[:, :], in_=ident[:, :], compare_op=ALU.not_equal, fill=1.0,
                                        base=0, pattern=[[-1, P]], channel_multiplier=1))
            own.done(pool.affine_select(out=trif[:, :], in_=trif[:, :], compare_op=ALU.is_gt, fill=0.0,
                                        base=0, pattern=[[1, P]], channel_multiplier=-1))
            own.need(own.n)
            pool.tensor_copy(tri[:, :], trif[:, :]).then_inc(consts, 1)

            for s in range(2):
                pool.sem_inc(scat_ok[s], 1)
            with pool.Fori(0, NPIECE // 2) as it:
                for s in range(2):
                    pool.wait_ge(ps2, it * 2 + s + 1)
                    apart(pool, pool_passed)
                    for k in range(SUB):
                        for c in range(K1):
                            pool.indirect_dma_start(
                                out=xs, out_offset=bass.IndirectOffsetOnAxis(ap=posi[:, s, k, c:c + 1], axis=0),
                                in_=xm[:, s, k, :], in_offset=None).then_inc(scat[s], 16)
                for s in range(2):
                    pool.wait_ge(scat[s], (it + 1) * (16 * SUB * K1))
                    pool.sem_inc(scat_ok[s], 1)
            pool.wait_ge(tails, 1)
            for e in range(E1):
                pool.indirect_dma_start(out=xs, out_offset=bass.IndirectOffsetOnAxis(ap=tail[:, e:e + 1], axis=0),
                                        in_=zrow[:, :], in_offset=None).then_inc(tails_in, 16)

            pool.wait_ge(w_hi, 4)
            pool.tensor_tensor(lv[:, :, 0:JC - 1, :], stv[:, :, 0:JC - 1, :], hv[:, :, 0:JC - 1, :].bitcast(F32),
                               op=ALU.subtract).then_inc(w_lo, 1)
            pool.tensor_tensor(lv[0:R1, :, JC - 1, :], stv[0:R1, :, JC - 1, :], hv[0:R1, :, JC - 1, :].bitcast(F32),
                               op=ALU.subtract).then_inc(w_lo, 1)

            pool.wait_ge(gp_r, 1)
            for u in range(4):
                pool.wait_ge(ys_out[u], 16 * (NBLK // 4 + 1))
            def gather(b, p):
                if not isinstance(b, int) or b >= 2:
                    pool.wait_ge(x2_r, 2 * b - 2)
                    apart(pool, pool_passed)
                pool.tensor_copy(gps[:, p, :], gpi[:, ds(b * (2 * K1), 2 * K1)]).then_inc(gps_r, 1)
                pool.wait_ge(gps_r, b + 1)
                apart(pool, pool_passed)
                for u in range(2):
                    for c in range(K1):
                        pool.indirect_dma_start(
                            out=yg[:, 2 * p + u, c, :], out_offset=None, in_=ys,
                            in_offset=bass.IndirectOffsetOnAxis(ap=gps[:, p, u * K1 + c:u * K1 + c + 1], axis=0),
                        ).then_inc(yg_in[2 * p + u], 16)

            gather(0, 0)

            own = Tickets(pool, pool_c)
            own.done(pool.memset(identb[:, :], 0.0))
            own.done(pool.memset(mskf[:, :, :, :], 0.0))
            own.done(pool.memset(qs[:, :, :, :, :], 0.0))
            own.done(pool.memset(ks[:, :, :, :, :], 0.0))
            own.done(pool.memset(vp[:, :, :, :, :], 0.0))
            own.need(own.n)
            own.done(pool.affine_select(out=identb[:, :], in_=identb[:, :], compare_op=ALU.not_equal, fill=1.0,
                                        base=0, pattern=[[-1, P]], channel_multiplier=1))
            own.done(pool.affine_select(out=mskf[:, 0, :, :], in_=mskf[:, 0, :, :], compare_op=ALU.is_ge, fill=-BIG,
                                        base=0, pattern=[[0, 2], [-1, P]], channel_multiplier=1))
            own.done(pool.affine_select(out=mskf[:, 1, :, :], in_=mskf[:, 1, :, :], compare_op=ALU.is_ge, fill=-BIG,
                                        base=0, pattern=[[0, 2], [1, P]], channel_multiplier=-1))
            own.done(pool.memset(ks[:, :, :, :, KS:KS + 2], 1.0))
            own.done(pool.memset(vp[:, :, :, :, S:S + 1], 1.0))
            own.need(own.n)
            pool.tensor_copy(msk[:, :, :, :], mskf[:, :, :, :]).then_inc(c_const, 1)

            def p1_pool(b, p):
                pool.wait_ge(c_n, b + 1)
                pool.tensor_tensor(nq[:, 1, :, :], nq[:, 0, :, :], over_tiles(lnw), op=ALU.mult).then_inc(pool_w, 1)
                pool.wait_ge(pool_w, b + 1)
                pool.tensor_tensor(nq[:, 2, :, :], nq[:, 1, :, :], over_tiles(lnb), op=ALU.add).then_inc(c_wb, 1)

            def p1_spread(b, p):
                pool.wait_ge(c_nh, b + 1)
                apart(pool, pool_passed)
                for dst, c, o in ((qs, 0, 0), (qs, 0, S), (ks, 1, 0), (ks, 1, 2 * S)):
                    ins = pool.tensor_copy(dst[:, p, :, :, o:o + S], heads_of(nqh, c).bitcast(F32))
                ins.then_inc(c_dup, 1)

            def p2_pool(b, p):
                if not isinstance(b, int) or b >= 2:
                    pool.wait_ge(c_PV, (b - 1) * H)
                    apart(pool, pool_passed)
                pool.tensor_copy(vp[:, p, :, :, 0:S],
                                 zs[:, p, :, 2 * D:3 * D].rearrange("p u (h s) -> p u h s", h=H)).then_inc(c_vp, 1)

            def parts(c, p, loads):
                pool.wait_ge(w_in[p], loads)
                apart(pool, pool_passed)
                pool.tensor_copy(wh[:, ds(c * WC, WC)], wst[:, p, :]).then_inc(pool_h, 1)
                pool.wait_ge(pool_h, c + 1)
                apart(pool, pool_passed)
                pool.tensor_tensor(wl[:, ds(c * WC, WC)], wst[:, p, :], wh[:, ds(c * WC, WC)].bitcast(F32),
                                   op=ALU.subtract).then_inc(wd_done, 1)

            def pool_turn(i, half, p, E, F, M, P1, G):
                if G:
                    gather(i + 3, 1 - p)
                if M:
                    p2_pool(i + 1, 1 - p)
                if E:
                    parts(i, p, (half + 1) * (16 * WC // D))
                if P1:
                    p1_pool(i + 2, p)
                    p1_spread(i + 2, p)

            turns(pool_turn, pool)
            pool.wait_ge(sh_in, 16 * 4)
            for rows_, cols in ((slice(0, P), slice(0, F2)), (slice(0, F2), slice(F2, F2 + D))):
                pool.tensor_copy(shh[rows_, cols], shf[rows_, cols]).then_inc(sh_done, 1)
            pool.wait_ge(sh_done, 2)
            for rows_, cols in ((slice(0, P), slice(0, F2)), (slice(0, F2), slice(F2, F2 + D))):
                pool.tensor_tensor(shl[rows_, cols], shf[rows_, cols], shh[rows_, cols].bitcast(F32),
                                   op=ALU.subtract).then_inc(sh_done, 1)
            pool.wait_ge(c_F6, B)
            pool.memset(selz[:, :, :], 0.0).then_inc(d_const, 1)
            for k in range(2):
                pool.wait_ge(d_const, k + 1)
                pool.affine_select(out=selz[:, :, :], in_=selz[:, :, :], compare_op=ALU.not_equal, fill=1.0,
                                   base=-k * E2, pattern=[[-1, E2], [0, F2]], channel_multiplier=1).then_inc(d_const, 1)

        @block.scalar
        def _(act):
            TABLE = "natural_log_exp_and_others"
            act.preload_act_table_set(TABLE)
            act.wait_ge(consts, 1)

            def rstd_of(ready, stats, s, i):
                act.wait_ge(stats, i)
                own.link(act.activation(lnv[:, s, :], mv[:, s, :, 1], ACT.Ln, bias=eps_c[:, 0:1]))
                act.activation(rstd[:, s, :], lnv[:, s, :], ACT.Exp, scale=-0.5).then_inc(ready, 1)

            def copy_T(ready, made, s, i):
                act.wait_ge(made, i)
                act.activation(xnT[:, s, :, :].rearrange("p k d -> p (k d)"), bank[s][:, :], ACT.Copy).then_inc(ready, 1)

            with act.Fori(0, NPIECE // 2) as it:
                act.preload_act_table_set(TABLE)
                own = Tickets(act, act_own, it * ACT_A)
                for s in range(2):
                    rstd_of(rs1, mv1, s, it * 2 + s + 1)
                for s in range(2):
                    copy_T(tc1, tr1, s, it * 2 + s + 1)
                q = []
                for s in range(2):
                    act.wait_ge(zc1, it * 2 + s + 1)
                    q.append(own.done(act.activation(sp[:, s, 0, :, :], z[:, s, :, 0:D], ACT.Abs)))
                for s in range(2):
                    own.need(q[s])
                    q.append(own.done(act.activation(sp[:, s, 1, :, :], sp[:, s, 0, :, :], ACT.Exp, scale=-1.0)))
                for s in range(2):
                    own.need(q[2 + s])
                    act.activation(sp[:, s, 0, :, :], sp[:, s, 1, :, :], ACT.Ln, bias=1.0).then_inc(sp1, 1)
                for s in range(2):
                    rstd_of(rs2, mv2, s, it * 2 + s + 1)
                for s in range(2):
                    copy_T(tc2, tr2, s, it * 2 + s + 1)
                for s in range(2):
                    act.wait_ge(df2, it * 2 + s + 1)
                    act.activation(r1[:, s, 4, :], r1[:, s, 3, :], ACT.Exp).then_inc(ex2, 1)
                assert own.n == ACT_A, own.n

            for src_in, src, hi in ((wg_in, stg, wgh), (wu_in, stu, wuh)):
                act.wait_ge(src_in, 16)
                act.activation(hi[:, :], src[:, :], ACT.Copy).then_inc(w_hi, 1)
            act.wait_ge(wd_in, 16 * JC)
            act.activation(hv[:, :, 0:JC - 1, :], stv[:, :, 0:JC - 1, :], ACT.Copy).then_inc(w_hi, 1)
            act.activation(hv[0:R1, :, JC - 1, :], stv[0:R1, :, JC - 1, :], ACT.Copy).then_inc(w_hi, 1)

            def x_hi(b, v):
                act.wait_ge(xT_r, b + 1)
                act.activation(xbh[:, v, :], bank[0][:, 0:D], ACT.Copy).then_inc(xh_r, 1)

            def silu(b, v):
                act.wait_ge(gu_r, b + 1)
                act.activation(sg[:, v, :], bank[4 + v][:, 0:I1], ACT.Silu).then_inc(sg_r, 1)

            def h_hi(b, v):
                act.wait_ge(hT_r, b + 1)
                act.activation(hh[:, v, :], bank[2 + v][:, 0:IP], ACT.Copy).then_inc(hh_r, 1)

            def y_out(b, u, again):
                act.wait_ge(y_r, b + 1)
                if again is not None:
                    act.wait_ge(ys_out[u], again + 16)
                act.activation(yb[:, u, :], bank[1][:, 0:D], ACT.Copy).then_inc(yb_r, 1)

            x_hi(0, 0)
            for b in range(4):
                silu(b, b % 2)
                x_hi(b + 1, (b + 1) % 2)
                if b >= 1:
                    h_hi(b - 1, (b - 1) % 2)
                if b >= 2:
                    y_out(b - 2, b - 2, None)
            with act.Fori(1, NBLK // 4 - 1) as it:
                for u in range(4):
                    b = it * 4 + u
                    silu(b, u % 2)
                    x_hi(b + 1, (u + 1) % 2)
                    h_hi(b - 1, (u - 1) % 2)
                    y_out(b - 2, (u - 2) % 4, (it if u >= 2 else it - 1) * 16)
            for b in range(NBLK - 4, NBLK + 2):
                if b < NBLK:
                    silu(b, b % 2)
                if b + 1 < NBLK:
                    x_hi(b + 1, (b + 1) % 2)
                if b - 1 < NBLK:
                    h_hi(b - 1, (b - 1) % 2)
                y_out(b - 2, (b - 2) % 4, 16 * ((b - 2) // 4))

            act.wait_ge(c_in, 16 * 8)
            act.wait_ge(c_const, 1)
            act.activation(wqh[:, :], wqkv[:, :], ACT.Copy).then_inc(c_w, 1)
            act.wait_ge(c_w, 4)

            def act_turn(i, half, p, E, F, M, P1, G):
                if not isinstance(i, int) or i in (-2, B - 3):
                    act.preload_act_table_set(TABLE)

                def exp(h):
                    if E:
                        act.wait_ge(c_S2, i * H + h + 1)
                        if h >= 4 or not isinstance(i, int) or i > 0:
                            act.wait_ge(c_PV, i * H + h - 3)
                        act.activation(pt[:, h % 4, :], bank[4 + h % 2][:, 0:3 * P], ACT.Exp).then_inc(c_P, 1)

                def out_copy(g):
                    if E:
                        act.wait_ge(c_PV, i * H + 4 * g + 4)
                        act.activation(ot[:, p, g, :], bank[6][:, 0:2 * P], ACT.Copy).then_inc(c_OT, 1)

                b1, b2 = i + 1, i + 2
                if M:
                    act.wait_ge(c_T, b1 + 1)
                    act.activation(qT[:, :, :], ps[:, 0:2, :].rearrange("p a (g t) -> p (a g) t", g=2),
                                   ACT.Copy).then_inc(c_qT, 1)
                exp(0)
                exp(1)
                if P1:
                    act.wait_ge(c_mv, b2 + 1)
                    act.activation(cln[:, :], cmv[:, :, 1], ACT.Ln, bias=eps_c[:, 0:1]).then_inc(act_c, 1)
                    act.wait_ge(act_c, b2 + 1)
                    act.activation(crs[:, :], cln[:, :], ACT.Exp, scale=-0.5).then_inc(c_rs, 1)
                exp(2)
                if F:
                    act.wait_ge(c_F3, i)
                    act.activation(ooT[:, :, :], bank[7][:, 0:2 * P].rearrange("p (u t) -> p u t", u=2),
                                   ACT.Copy).then_inc(c_F4, 1)
                exp(3)
                if P1:
                    act.wait_ge(c_xT, b2 + 1)
                    act.activation(xch[:, :, :], bank[7][:, 0:2 * P].rearrange("p (u t) -> p u t", u=2),
                                   ACT.Copy).then_inc(c_xh, 1)
                exp(4)
                out_copy(0)
                exp(5)
                exp(6)
                if P1:
                    act.wait_ge(c_z, 2 * b2 + 1)
                    act.activation(zs[:, p, 0, :], bank[7][:, 0:3 * D], ACT.Copy).then_inc(c_zs, 1)
                exp(7)
                if P1:
                    act.wait_ge(c_z, 2 * b2 + 2)
                    act.activation(zs[:, p, 1, :], bank[7][:, 0:3 * D], ACT.Copy).then_inc(c_zs, 1)
                exp(8)
                out_copy(1)
                exp(9)
                if P1:
                    act.wait_ge(c_cen, b2 + 1)
                    act.activation(csq[:, :, :], cen[:, :, :], ACT.Square).then_inc(c_sq, 1)
                exp(10)
                if P1:
                    act.wait_ge(c_vs, b2 + 1)
                    act.activation(rql[:, :, :], vsm[:, :, :], ACT.Ln, bias=eps_c[:, 0:1], scale=1.0 / S).then_inc(act_c2, 1)
                    act.wait_ge(act_c2, b2 + 1)
                    act.activation(rq[:, :, :], rql[:, :, :], ACT.Exp, scale=-0.5).then_inc(c_rq, 1)
                exp(11)
                exp(12)
                out_copy(2)
                exp(13)
                if P1:
                    act.wait_ge(c_wb, b2 + 1)
                    act.activation(nqh[:, :, :], nq[:, 2, :, :], ACT.Copy).then_inc(c_nh, 1)
                exp(14)
                exp(15)
                if M:
                    act.wait_ge(c_T2, b1 + 1)
                    act.activation(qT2[:, 1 - p, :, :], ps[:, 0:2, :].rearrange("p a (g t) -> p (a g) t", g=2),
                                   ACT.Copy).then_inc(c_q2, 1)
                out_copy(3)

            turns(act_turn, act)

            act.wait_ge(d_const, 3)
            act.activation(selr[:, :], selz[:, :, :].rearrange("p e f -> p (e f)"), ACT.Copy).then_inc(d_sel, 1)
            with act.Fori(0, NPIECE // 2) as it:
                act.preload_act_table_set(TABLE)
                for s in range(2):
                    act.wait_ge(d_mv, it * 2 + s + 1)
                    act.activation(lnv[:, s, :], mv[:, s, :, 1], ACT.Ln, bias=eps_c[:, 0:1]).then_inc(act_d, 1)
                    act.wait_ge(act_d, it * 2 + s + 1)
                    act.activation(rstd[:, s, :], lnv[:, s, :], ACT.Exp, scale=-0.5).then_inc(d_rs, 1)
                for s in range(2):
                    copy_T(d_Tc, d_T, s, it * 2 + s + 1)
                for s in range(2):
                    act.wait_ge(d_afc, it * 2 + s + 1)
                    act.activation(g4[:, s, 0, :, :], af[:, s, :, :], ACT.Exp, scale=-1.0).then_inc(d_ex, 1)
                for s in range(2):
                    act.wait_ge(d_cT, it * 2 + s + 1)
                    apart(act, act_passed)
                    act.activation(cwT[:, ds((it * 2 + s) * TT, TT)], bank[4 + s][:, :], ACT.Copy).then_inc(d_cw, 1)

            def e_silu(t, u):
                act.wait_ge(u_up, t * NU + u + 1)
                r = slice(0, F2 if u == 0 else P)
                if u == 0:
                    if not (isinstance(t, int) and t == 0):
                        act.wait_ge(u_hl, t * NU - 2)
                    act.activation(h4[r, u % 3, :], bank[u % 3][r, :], ACT.Silu).then_inc(u_sg0, 1)
                else:
                    act.activation(sg4[r, u % 3, :], bank[u % 3][r, :], ACT.Silu).then_inc(u_sg, 1)

            def e_hi(t, u):
                r = slice(0, F2 if u == 0 else P)
                if u == 0:
                    act.wait_ge(u_sg0, t + 1)
                else:
                    act.wait_ge(u_h, t * NP2 + u)
                if u >= 3:
                    act.wait_ge(u_dn, t * NU + u - 2)
                elif not (isinstance(t, int) and t == 0):
                    act.wait_ge(u_dn, (t - 1) * NU + NU + u - 2)
                act.activation(hh4[r, u % 3, :], h4[r, u % 3, :], ACT.Copy).then_inc(u_hh, 1)

            def out_copy4(t, p):
                act.wait_ge(u_dn, (t + 1) * NU)
                act.activation(oT4[:, :], bank[5 + 2 * p][:, :], ACT.Copy).then_inc(u_oT, 1)

            def act_tile(t, p, before):
                for u in range(NU):
                    e_silu(t, u)
                    if u >= 1:
                        e_hi(t, u - 1)
                    elif before is not None:
                        e_hi(before[0], NU - 1)
                    if u == 5 and before is not None:
                        out_copy4(before[0], before[1])

            tiles_of(act, act_tile)
            e_hi(T // TT - 1, NU - 1)
            out_copy4(T // TT - 1, 1)

        @block.vector
        def _(dve):
            dve.wait_ge(x_in, 64)
            dve.wait_ge(consts, 1)
            dve.wait_ge(small_in, 16 * 10)

            def stats(own, s, t0, ready):
                for k in range(SUB):
                    last = own.done(dve.bn_stats(out=st[:, s, k, :], in_=x_res[:, ds(t0 + k, 1), :]))
                own.need(last)
                apart(dve, dve_passed)
                for k in range(SUB):
                    ins = dve.bn_aggr(out=mv[:, s, k, :], in_=st[:, s, k, :])
                ins.then_inc(ready, 1)

            def normed(dst, s, t0, scaled, i, ready):
                dve.wait_ge(scaled, i)
                for k in range(SUB):
                    ins = dve.tensor_scalar(dst[:, s, k:k + 1, :], x_res[:, ds(t0 + k, 1), :], mv[:, s, k, 0:1],
                                            rstd[:, s, k:k + 1], ALU.subtract, ALU.mult)
                ins.then_inc(ready, 1)

            with dve.Fori(0, NPIECE // 2) as it:
                own = Tickets(dve, dve_own, it * DVE_A)
                for s in range(2):
                    stats(own, s, (it * 2 + s) * SUB, mv1)
                for s in range(2):
                    normed(xn, s, (it * 2 + s) * SUB, rs1, it * 2 + s + 1, xn1)
                q = []
                for s in range(2):
                    dve.wait_ge(zz1, it * 2 + s + 1)
                    zv = z[:, s, :, :].rearrange("p (a b) m -> p a (b m)", a=2)
                    for a in range(2):
                        ins = dve.tensor_tensor(zv[:, a, :], bank[2 + 2 * s + a][:, 0:2 * M1],
                                                bias[:, :, :].rearrange("p a m -> p (a m)"), op=ALU.add)
                    ins.then_inc(zc1, 1)
                for s in range(2):
                    dve.wait_ge(zc1, it * 2 + s + 1)
                    q.append(own.done(dve.tensor_tensor(bc[:, s, :, :], z[:, s, :, D:D + N], z[:, s, :, D + N:M1],
                                                        op=ALU.mult)))
                for s in range(2):
                    own.need(q[s])
                    own.done(dve.tensor_reduce(bcs[:, s, :], bc[:, s, :, :], axis=AX.X, op=ALU.add))
                q = []
                for s in range(2):
                    dve.wait_ge(sp1, it * 2 + s + 1)
                    q.append(own.done(dve.scalar_tensor_tensor(
                        sp[:, s, 1, :, :], z[:, s, :, 0:D], 0.0, sp[:, s, 0, :, :], ALU.max, ALU.add)))
                for s in range(2):
                    own.need(q[s])
                    q.append(own.done(dve.tensor_tensor(sp[:, s, 2, :, :], sp[:, s, 1, :, :], xn[:, s, :, :], op=ALU.mult)))
                for s in range(2):
                    own.need(q[2 + s])
                    for k in range(SUB):
                        t = ds((it * 2 + s) * SUB + k, 1)
                        q.append(own.done(dve.scalar_tensor_tensor(
                            x_res[:, t, :], sp[:, s, 2, k:k + 1, :], bcs[:, s, k:k + 1], x_res[:, t, :],
                            ALU.mult, ALU.add)))
                for s in range(2):
                    own.need(q[4 + SUB * (s + 1) - 1])
                    apart(dve, dve_passed)
                    stats(own, s, (it * 2 + s) * SUB, mv2)
                for s in range(2):
                    dve.wait_ge(scat_ok[s], it + 1)
                    normed(xm, s, (it * 2 + s) * SUB, rs2, it * 2 + s + 1, xn2)
                q = []
                for s in range(2):
                    dve.wait_ge(lg2, it * 2 + s + 1)
                    q.append(own.done(dve.tensor_copy(
                        lg[:, s, :, :], bank[2 + 2 * s][:, 0:16 * SUB].rearrange("p (k e) -> p k e", e=16)[:, :, 0:E1])))

                def both(op):
                    was = list(q)
                    for s in range(2):
                        own.need(was[s])
                        q[s] = own.done(op(s))

                def wide(v):
                    return v.unsqueeze(2).broadcast_to([P, SUB, E1])

                def tiles(s):
                    return ds((it * 2 + s) * SUB, SUB)

                for c in range(K1):
                    row = (lambda s: lg[:, s, :, :]) if c == 0 else (lambda s: r9[:, s, 2, :, :])
                    both(lambda s: dve.tensor_reduce(r1[:, s, c, :], row(s), axis=AX.X, op=ALU.max))
                    both(lambda s: dve.tensor_tensor(r9[:, s, 0, :, :], row(s), wide(r1[:, s, c, :]), op=ALU.is_equal))
                    both(lambda s: dve.tensor_tensor(r9[:, s, 1, :, :], r9[:, s, 0, :, :], rev9[:, :, :], op=ALU.mult))
                    both(lambda s: dve.tensor_reduce(r1[:, s, 2, :], r9[:, s, 1, :, :], axis=AX.X, op=ALU.max))
                    both(lambda s: dve.tensor_tensor(pick[:, tiles(s), c, :], r9[:, s, 1, :, :], wide(r1[:, s, 2, :]),
                                                     op=ALU.is_equal))
                    if c == 0:
                        both(lambda s: dve.scalar_tensor_tensor(r9[:, s, 2, :, :], pick[:, tiles(s), c, :], -BIG,
                                                                lg[:, s, :, :], ALU.mult, ALU.add))
                for s in range(2):
                    dve.tensor_tensor(r1[:, s, 3, :], r1[:, s, 1, :], r1[:, s, 0, :], op=ALU.subtract).then_inc(df2, 1)
                for s in range(2):
                    own.need(q[s])
                    dve.tensor_tensor(sel[:, s, :, :], pick[:, tiles(s), 0, :], pick[:, tiles(s), 1, :],
                                      op=ALU.add).then_inc(sl2, 1)
                for s in range(2):
                    dve.wait_ge(ex2, it * 2 + s + 1)
                    q[s] = own.done(dve.tensor_scalar(r1[:, s, 5, :], r1[:, s, 4, :], 1.0, None, ALU.add))
                both(lambda s: dve.reciprocal(r1[:, s, 6, :], r1[:, s, 5, :]))
                both(lambda s: dve.tensor_scalar(wgt[:, tiles(s), 0], r1[:, s, 6, :], 0.0, None, ALU.add))
                both(lambda s: dve.tensor_tensor(wgt[:, tiles(s), 1], r1[:, s, 6, :], r1[:, s, 4, :], op=ALU.mult))
                for s in range(2):
                    dve.wait_ge(rk2, it * 2 + s + 1)
                    own.link(dve.tensor_tensor(
                        r9[:, s, 3, :, :], bank[3 + 2 * s][:, 0:SUB * E1].rearrange("p (k e) -> p k e", e=E1),
                        base[:, :].unsqueeze(1).broadcast_to([P, SUB, E1]), op=ALU.add))
                    own.done(dve.tensor_tensor(base[:, :], bank[3 + 2 * s][:, SUB * E1:(SUB + 1) * E1], base[:, :],
                                               op=ALU.add))
                    own.link(dve.tensor_tensor(
                        r9[:, s, 4, :, :], r9[:, s, 3, :, :],
                        off9[:, :].unsqueeze(1).broadcast_to([P, SUB, E1]), op=ALU.add))
                    for c in range(K1):
                        own.done(dve.tensor_tensor(r9[:, s, c, :, :], r9[:, s, 4, :, :], pick[:, tiles(s), c, :],
                                                   op=ALU.mult))
                    own.need(own.n)
                    for c in range(K1):
                        own.done(dve.tensor_reduce(posf[:, tiles(s), c], r9[:, s, c, :, :], axis=AX.X, op=ALU.add))
                    own.need(own.n)
                    apart(dve, dve_passed)
                    dve.tensor_copy(posi[:, s, :, :], posf[:, tiles(s), :]).then_inc(ps2, 1)
                assert own.n == DVE_A, own.n

            own = Tickets(dve, dve_own, (NPIECE // 2) * DVE_A)
            own.link(dve.tensor_tensor(q9[:, 0, :], base[:, :], off9[:, :], op=ALU.add))
            own.done(dve.tensor_scalar(cnti[:, :], base[:, :], float(P - 1), None, ALU.add))
            own.link(dve.tensor_tensor(q9[:, 1, :], q9[:, 0, :], prow[:, :], op=ALU.add))
            dve.tensor_copy(tail[:, :], q9[:, 1, :]).then_inc(tails, 1)
            own.link(dve.tensor_single_scalar(cnti[:, :], cnti[:, :], 7, ALU.logical_shift_right))
            own.link(dve.tensor_copy(nblk[:, :], cnti[:, :]))
            own.link(dve.tensor_copy(bend[:, 0:1], nblk[:, 0:1]))
            for e in range(1, E1):
                own.link(dve.tensor_tensor(bend[:, e:e + 1], bend[:, e - 1:e], nblk[:, e:e + 1], op=ALU.add))
            own.link(dve.tensor_tensor(bstart[:, :], bend[:, :], nblk[:, :], op=ALU.subtract))
            own.link(dve.scalar_tensor_tensor(q9[:, 2, :], bstart[:, :], -float(P), off9[:, :], ALU.mult, ALU.add))

            def over_e(v):
                return v.unsqueeze(2).broadcast_to([P, NBLK, E1])

            def over_b(v):
                return v.unsqueeze(1).broadcast_to([P, NBLK, E1])

            own.done(dve.tensor_tensor(b9[:, 0, :, :], over_e(iblk[:, :]), over_b(bstart[:, :]), op=ALU.is_ge))
            own.done(dve.tensor_tensor(b9[:, 1, :, :], over_e(iblk[:, :]), over_b(bend[:, :]), op=ALU.is_lt))
            own.need(own.n)
            own.done(dve.tensor_tensor(b9[:, 2, :, :], b9[:, 0, :, :], b9[:, 1, :, :], op=ALU.mult))
            own.need(own.n)
            own.link(dve.tensor_tensor(b9[:, 0, :, :], over_e(iblk[:, :]), over_b(bend[:, :]), op=ALU.is_ge))
            own.done(dve.tensor_reduce(bf[:, 0, :], b9[:, 0, :, :], axis=AX.X, op=ALU.add))
            own.link(dve.tensor_tensor(b9[:, 1, :, :], b9[:, 2, :, :], over_b(q9[:, 2, :]), op=ALU.mult))
            own.done(dve.tensor_reduce(bf[:, 1, :], b9[:, 1, :, :], axis=AX.X, op=ALU.add))
            own.done(dve.tensor_reduce(bf[:, 2, :], b9[:, 2, :, :], axis=AX.X, op=ALU.add))
            own.link(dve.tensor_scalar(bf[:, 0, :], bf[:, 0, :], float(E1 - 1), None, ALU.min))
            own.link(dve.scalar_tensor_tensor(b9[:, 0, 0:NBLK, 0], iblk[:, :], float(P), bf[:, 2, :], ALU.mult, ALU.mult))
            own.link(dve.tensor_tensor(bf[:, 1, :], bf[:, 1, :], b9[:, 0, 0:NBLK, 0], op=ALU.add))
            own.link(dve.tensor_scalar(bf[:, 2, :], bf[:, 2, :], -float((E1 - 1) * REG), float((E1 - 1) * REG),
                                       ALU.mult, ALU.add))
            own.link(dve.tensor_tensor(bf[:, 1, :], bf[:, 1, :], bf[:, 2, :], op=ALU.add))
            own.done(dve.tensor_copy(blk_e[:, :], bf[:, 0, :]))
            dve.tensor_copy(blk_src[:, :], bf[:, 1, :]).then_inc(list_ready, 1)
            pk = pick[:, :, :, :].rearrange("p t c e -> p (t c) e")
            own.link(dve.tensor_tensor(gp9[:, :, :], pk, q9[:, 2, :].unsqueeze(1).broadcast_to([P, NT * K1, E1]),
                                       op=ALU.mult))
            own.link(dve.tensor_reduce(gpf[:, :], gp9[:, :, :], axis=AX.X, op=ALU.add))
            own.link(dve.tensor_tensor(gpf[:, :], posf[:, :, :].rearrange("p t c -> p (t c)"), gpf[:, :], op=ALU.subtract))
            dve.tensor_copy(gpi[:, :], gpf[:, :]).then_inc(gp_r, 1)

            for i, (src, hi, lo) in enumerate(((stg, wgh, wgl), (stu, wuh, wul))):
                dve.wait_ge(w_hi, i + 1)
                dve.tensor_tensor(lo[:, :], src[:, :], hi[:, :].bitcast(F32), op=ALU.subtract).then_inc(w_lo, 1)

            def x_lo(b, v):
                dve.wait_ge(xh_r, b + 1)
                dve.tensor_tensor(xbl[:, v, :], bank[0][:, 0:D], xbh[:, v, :].bitcast(F32),
                                  op=ALU.subtract).then_inc(xl_r, 1)

            def h_of(b, v):
                dve.wait_ge(sg_r, b + 1)
                dve.tensor_tensor(hb[:, v, 0:I1], sg[:, v, :], bank[6 + v][:, 0:I1], op=ALU.mult).then_inc(h_r, 1)

            def h_lo(b, v, first):
                dve.wait_ge(hh_r, b + 1)
                if not first:
                    dve.wait_ge(y_r, b - 1)
                dve.tensor_tensor(hl[:, v, :], bank[2 + v][:, 0:IP], hh[:, v, :].bitcast(F32),
                                  op=ALU.subtract).then_inc(hl_r, 1)

            x_lo(0, 0)
            for b in range(4):
                h_of(b, b % 2)
                x_lo(b + 1, (b + 1) % 2)
                if b >= 1:
                    h_lo(b - 1, (b - 1) % 2, b < 3)
            with dve.Fori(1, NBLK // 4 - 1) as it:
                for u in range(4):
                    b = it * 4 + u
                    h_of(b, u % 2)
                    x_lo(b + 1, (u + 1) % 2)
                    h_lo(b - 1, (u - 1) % 2, False)
            for b in range(NBLK - 4, NBLK + 1):
                if b < NBLK:
                    h_of(b, b % 2)
                if b + 1 < NBLK:
                    x_lo(b + 1, (b + 1) % 2)
                h_lo(b - 1, (b - 1) % 2, False)

            def add_rows(b, p, loads):
                for u in range(2):
                    dve.wait_ge(yg_in[2 * p + u], loads)
                for c in range(K1):
                    for u in range(2):
                        t = ds(2 * b + u, 1)
                        if c == 1:
                            dve.wait_ge(x2_half, 2 * b + u + 1)
                        dve.scalar_tensor_tensor(x_res[:, t, :], yg[:, 2 * p + u, c:c + 1, :], wgt[:, t, c],
                                                 x_res[:, t, :], ALU.mult, ALU.add).then_inc(x2_half if c == 0 else x2_r, 1)

            dve.wait_ge(c_in, 16 * 8)
            dve.wait_ge(c_const, 1)
            dve.wait_ge(c_w, 1)
            dve.tensor_tensor(wql[:, :], wqkv[:, :], wqh[:, :].bitcast(F32), op=ALU.subtract).then_inc(c_w, 1)
            scale = 1.0 / float(S) ** 0.5
            for j, (dst, c) in enumerate(((lnw, 0), (lnw, 1), (lnb, 0), (lnb, 1))):
                ins = dve.tensor_scalar(dst[:, c, :, :], ln8[:, j, :].unsqueeze(1).broadcast_to([P, H, S]),
                                        scale if c == 0 else 1.0, None, ALU.mult)
                if j % 2:
                    ins.then_inc(c_w, 1)

            def dve_turn(i, half, p, E, F, M, P1, G):
                b1, b2 = i + 1, i + 2
                if M:
                    dve.wait_ge(c_T, b1 + 1)
                    dve.tensor_copy(kT[:, 1 - p, :, :], ps[:, 2:4, :].rearrange("p a (g t) -> p (a g) t", g=2)).then_inc(c_kT, 1)
                if F:
                    for u in range(2):
                        dve.wait_ge(c_F1, 2 * i - 1 + u)
                        o = bank[7][:, :].rearrange("p (h w) -> p h w", w=HW)
                        dve.reciprocal(rc[:, u, :], o[:, :, S]).then_inc(dve_cf, 1)
                        dve.wait_ge(dve_cf, 2 * i - 1 + u)
                        dve.tensor_tensor(oo[:, u, :].rearrange("p (h s) -> p h s", h=H), o[:, :, 0:S],
                                          rc[:, u, :].unsqueeze(2).broadcast_to([P, H, S]), op=ALU.mult).then_inc(c_F2, 1)
                if P1:
                    add_rows(b2, p, (half + 2) * (16 * K1))
                    dve.wait_ge(x2_r, 2 * b2 + 2)
                    apart(dve, dve_passed)
                    own = Tickets(dve, dve_c1, b2 * 3)
                    for u in range(2):
                        t = own.done(dve.bn_stats(out=cst[:, u, :], in_=x_res[:, ds(b2 * 2 + u, 1), :]))
                    own.need(t)
                    apart(dve, dve_passed)
                    for u in range(2):
                        ins = dve.bn_aggr(out=cmv[:, u, :], in_=cst[:, u, :])
                    ins.then_inc(c_mv, 1)
                    dve.wait_ge(c_rs, b2 + 1)
                    for u in range(2):
                        ins = dve.tensor_scalar(xc[:, u:u + 1, :], x_res[:, ds(b2 * 2 + u, 1), :], cmv[:, u, 0:1],
                                                crs[:, u:u + 1], ALU.subtract, ALU.mult)
                    ins.then_inc(c_xn, 1)
                    dve.wait_ge(c_xh, b2 + 1)
                    dve.tensor_tensor(xcl[:, :, :], bank[7][:, 0:2 * P].rearrange("p (u t) -> p u t", u=2),
                                      xch[:, :, :].bitcast(F32), op=ALU.subtract).then_inc(c_xl, 1)
                if F:
                    dve.wait_ge(c_F5, i)
                    t = ds((i - 1) * 2, 2)
                    dve.tensor_tensor(x_res[:, t, :], bank[7][:, 0:2 * D].rearrange("p (u d) -> p u d", u=2),
                                      x_res[:, t, :], op=ALU.add).then_inc(c_F6, 1)

                def maxima(k):
                    if M:
                        dve.wait_ge(c_S1, b1 * 8 + k + 1)
                        o = ps[:, 2 * (k % 2):2 * (k % 2) + 2, :]
                        dve.tensor_reduce(nm[:, 0, 2 * k:2 * k + 2], o[:, :, 0:P], axis=AX.X, op=ALU.max, negate=True)
                        dve.tensor_reduce(nm[:, 1, 2 * k:2 * k + 2], o[:, :, P:3 * P], axis=AX.X, op=ALU.max,
                                          negate=True).then_inc(c_mx, 1)

                for k in range(4):
                    maxima(k)
                if P1:
                    dve.wait_ge(c_zs, b2 * 2 + 2)
                    own.link(dve.tensor_reduce(ms[:, :, :], zs[:, p, :, 0:2 * D].rearrange("p u (g s) -> p u g s", s=S),
                                               axis=AX.X, op=ALU.add))
                    for u in range(2):
                        ins = dve.scalar_tensor_tensor(
                            cen[:, u, :].rearrange("p (g s) -> p g s", s=S),
                            ms[:, u, :].unsqueeze(2).broadcast_to([P, 2 * H, S]), -1.0 / S,
                            zs[:, p, u, 0:2 * D].rearrange("p (g s) -> p g s", s=S), ALU.mult, ALU.add)
                    ins.then_inc(c_cen, 1)
                maxima(4)
                if P1:
                    dve.wait_ge(c_sq, b2 + 1)
                    dve.tensor_reduce(vsm[:, :, :], csq[:, :, :].rearrange("p u (g s) -> p u g s", s=S),
                                      axis=AX.X, op=ALU.add).then_inc(c_vs, 1)
                maxima(5)
                if P1:
                    dve.wait_ge(c_rq, b2 + 1)
                    dve.tensor_tensor(nq[:, 0, :, :].rearrange("p u (g s) -> p u g s", s=S),
                                      cen[:, :, :].rearrange("p u (g s) -> p u g s", s=S),
                                      rq[:, :, :].unsqueeze(3).broadcast_to([P, 2, 2 * H, S]), op=ALU.mult).then_inc(c_n, 1)
                maxima(6)
                maxima(7)
                if M:
                    dve.wait_ge(c_mx, b1 * 8 + 8)
                    dve.tensor_scalar(nmh[:, :, :], nm[:, :, :], 0.0, None, ALU.add).then_inc(dve_nm, 1)
                    dve.wait_ge(dve_nm, b1 + 1)
                    dve.tensor_copy(qs[:, 1 - p, :, :, KS], nmh[:, :, :].bitcast(F32))
                    dve.tensor_tensor(qs[:, 1 - p, :, :, KS + 1], nm[:, :, :], nmh[:, :, :].bitcast(F32),
                                      op=ALU.subtract).then_inc(c_nm, 1)
                if P1:
                    dve.wait_ge(c_nh, b2 + 1)
                    dve.tensor_tensor(qs[:, p, :, :, 2 * S:3 * S], heads4(nq[:, 2, :, :], 0), heads_of(nqh, 0).bitcast(F32),
                                      op=ALU.subtract)
                    dve.tensor_tensor(ks[:, p, :, :, S:2 * S], heads4(nq[:, 2, :, :], 1), heads_of(nqh, 1).bitcast(F32),
                                      op=ALU.subtract).then_inc(c_lo, 1)
                    assert own.n == 3

            turns(dve_turn, dve)

            with dve.Fori(0, NPIECE // 2) as it:
                own = Tickets(dve, dve_d, it * DVE_D)
                for s in range(2):
                    stats(own, s, (it * 2 + s) * SUB, d_mv)
                for s in range(2):
                    normed(xm4, s, (it * 2 + s) * SUB, d_rs, it * 2 + s + 1, d_xn)
                for s in range(2):
                    dve.wait_ge(d_Tc, it * 2 + s + 1)
                    tok = ds((it * 2 + s) * TT, TT)
                    apart(dve, dve_passed)
                    own.link(dve.tensor_copy(xh4[:, tok], xnT[:, s, :, :].rearrange("p k t -> p (k t)")))
                    dve.tensor_tensor(xl4[:, tok], xnT[:, s, :, :].rearrange("p k t -> p (k t)"),
                                      xh4[:, tok].bitcast(F32), op=ALU.subtract)
                q = []
                for s in range(2):
                    dve.wait_ge(d_af, it * 2 + s + 1)
                    dve.tensor_copy(af[:, s, :, :], bank[2 + s][:, 0:SUB * E2].rearrange("p (k e) -> p k e", e=E2)).then_inc(d_afc, 1)
                for s in range(2):
                    dve.wait_ge(d_afc, it * 2 + s + 1)
                    q.append(own.done(dve.tensor_tensor(bi[:, s, :, :], af[:, s, :, :],
                                                        ebi[:, :].unsqueeze(1).broadcast_to([P, SUB, E2]), op=ALU.add)))
                for s in range(2):
                    own.need(q[s])
                    apart(dve, dve_passed)
                    for k in range(SUB):
                        t = own.done(dve.max(out=m8[:, s, k, :], in_=bi[:, s, k, :]))
                    q[s] = t
                for s in range(2):
                    own.need(q[s])
                    apart(dve, dve_passed)
                    for k in range(SUB):
                        t = own.done(dve.match_replace(out=mr[:, s, k, :], in_to_replace=m8[:, s, k, :],
                                                       in_values=bi[:, s, k, :], imm_value=-BIG))
                    q[s] = t
                both4(lambda s: dve.tensor_tensor(g4[:, s, 1, :, :], mr[:, s, :, :], bi[:, s, :, :], op=ALU.not_equal), q, own)
                for s in range(2):
                    dve.wait_ge(d_ex, it * 2 + s + 1)
                    q[s] = own.done(dve.tensor_scalar(g4[:, s, 2, :, :], g4[:, s, 0, :, :], 1.0, None, ALU.add))
                both4(lambda s: dve.reciprocal(g4[:, s, 3, :, :], g4[:, s, 2, :, :]), q, own)
                both4(lambda s: dve.tensor_tensor(g4[:, s, 4, :, :], g4[:, s, 3, :, :], g4[:, s, 1, :, :], op=ALU.mult), q, own)
                both4(lambda s: dve.tensor_reduce(s4[:, s, 0, :], g4[:, s, 4, :, :], axis=AX.X, op=ALU.add), q, own)
                both4(lambda s: dve.tensor_scalar(s4[:, s, 1, :], s4[:, s, 0, :], 1e-8, None, ALU.add), q, own)
                both4(lambda s: dve.reciprocal(s4[:, s, 2, :], s4[:, s, 1, :]), q, own)
                both4(lambda s: dve.tensor_tensor(g4[:, s, 2, :, :], g4[:, s, 4, :, :],
                                                  s4[:, s, 2, :].unsqueeze(2).broadcast_to([P, SUB, E2]), op=ALU.mult), q, own)
                both4(lambda s: dve.tensor_scalar(cwh[:, s, :, :], g4[:, s, 2, :, :], 0.0, None, ALU.add), q, own)
                for s in range(2):
                    own.need(q[s])
                    apart(dve, dve_passed)
                    dve.tensor_copy(cs[:, s, :, 0:E2], cwh[:, s, :, :].bitcast(F32))
                    dve.tensor_tensor(cs[:, s, :, E2:2 * E2], g4[:, s, 2, :, :], cwh[:, s, :, :].bitcast(F32),
                                      op=ALU.subtract).then_inc(d_cs, 1)
                assert own.n == DVE_D, own.n

            def e_h(t, u):
                dve.wait_ge(u_sg, t * NP2 + u)
                dve.wait_ge(u_cw, t * NP2 + u)
                if u >= 3 or not (isinstance(t, int) and t == 0):
                    dve.wait_ge(u_hl, t * NU + u - 2)
                dve.tensor_tensor(h4[:, u % 3, :], sg4[:, u % 3, :], bank[3 + u % 2][:, :], op=ALU.mult).then_inc(u_h, 1)

            def e_lo(t, u):
                r = slice(0, F2 if u == 0 else P)
                dve.wait_ge(u_hh, t * NU + u + 1)
                dve.tensor_tensor(hl4[r, u % 3, :], h4[r, u % 3, :], hh4[r, u % 3, :].bitcast(F32),
                                  op=ALU.subtract).then_inc(u_hl, 1)

            def result(t, p, stored=0):
                dve.wait_ge(u_T, t + 1)
                if not isinstance(t, int) or t >= 2:
                    dve.wait_ge(o_out[p], stored * 16 + 16)
                dve.tensor_tensor(y4[:, p, :, :], bank[6][:, :].rearrange("p (k d) -> p k d", k=SUB),
                                  x_res[:, ds(t * SUB, SUB), :], op=ALU.add).then_inc(u_y, 1)

            def dve_tile(t, p, before):
                if before is not None:
                    e_lo(before[0], NU - 1)
                for u in range(1, NU):
                    e_h(t, u)
                    e_lo(t, u - 1)
                    if u == 9 and before is not None:
                        result(*before)

            tiles_of(dve, dve_tile)
            e_lo(T // TT - 1, NU - 1)
            result(T // TT - 1, 1, T // TT // 2 - 1)

        @block.tensor
        def _(pe):
            pe.wait_ge(consts, 1)
            pe.wait_ge(small_in, 16 * 10)

            def transposed(src, s, made, i, done):
                pe.wait_ge(made, i)
                for k in range(SUB):
                    ins = pe.transpose(bank[s][:, k * P:(k + 1) * P], src[:, s, k, :], ident[:, :])
                ins.then_inc(done, 1)

            with pe.Fori(0, NPIECE // 2) as it:
                for s in range(2):
                    transposed(xn, s, xn1, it * 2 + s + 1, tr1)
                for s in range(2):
                    pe.wait_ge(tc1, it * 2 + s + 1)
                    for k in range(SUB):
                        ins = pe.matmul(bank[2 + 2 * s + k // 2][:, (k % 2) * M1:(k % 2 + 1) * M1], xnT[:, s, k, :],
                                        w123[:, :], start=True, stop=True)
                    ins.then_inc(zz1, 1)
                for s in range(2):
                    transposed(xm, s, xn2, it * 2 + s + 1, tr2)
                for s in range(2):
                    pe.wait_ge(tc2, it * 2 + s + 1)
                    for k in range(SUB):
                        ins = pe.matmul(bank[2 + 2 * s][:, k * 16:k * 16 + E1], xnT[:, s, k, :], wr_s[:, :],
                                        start=True, stop=True)
                    ins.then_inc(lg2, 1)
                for s in range(2):
                    pe.wait_ge(sl2, it * 2 + s + 1)
                    for k in range(SUB + 1):
                        o = bank[3 + 2 * s][:, k * E1:(k + 1) * E1]
                        for j in range(k):
                            ins = pe.matmul(o, ones[:, :], sel[:, s, j, :], start=j == 0, stop=(k == SUB and j == k - 1))
                        if k < SUB:
                            ins = pe.matmul(o, tri[:, :], sel[:, s, k, :], start=k == 0, stop=True)
                    ins.then_inc(rk2, 1)

            def x_T(b, u, loads):
                pe.wait_ge(xb_in[u], 16 * loads)
                pe.transpose(bank[0][:, 0:P], xb[:, u, :], ident[:, :]).then_inc(xT_r, 1)

            def expert_of(b):
                return pe.value_load(blk_e[0:1, ds(b, 1)], min_val=0, max_val=E1 - 1)

            def up(b, v):
                e = expert_of(b)
                pe.wait_ge(xh_r, b + 1)
                pe.wait_ge(xl_r, b + 1)
                for o, hi, lo in ((bank[4 + v], wgh, wgl), (bank[6 + v], wuh, wul)):
                    w = ds(e * I1, I1)
                    pe.matmul(o[:, 0:I1], xbh[:, v, :], hi[:, w], start=True, stop=False)
                    pe.matmul(o[:, 0:I1], xbh[:, v, :], lo[:, w], start=False, stop=False)
                    ins = pe.matmul(o[:, 0:I1], xbl[:, v, :], hi[:, w], start=False, stop=True)
                ins.then_inc(gu_r, 1)

            def h_T(b, v):
                pe.wait_ge(h_r, b + 1)
                for j in range(JC):
                    ins = pe.transpose(bank[2 + v][:, j * P:(j + 1) * P], hb[:, v, j * P:(j + 1) * P], ident[:, :])
                ins.then_inc(hT_r, 1)

            def down(b, v, first):
                e = expert_of(b)
                pe.wait_ge(hh_r, b + 1)
                pe.wait_ge(hl_r, b + 1)
                if not first:
                    pe.wait_ge(yb_r, b)
                o = bank[1][:, 0:D]
                for j in range(JC):
                    r = min(P, I1 - j * P)
                    w = ds(e * (JC * D) + j * D, D)
                    hhj, hlj = hh[0:r, v, j * P:(j + 1) * P], hl[0:r, v, j * P:(j + 1) * P]
                    pe.matmul(o, hhj, wdh[0:r, w], start=j == 0, stop=False)
                    pe.matmul(o, hhj, wdl[0:r, w], start=False, stop=False)
                    ins = pe.matmul(o, hlj, wdh[0:r, w], start=False, stop=j == JC - 1)
                ins.then_inc(y_r, 1)

            pe.wait_ge(w_hi, 4)
            pe.wait_ge(w_lo, 4)
            pe.wait_ge(list_ready, 1)
            x_T(0, 0, 1)
            for b in range(4):
                up(b, b % 2)
                x_T(b + 1, (b + 1) % 4, (b + 1) // 4 + 1)
                if b >= 1:
                    h_T(b - 1, (b - 1) % 2)
                if b >= 2:
                    down(b - 2, b % 2, b == 2)
            with pe.Fori(1, NBLK // 4 - 1) as it:
                for u in range(4):
                    b = it * 4 + u
                    up(b, u % 2)
                    x_T(b + 1, (u + 1) % 4, it + 1 if u < 3 else it + 2)
                    h_T(b - 1, (u - 1) % 2)
                    down(b - 2, u % 2, False)
            for b in range(NBLK - 4, NBLK + 2):
                if b < NBLK:
                    up(b, b % 2)
                if b + 1 < NBLK:
                    x_T(b + 1, (b + 1) % 4, (b + 1) // 4 + 1)
                if b - 1 < NBLK:
                    h_T(b - 1, (b - 1) % 2)
                down(b - 2, b % 2, False)

            pe.wait_ge(c_in, 16 * 8)
            pe.wait_ge(c_const, 1)
            pe.wait_ge(c_w, 4)

            def pe_turn(i, half, p, E, F, M, P1, G):
                b1, b2 = i + 1, i + 2

                def masked(o, which):
                    pe.matmul(o.rearrange("p (a k) -> p a k", k=P)[:, 0:3:2, :], identb[:, :], msk[:, which, :, :],
                              start=True, stop=False, skip_group_check=True)

                def scores_k(h):
                    if E:
                        g = h // 4
                        if h >= 2 or not isinstance(i, int) or i > 0:
                            pe.wait_ge(c_P, i * H + h - 1)
                        if h == 0:
                            pe.wait_ge(c_q2, i + 1)
                        o = bank[4 + h % 2][:, 0:3 * P]
                        masked(o, 1)
                        pe.matmul(o[:, 0:2 * P], kT[rows(h, KS + 2), p, g, 0:P], qT2[rows(h, KS + 2), p, g, :],
                                  start=False, stop=False, skip_group_check=True)
                        pe.matmul(o[:, 2 * P:3 * P], kT[rows(h, KS + 2), p, g, P:2 * P], qT2[rows(h, KS + 2), p, g, P:2 * P],
                                  start=False, stop=True, skip_group_check=True).then_inc(c_S2, 1)

                def values(h):
                    if E:
                        g, j = h // 4, h % 4
                        pe.wait_ge(c_P, i * H + h + 1)
                        if h == 0:
                            pe.wait_ge(c_vp, i + 1)
                        if j == 0 and (g > 0 or not isinstance(i, int) or i > 0):
                            pe.wait_ge(c_OT, i * 4 + g)
                        o = bank[6][j * HW:(j + 1) * HW, 0:2 * P]
                        pe.matmul(o, vp[:, p, 0, h, :], pt[:, h % 4, 0:2 * P], start=True, stop=False,
                                  skip_group_check=True)
                        pe.matmul(o[:, P:2 * P], vp[:, p, 1, h, :], pt[:, h % 4, 2 * P:3 * P], start=False, stop=True,
                                  skip_group_check=True).then_inc(c_PV, 1)

                def scores_q(k):
                    if M:
                        if k >= 2:
                            pe.wait_ge(c_mx, b1 * 8 + k - 1)
                        if k == 0:
                            pe.wait_ge(c_qT, b1 + 1)
                            pe.wait_ge(c_kT, b1 + 1)
                        for h in (2 * k, 2 * k + 1):
                            o = bank[2 * (k % 2) + h % 2][:, 0:3 * P]
                            masked(o, 0)
                            g = h // 4
                            pe.matmul(o[:, 0:P], qT[rows(h, KS), g, 0:P], kT[rows(h, KS), 1 - p, g, 0:P],
                                      start=False, stop=False, skip_group_check=True)
                            ins = pe.matmul(o[:, P:3 * P], qT[rows(h, KS), g, P:2 * P], kT[rows(h, KS), 1 - p, g, :],
                                            start=False, stop=True, skip_group_check=True)
                        ins.then_inc(c_S1, 1)

                def turned(src, q, first_bank):
                    for g in range(4):
                        for u in range(2):
                            c = (g % 2) * 2 * P + u * P
                            ins = pe.transpose(bank[first_bank + g // 2][:, c:c + P],
                                               src[:, q, u, 4 * g:4 * g + 4, :].rearrange("p h w -> p (h w)"), ident[:, :])
                    return ins

                def att_T(u):
                    if F:
                        if u == 0:
                            pe.wait_ge(c_OT, i * 4)
                            if P1 or M:
                                pe.wait_ge(c_zs, 2 * i + 4)
                            if not P1:
                                pe.wait_ge(c_F6, i - 1)
                        else:
                            pe.wait_ge(c_F2, 2 * i - 1)
                        for g in range(4):
                            ins = pe.transpose(bank[7][:, g * P:(g + 1) * P], ot[:, 1 - p, g, u * P:(u + 1) * P], ident[:, :])
                        ins.then_inc(c_F1, 1)

                if M:
                    pe.wait_ge(c_dup, b1 + 1)
                    pe.wait_ge(c_lo, b1 + 1)
                    if not isinstance(i, int) or i > -1:
                        pe.wait_ge(c_q2, b1)
                    turned(qs, 1 - p, 0)
                    turned(ks, 1 - p, 2).then_inc(c_T, 1)
                scores_k(0)
                att_T(0)
                scores_k(1)
                att_T(1)
                scores_k(2)
                values(0)
                if F:
                    pe.wait_ge(c_F2, 2 * i)
                    for u in range(2):
                        ins = pe.transpose(bank[7][:, u * P:(u + 1) * P], oo[:, u, :], ident[:, :])
                    ins.then_inc(c_F3, 1)
                scores_k(3)
                values(1)
                if P1:
                    pe.wait_ge(c_xn, b2 + 1)
                    if F:
                        pe.wait_ge(c_F4, i)
                    elif not isinstance(i, int) or i > -2:
                        pe.wait_ge(c_zs, 2 * b2)
                    for u in range(2):
                        ins = pe.transpose(bank[7][:, u * P:(u + 1) * P], xc[:, u, :], ident[:, :])
                    ins.then_inc(c_xT, 1)
                scores_k(4)
                values(2)
                if P1:
                    pe.wait_ge(c_xl, b2 + 1)
                if F:
                    pe.wait_ge(c_F4, i)
                    for u in range(2):
                        ins = pe.matmul(bank[7][:, u * D:(u + 1) * D], ooT[:, u, :], wuT[:, :], start=True, stop=True)
                    ins.then_inc(c_F5, 1)
                scores_q(0)
                scores_k(5)
                values(3)
                scores_q(1)
                scores_k(6)
                values(4)
                for u in range(2):
                    if P1:
                        if u:
                            pe.wait_ge(c_zs, 2 * b2 + 1)
                        elif F:
                            pe.wait_ge(c_F6, i)
                        o = bank[7][:, 0:3 * D]
                        pe.matmul(o, xch[:, u, :], wqh[:, :], start=True, stop=False)
                        pe.matmul(o, xch[:, u, :], wql[:, :], start=False, stop=False)
                        pe.matmul(o, xcl[:, u, :], wqh[:, :], start=False, stop=True).then_inc(c_z, 1)
                    scores_q(2 + u)
                    scores_k(7 + u)
                    values(5 + u)
                for k in range(4, 8):
                    scores_q(k)
                    scores_k(5 + k)
                    values(3 + k)
                scores_k(13)
                values(11)
                scores_k(14)
                values(12)
                scores_k(15)
                values(13)
                if M:
                    pe.wait_ge(c_nm, b1 + 1)
                    turned(qs, 1 - p, 0).then_inc(c_T2, 1)
                values(14)
                values(15)

            turns(pe_turn, pe)

            pe.wait_ge(sh_in, 16 * 4)
            with pe.Fori(0, NPIECE // 2) as it:
                for s in range(2):
                    transposed(xm4, s, d_xn, it * 2 + s + 1, d_T)
                for s in range(2):
                    pe.wait_ge(d_Tc, it * 2 + s + 1)
                    for k in range(SUB):
                        ins = pe.matmul(bank[2 + s][:, k * E2:(k + 1) * E2], xnT[:, s, k, :], cen_s[:, :],
                                        start=True, stop=True)
                    ins.then_inc(d_af, 1)
                for s in range(2):
                    pe.wait_ge(d_cs, it * 2 + s + 1)
                    for k in range(SUB):
                        ins = pe.transpose(bank[4 + s][:, k * P:(k + 1) * P], cs[:, s, k, :], ident[:, :])
                    ins.then_inc(d_cT, 1)

            pe.wait_ge(d_cw, NPIECE)
            pe.wait_ge(d_sel, 1)
            pe.wait_ge(sh_done, 4)
            pe.wait_ge(wd_done, NC)

            def e_up(t, u):
                first = isinstance(t, int) and t == 0
                if u >= 3:
                    pe.wait_ge(u_sg, t * NP2 + u - 3)
                    if u == 3:
                        pe.wait_ge(u_sg0, t + 1)
                elif not first:
                    pe.wait_ge(u_sg, (t - 1) * NP2 + NU + u - 3)
                tok = ds(t * TT, TT)
                if u == 0:
                    o, hi, lo = bank[0][0:F2, :], shh[:, 0:F2], shl[:, 0:F2]
                else:
                    c = slice((u - 1) * P, u * P)
                    o, hi, lo = bank[u % 3][:, :], wh[:, c], wl[:, c]
                pe.matmul(o, hi, xh4[:, tok], start=True, stop=False)
                pe.matmul(o, hi, xl4[:, tok], start=False, stop=False)
                pe.matmul(o, lo, xh4[:, tok], start=False, stop=True).then_inc(u_up, 1)
                if u > 0:
                    if u > 2:
                        pe.wait_ge(u_h, t * NP2 + u - 2)
                    elif not first:
                        pe.wait_ge(u_h, (t - 1) * NP2 + NP2 + u - 2)
                    pe.matmul(bank[3 + u % 2][:, :], selr[:, c], cwT[:, tok], start=True, stop=True).then_inc(u_cw, 1)

            def e_down(t, p, u):
                if u == 0 and not (isinstance(t, int) and t < 2):
                    pe.wait_ge(u_oT, t - 1)
                pe.wait_ge(u_hl, t * NU + u + 1)
                if u == 0:
                    r, hi, lo = slice(0, F2), shh[0:F2, F2:F2 + D], shl[0:F2, F2:F2 + D]
                else:
                    c = slice(E2 * F2 + (u - 1) * D, E2 * F2 + u * D)
                    r, hi, lo = slice(0, P), wh[:, c], wl[:, c]
                o = bank[5 + 2 * p][:, :]
                pe.matmul(o, hi, hh4[r, u % 3, :], start=u == 0, stop=False)
                pe.matmul(o, hi, hl4[r, u % 3, :], start=False, stop=False)
                ins = pe.matmul(o, lo, hh4[r, u % 3, :], start=False, stop=u == NU - 1)
                ins.then_inc(u_dn, 1)

            def out_T(t):
                pe.wait_ge(u_oT, t + 1)
                if not isinstance(t, int) or t >= 1:
                    pe.wait_ge(u_y, t)
                for k in range(SUB):
                    ins = pe.transpose(bank[6][:, k * P:(k + 1) * P], oT4[:, k * P:(k + 1) * P], ident[:, :])
                ins.then_inc(u_T, 1)

            LAG = 3

            def pe_tile(t, p, before):
                for u in range(NU):
                    e_up(t, u)
                    if u >= LAG:
                        e_down(t, p, u - LAG)
                    elif before is not None:
                        e_down(before[0], 1 - p, NU + u - LAG)
                    if u == 7 and before is not None:
                        out_T(before[0])

            tiles_of(pe, pe_tile)
            for u in range(NU - LAG, NU):
                e_down(T // TT - 1, 1, u)
            out_T(T // TT - 1)


_INS = ['L0_attn_x', 'L0_attn_W1', 'L0_attn_b1', 'L0_attn_W2', 'L0_attn_b2', 'L0_attn_W3', 'L0_attn_b3',
        'L0_ffn_Wr', 'L0_ffn_Wg', 'L0_ffn_Wu', 'L0_ffn_Wd', 'L1_attn_Wk', 'L1_attn_Wq', 'L1_attn_Wv', 'L1_attn_Wu',
        'L1_attn_kln_w', 'L1_attn_kln_b', 'L1_attn_qln_w', 'L1_attn_qln_b', 'L1_ffn_centroids', 'L1_ffn_expert_biases',
        'L1_ffn_Ws_up', 'L1_ffn_Ws_down', 'L1_ffn_W_up', 'L1_ffn_W_down']
_TURNED = ('L1_attn_Wk', 'L1_attn_Wq', 'L1_attn_Wv', 'L1_attn_Wu', 'L1_ffn_centroids')
_OUTS = [((16, 256, 128), 'float32')]


def kernel(**inputs):
    import numpy as _np
    import concourse.bacc as _bacc
    from concourse import mybir as _mybir
    from concourse.bass_utils import run_bass_kernel_spmd as _run

    nc = _bacc.Bacc("TRN2", target_bir_lowering=False, num_devices=1)
    arrays, args = {}, []
    for name in _INS:
        a = _np.asarray(inputs[name])
        a = _np.ascontiguousarray(a.T if name in _TURNED else a)
        arrays[f"in_{name}_dram"] = a
        args.append(nc.dram_tensor(f"in_{name}_dram", a.shape, _mybir.dt.from_np(a.dtype), kind="ExternalInput").ap())
    for i, (shape, dtype) in enumerate(_OUTS):
        dt = _mybir.dt.from_np(_np.dtype(dtype))
        args.append(nc.dram_tensor(f"out_{i}_dram", shape, dt, kind="ExternalOutput").ap())
    bass_two_layers(nc, *args)
    r = _run(nc, [arrays], core_ids=[0])
    got = tuple(r.results[0][f"out_{i}_dram"] for i in range(len(_OUTS)))
    return got[0]
```

```python
from contextlib import ExitStack

import concourse.bass as bass
from concourse import mybir

F32 = mybir.dt.float32
F32R = mybir.dt.float32r
BF16 = mybir.dt.bfloat16
I32 = mybir.dt.int32
ALU = mybir.AluOpType
ACT = mybir.ActivationFunctionType
AX = mybir.AxisListType
ds = bass.ds

P = 128
LN_EPS = 1e-5
BIG = 1.0e30


def apart(eng, passed):
    eng.sem_inc(passed, 1)


class Tickets:

    def __init__(self, eng, sem, base=0):
        self.eng, self.sem, self.base, self.n = eng, sem, base, 0

    def done(self, ins):
        ins.then_inc(self.sem, 1)
        self.n += 1
        return self.n

    def need(self, ticket):
        self.eng.wait_ge(self.sem, self.base + ticket)

    def link(self, ins):
        self.need(self.done(ins))


def bass_two_layers(nc, x, W1, b1, W2, b2, W3, b3, Wr, Wg, Wu, Wd, WkT, WqT, WvT, WuT, kln_w, kln_b, qln_w, qln_b,
                    cent, ebias, Ws_up, Ws_down, W_up, W_down, out):
    B, L, D = x.shape
    T = B * L
    NT = T // P
    N = W2.shape[1]
    M1 = D + 2 * N
    E1, _, I1 = Wg.shape
    JC = -(-I1 // P)
    IP = JC * P
    K1 = 2
    SUB = 4
    NPIECE = NT // SUB
    REG = T + P
    NBLK = T * K1 // P + E1 - 1
    NBLK = -(-NBLK // 4) * 4
    assert D == P and NPIECE % 2 == 0

    x_tok = x.rearrange("b (u p) d -> p (b u) d", p=P)
    out_tok = out.rearrange("b (u p) d -> p (b u) d", p=P)

    xs = nc.dram_tensor("xs", [E1 * REG, D], F32).ap()
    ys = nc.dram_tensor("ys", [NBLK * P, D], F32).ap()

    with ExitStack() as ctx:
        def sb(name, shape, dt):
            return ctx.enter_context(nc.sbuf_tensor(name, shape, dt))

        def sem(name):
            return ctx.enter_context(nc.semaphore(name))

        ps = ctx.enter_context(nc.psum_tensor("ps", [P, 8, 512], F32))
        bank = [ps[:, i, :] for i in range(8)]

        x_res = sb("x_res", [P, NT, D], F32)
        ident = sb("ident", [P, P], F32)
        eps_c = sb("eps_c", [P, 1], F32)
        st = sb("st", [P, 2, SUB, 6], F32)
        mv = sb("mv", [P, 2, SUB, 2], F32)
        lnv = sb("lnv", [P, 2, SUB], F32)
        rstd = sb("rstd", [P, 2, SUB], F32)
        wgt = sb("wgt", [P, NT, K1], F32)
        gpi = sb("gpi", [P, NT * K1], I32)
        gps = sb("gps", [P, 2, 2 * K1], I32)
        yg = sb("yg", [P, 4, K1, D], F32)
        first = ExitStack()

        def sb1(name, shape, dt):
            return first.enter_context(nc.sbuf_tensor(name, shape, dt))

        xnT = sb1("xnT", [P, 2, SUB, P], F32)
        w123 = sb1("w123", [P, M1], F32)
        bias = sb1("bias", [P, 2, M1], F32)
        tri = sb1("tri", [P, P], BF16)
        ones = sb1("ones", [P, P], BF16)
        trif = sb1("trif", [P, P], F32)
        zrow = sb1("zrow", [P, P], F32)
        wr_s = sb1("wr_s", [P, E1], F32)
        rev9 = sb1("rev9", [P, SUB, E1], F32)
        off9 = sb1("off9", [P, E1], F32)
        prow = sb1("prow", [P, E1], F32)
        iblk = sb1("iblk", [P, NBLK], F32)
        xn = sb1("xn", [P, 2, SUB, D], F32)
        xm = sb1("xm", [P, 2, SUB, D], F32)
        z = sb1("z", [P, 2, SUB, M1], F32)
        sp = sb1("sp", [P, 2, 3, SUB, D], F32)
        bc = sb1("bc", [P, 2, SUB, N], F32)
        bcs = sb1("bcs", [P, 2, SUB], F32)
        lg = sb1("lg", [P, 2, SUB, E1], F32)
        r9 = sb1("r9", [P, 2, 5, SUB, E1], F32)
        r1 = sb1("r1", [P, 2, 8, SUB], F32)
        sel = sb1("sel", [P, 2, SUB, E1], BF16)
        pick = sb1("pick", [P, NT, K1, E1], F32)
        posf = sb1("posf", [P, NT, K1], F32)
        posi = sb1("posi", [P, 2, SUB, K1], I32)
        base = sb1("base", [P, E1], F32)
        stg = sb1("stg", [P, E1 * I1], F32)
        stu = sb1("stu", [P, E1 * I1], F32)
        std = sb1("std", [P, E1 * JC * D], F32)
        wgh = sb1("wgh", [P, E1 * I1], F32R)
        wgl = sb1("wgl", [P, E1 * I1], F32R)
        wuh = sb1("wuh", [P, E1 * I1], F32R)
        wul = sb1("wul", [P, E1 * I1], F32R)
        wdh = sb1("wdh", [P, E1 * JC * D], F32R)
        wdl = sb1("wdl", [P, E1 * JC * D], F32R)
        cnti = sb1("cnti", [P, E1], I32)
        nblk = sb1("nblk", [P, E1], F32)
        bend = sb1("bend", [P, E1], F32)
        bstart = sb1("bstart", [P, E1], F32)
        q9 = sb1("q9", [P, 3, E1], F32)
        tail = sb1("tail", [P, E1], I32)
        b9 = sb1("b9", [P, 3, NBLK, E1], F32)
        bf = sb1("bf", [P, 3, NBLK], F32)
        blk_src = sb1("blk_src", [P, NBLK], I32)
        blk_e = sb1("blk_e", [P, NBLK], I32)
        gp9 = sb1("gp9", [P, NT * K1, E1], F32)
        gpf = sb1("gpf", [P, NT * K1], F32)
        xb = sb1("xb", [P, 4, D], F32)
        xbh = sb1("xbh", [P, 2, D], F32R)
        xbl = sb1("xbl", [P, 2, D], F32R)
        sg = sb1("sg", [P, 2, I1], F32)
        hb = sb1("hb", [P, 2, IP], F32)
        hh = sb1("hh", [P, 2, IP], F32R)
        hl = sb1("hl", [P, 2, IP], F32R)
        yb = sb1("yb", [P, 4, D], F32)

        first.close()

        E2, F2 = cent.shape[1], W_up.shape[2]
        K2 = 8
        NP2 = E2 * F2 // P
        WC = 512
        TT = 4 * P
        NC = (E2 * F2 + NP2 * D) // WC
        assert NC == B and 2 * F2 == P
        wh = sb("wh", [P, E2 * F2 + NP2 * D], F32R)
        wl = sb("wl", [P, E2 * F2 + NP2 * D], F32R)
        wst = sb("wst", [P, 2, WC], F32)
        shf = sb("shf", [P, F2 + D], F32)
        shh = sb("shh", [P, F2 + D], F32R)
        shl = sb("shl", [P, F2 + D], F32R)
        cen_s = sb("cen_s", [P, E2], F32)
        ebi = sb("ebi", [P, E2], F32)
        attn = ExitStack()

        def sb2(name, shape, dt):
            return attn.enter_context(nc.sbuf_tensor(name, shape, dt))

        H = 16
        S = D // H
        HW = 32
        KA, QA = 2, 3
        KS = 3 * S
        wqkv = sb2("wqkv", [P, 3 * D], F32)
        wqh = sb2("wqh", [P, 3 * D], F32R)
        wql = sb2("wql", [P, 3 * D], F32R)
        wuT = sb2("wuT", [P, D], F32)
        ln8 = sb2("ln8", [P, 4, S], F32)
        lnw = sb2("lnw", [P, 2, H, S], F32)
        lnb = sb2("lnb", [P, 2, H, S], F32)
        identb = sb2("identb", [P, P], BF16)
        idr = sb2("idr", [P, 3, P], F32R)
        mskf = sb2("mskf", [P, 2, P], F32)
        msk = sb2("msk", [P, 2, 4, P], BF16)
        cst = sb2("cst", [P, 2, 6], F32)
        cmv = sb2("cmv", [P, 2, 2], F32)
        cln = sb2("cln", [P, 2], F32)
        crs = sb2("crs", [P, 2], F32)
        xc = sb2("xc", [P, 2, D], F32)
        xch = sb2("xch", [P, 2, P], F32R)
        xcl = sb2("xcl", [P, 2, P], F32R)
        zs = sb2("zs", [P, 2, 2, 3 * D], F32)
        ms = sb2("ms", [P, 2, 2 * H], F32)
        cen = sb2("cen", [P, 2, 2 * D], F32)
        csq = sb2("csq", [P, 2, 2 * D], F32)
        vsm = sb2("vsm", [P, 2, 2 * H], F32)
        rql = sb2("rql", [P, 2, 2 * H], F32)
        rq = sb2("rq", [P, 2, 2 * H], F32)
        nq = sb2("nq", [P, 2, 2, 2 * D], F32)
        qs = sb2("qs", [P, 2, 2, H, HW], F32R)
        ks = sb2("ks", [P, 2, 2, H, HW], F32R)
        vp = sb2("vp", [P, 2, 2, H, S + 1], F32)
        qT = sb2("qT", [P, 4, 2 * P], F32R)
        kT = sb2("kT", [P, 2, 4, 2 * P], F32R)
        kz = sb2("kz", [P, 4, 4, 2 * P], F32R)
        qz = sb2("qz", [P, 4, 4, 2 * P], F32R)
        nm = sb2("nm", [P, 2, H], F32)
        nmh = sb2("nmh", [P, 2, H], F32R)
        pt = sb2("pt", [P, 2, 3, 4, P], F32)
        ot = sb2("ot", [P, 2, 4, 2 * P], F32)
        rc = sb2("rc", [P, 2, H], F32)
        oo = sb2("oo", [P, 2, D], F32)
        ooT = sb2("ooT", [P, 2, P], F32)

        attn.close()

        xh4 = sb("xh4", [P, T], F32R)
        xl4 = sb("xl4", [P, T], F32R)
        cwT = sb("cwT", [P, T], F32R)
        selr = sb("selr", [P, E2 * F2], F32R)
        route = ExitStack()

        def sb3(name, shape, dt):
            return route.enter_context(nc.sbuf_tensor(name, shape, dt))

        selz = sb3("selz", [P, E2, F2], F32)
        xnT4 = sb3("xnT4", [P, 2, SUB, P], F32)
        xm4 = sb3("xm4", [P, 2, SUB, D], F32)
        af = sb3("af", [P, 2, SUB, E2], F32)
        bi = sb3("bi", [P, 2, SUB, E2], F32)
        m8 = sb3("m8", [P, 2, SUB, 8], F32)
        mr = sb3("mr", [P, 2, SUB, E2], F32)
        g4 = sb3("g4", [P, 2, 5, SUB, E2], F32)
        s4 = sb3("s4", [P, 2, 3, SUB], F32)
        cwh = sb3("cwh", [P, 2, SUB, E2], F32R)
        cs = sb3("cs", [P, 2, SUB, 2 * E2], F32)
        route.close()
        sg4 = sb("sg4", [P, 3, TT], F32)
        h4 = sb("h4", [P, 3, TT], F32)
        hh4 = sb("hh4", [P, 3, TT], F32R)
        hl4 = sb("hl4", [P, 3, TT], F32R)
        oT4 = sb("oT4", [P, TT], F32)
        y4 = sb("y4", [P, 2, SUB, D], F32)
        NU = NP2 + 1

        x_in = sem("x_in")
        small_in = sem("small_in")
        wg_in, wu_in, wd_in = sem("wg_in"), sem("wu_in"), sem("wd_in")
        w_hi, w_lo = sem("w_hi"), sem("w_lo")
        consts = sem("consts")
        pool_own, dve_own, act_own = sem("pool_own"), sem("dve_own"), sem("act_own")
        dve_passed, pool_passed = sem("dve_passed"), sem("pool_passed")
        mv1, rs1, xn1, tr1, tc1, zz1, zc1, sp1 = (sem(n) for n in (
            "ln1_stats", "ln1_rstd", "ln1_out", "ln1_T", "ln1_T_copied", "mix_z", "mix_z_copied", "mix_softplus"))
        mv2, rs2, xn2, tr2, tc2, lg2, df2, ex2, sl2, rk2, ps2 = (sem(n) for n in (
            "ln2_stats", "ln2_rstd", "ln2_out", "ln2_T", "ln2_T_copied", "r1_logits", "r1_diff", "r1_exp",
            "r1_sel", "r1_rank", "r1_pos"))
        scat = [sem("scat0"), sem("scat1")]
        scat_ok = [sem("scat_ok0"), sem("scat_ok1")]
        tails = sem("tails")
        tails_in = sem("tails_in")
        list_ready = sem("list_ready")
        xb_in = [sem(f"xb_in{u}") for u in range(4)]
        ys_out = [sem(f"ys_out{u}") for u in range(4)]
        xT_r, xh_r, xl_r, gu_r, sg_r, h_r, hT_r, hh_r, hl_r, y_r, yb_r = (sem(n) for n in (
            "blk_xT", "blk_xh", "blk_xl", "blk_gu", "blk_silu", "blk_h", "blk_hT", "blk_hh", "blk_hl", "blk_y", "blk_yb"))
        yg_in = [sem(f"yg_in{u}") for u in range(4)]
        x2_half, x2_r = sem("x2_first_row"), sem("x2_ready")
        gps_r = sem("batch_rows")
        gp_r = sem("gather_rows")
        o_out = [sem("o_out0"), sem("o_out1")]
        w_in = [sem("w_in0"), sem("w_in1")]
        wd_done, sh_in, sh_done, d_const, d_sel, act_passed = (sem(n) for n in (
            "w2_parts", "shared_in", "shared_parts", "d_const", "d_sel", "act_passed"))
        act_d, dve_d = sem("act_d"), sem("dve_d")
        d_mv, d_rs, d_xn, d_T, d_Tc, d_hl, d_af, d_afc, d_ex, d_cs, d_cT, d_cw = (sem(n) for n in (
            "ln4_stats", "ln4_rstd", "ln4_out", "ln4_T", "ln4_T_copied", "x4_parts", "r2_logits", "r2_copied", "r2_exp",
            "r2_weights", "r2_T", "r2_done"))
        u_up, u_cw, u_sg, u_h, u_hh, u_hl, u_dn, u_oT, u_y, u_T = (sem(n) for n in (
            "e_up", "e_weight", "e_silu", "e_h", "e_hh", "e_hl", "e_down", "e_outT", "e_y", "e_out_T"))
        c_in, c_const, c_w = sem("c_in"), sem("c_const"), sem("c_w")
        act_c, dve_c1, dve_cf, pool_c = sem("act_c"), sem("dve_c1"), sem("dve_cf"), sem("pool_c")
        c_mv, c_rs, c_xn, c_xT, c_xh, c_xl, c_z, c_zs, c_cen, c_sq, c_vs, c_rq, c_n, c_wb, c_nh, c_lo, c_dup, c_vp = (
            sem(n) for n in ("ln3_stats", "ln3_rstd", "ln3_out", "ln3_T", "ln3_T_hi", "ln3_T_lo", "qkv", "qkv_copied",
                             "qk_centred", "qk_squares", "qk_vars", "qk_rstd", "qk_scaled", "qk_affine", "qk_hi", "qk_lo",
                             "qk_spread", "v_spread"))
        c_T, c_qT, c_kT, c_S1, c_mx, c_nm, c_T2, c_q2, c_S2, c_P, c_PV, c_OT, c_F1, c_F2, c_F3, c_F4, c_F5, c_F6 = (
            sem(n) for n in ("qk_T", "q_T_copied", "k_T_copied", "scores_q", "row_max", "max_spread", "q2_T", "q2_T_copied",
                             "scores_k", "probs", "pv", "pv_copied", "att_T", "att_norm", "att_T2", "att_T2_copied",
                             "att_proj", "x3"))

        R1 = I1 - (JC - 1) * P
        stv, hv, lv = (w[:, 0:E1 * JC * D].rearrange("p (e j d) -> p e j d", e=E1, j=JC) for w in (std, wdh, wdl))
        ACT_A, DVE_A, DVE_D = 8, 78, 46

        c_q2d, c_kz, c_T3 = sem("q2_T_copied_dve"), sem("k_T_spread"), sem("k_T")
        dve_ln = sem("dve_ln")
        pool_w, act_c2, dve_nm = sem("pool_w"), sem("act_c2"), sem("dve_nm")
        pool_h, u_sg0 = sem("pool_h"), sem("e_silu_shared")

        def both4(op, q, own):
            was = list(q)
            for s in range(2):
                own.need(was[s])
                q[s] = own.done(op(s))

        def tiles_of(eng, tile):
            tile(0, 0, None)
            tile(1, 1, (0, 0, 0))
            with eng.Fori(1, T // TT // 2) as it:
                tile(it * 2, 0, (it * 2 - 1, 1, it - 1))
                tile(it * 2 + 1, 1, (it * 2, 0, it))

        def rows(h, n):
            return slice((h % 4) * HW, (h % 4) * HW + n)

        def one_bank(b, r):
            return bank[b][r, :].rearrange("p (g t) -> p g t", g=2)

        def two_banks(b, r):
            return ps[r, b:b + 2, :].rearrange("p a (g t) -> p (a g) t", g=2)

        def heads4(v, c):
            return v[:, :, c * D:(c + 1) * D].rearrange("p u (h s) -> p u h s", h=H)

        def over_tiles(w):
            return w[:, :, :, :].rearrange("p c h s -> p (c h s)").unsqueeze(1).broadcast_to([P, 2, 2 * D])

        def turns(turn, eng):
            turn(-3, -2, 1, False, False, False, False, True)
            turn(-2, -1, 0, False, False, False, True, True)
            turn(-1, -1, 1, False, False, True, True, True)
            turn(0, 0, 0, True, False, True, True, True)
            with eng.Fori(0, (B - 4) // 2) as it:
                turn(it * 2 + 1, it, 1, True, True, True, True, True)
                turn(it * 2 + 2, it + 1, 0, True, True, True, True, True)
            turn(B - 3, (B - 3) // 2, 1, True, True, True, True, False)
            turn(B - 2, (B - 2) // 2, 0, True, True, True, False, False)
            turn(B - 1, (B - 1) // 2, 1, True, True, False, False, False)
            turn(B, B // 2, 0, False, True, False, False, False)

        block = ctx.enter_context(nc.Block())

        @block.sync
        def _(sp_):
            for i in range(4):
                n = NT // 4
                sp_.dma_start(x_res[:, i * n:(i + 1) * n, :], x_tok[:, i * n:(i + 1) * n, :]).then_inc(x_in, 16)
            for o, src in ((0, W1), (D, W2), (D + N, W3)):
                sp_.dma_start(w123[:, o:o + src.shape[1]], src).then_inc(small_in, 16)
            for r in range(2):
                for o, src in ((0, b1), (D, b2), (D + N, b3)):
                    n = src.shape[0]
                    sp_.dma_start(bias[:, r, o:o + n],
                                  src.rearrange("(a n) -> a n", a=1).broadcast_to([P, n])).then_inc(small_in, 16)
            sp_.dma_start(wr_s[:, :], Wr).then_inc(small_in, 16)
            for dst, src, arrived in ((stg, Wg, wg_in), (stu, Wu, wu_in)):
                sp_.dma_start(dst[:, :].rearrange("p (e i) -> p e i", e=E1), src.rearrange("e d i -> d e i")).then_inc(arrived, 16)
            for j in range(JC - 1):
                sp_.dma_start(stv[:, :, j, :], Wd[:, j * P:(j + 1) * P, :].rearrange("e p d -> p e d")).then_inc(wd_in, 16)
            sp_.dma_start(stv[0:R1, :, JC - 1, :],
                          Wd[:, (JC - 1) * P:I1, :].rearrange("e p d -> p e d")).then_inc(wd_in, 16)

            def load_block(b, u):
                src = sp_.value_load(blk_src[0:1, ds(b, 1)], min_val=0, max_val=(E1 - 1) * REG + T)
                sp_.dma_start(xb[:, u, :], xs[ds(src, P), :]).then_inc(xb_in[u], 16)

            for u in range(4):
                sp_.sem_inc(ys_out[u], 16)

            def store_block(b, u):
                sp_.wait_ge(yb_r, b + 1)
                sp_.dma_start(ys[ds(b * P, P), :], yb[:, u, :]).then_inc(ys_out[u], 16)

            sp_.wait_ge(list_ready, 1)
            for s in range(2):
                sp_.wait_ge(scat[s], 16 * (SUB * K1 * NPIECE // 2))
            sp_.wait_ge(tails_in, 16 * E1)
            for b in range(4):
                load_block(b, b)
            for b in range(4):
                sp_.wait_ge(xT_r, b + 1)
                load_block(b + 4, b)
                if b >= 2:
                    store_block(b - 2, b - 2)
            with sp_.Fori(1, NBLK // 4 - 1) as it:
                for u in range(4):
                    b = it * 4 + u
                    sp_.wait_ge(xT_r, b + 1)
                    load_block(b + 4, u)
                    store_block(b - 2, (u - 2) % 4)
            for b in range(NBLK - 6, NBLK):
                store_block(b, b % 4)
            for u in range(4):
                sp_.wait_ge(ys_out[u], 16 * (NBLK // 4 + 1))
            for j, w in enumerate((WqT, WkT, WvT)):
                sp_.dma_start(wqkv[:, j * D:(j + 1) * D], w).then_inc(c_in, 16)
            sp_.dma_start(wuT[:, :], WuT).then_inc(c_in, 16)
            for j, w in enumerate((qln_w, kln_w, qln_b, kln_b)):
                sp_.dma_start(ln8[:, j, :], w.rearrange("(a n) -> a n", a=1).broadcast_to([P, S])).then_inc(c_in, 16)
            sp_.dma_start(shf[:, 0:F2], Ws_up).then_inc(sh_in, 16)
            sp_.dma_start(shf[0:F2, F2:F2 + D], Ws_down).then_inc(sh_in, 16)
            sp_.dma_start(cen_s[:, :], cent).then_inc(sh_in, 16)
            sp_.dma_start(ebi[:, :], ebias.rearrange("(a n) -> a n", a=1).broadcast_to([P, E2])).then_inc(sh_in, 16)
            PC = WC // D
            for c in range(NC):
                if c >= 2:
                    sp_.wait_ge(wd_done, c - 1)
                for q in range(PC):
                    pair = (c % (NC // 2)) * PC + q
                    dst = wst[:, c % 2, q * D:(q + 1) * D]
                    if c < NC // 2:
                        sp_.dma_start(dst.rearrange("p (two f) -> p two f", two=2),
                                      W_up[2 * pair:2 * pair + 2].rearrange("two d f -> d two f")).then_inc(w_in[c % 2], 16)
                    else:
                        sp_.dma_start(dst, W_down[2 * pair:2 * pair + 2].rearrange("two f d -> (two f) d")).then_inc(w_in[c % 2], 16)
            for p in range(2):
                sp_.sem_inc(o_out[p], 16)
            for t in range(T // TT):
                sp_.wait_ge(u_y, t + 1)
                sp_.dma_start(out_tok[:, t * SUB:(t + 1) * SUB, :], y4[:, t % 2, :, :]).then_inc(o_out[t % 2], 16)
            for p in range(2):
                sp_.wait_ge(o_out[p], 16 * ((T // TT) // 2 + 1))

        @block.gpsimd
        def _(pool):
            own = Tickets(pool, pool_own)
            own.done(pool.memset(ident[:, :], 0.0))
            own.done(pool.memset(trif[:, :], 1.0))
            own.done(pool.memset(eps_c[:, :], LN_EPS))
            own.done(pool.memset(zrow[:, :], 0.0))
            own.done(pool.memset(base[:, :], 0.0))
            own.done(pool.memset(ones[:, :], 1.0))
            own.done(pool.memset(hb[:, :, :], 0.0))
            for dst, pattern, cm, b0 in ((rev9[:, :, :], [[0, SUB], [-1, E1]], 0, E1), (off9[:, :], [[REG, E1]], 0, 0),
                                         (prow[:, :], [[0, E1]], 1, 0), (iblk[:, :], [[1, NBLK]], 0, 0)):
                own.done(pool.iota(dst, pattern=pattern, base=b0, channel_multiplier=cm,
                                   allow_small_or_imprecise_dtypes=True))
            own.need(own.n)
            own.done(pool.affine_select(out=ident[:, :], in_=ident[:, :], compare_op=ALU.not_equal, fill=1.0,
                                        base=0, pattern=[[-1, P]], channel_multiplier=1))
            own.done(pool.affine_select(out=trif[:, :], in_=trif[:, :], compare_op=ALU.is_gt, fill=0.0,
                                        base=0, pattern=[[1, P]], channel_multiplier=-1))
            own.need(own.n)
            pool.tensor_copy(tri[:, :], trif[:, :]).then_inc(consts, 1)

            for s in range(2):
                pool.sem_inc(scat_ok[s], 1)
            with pool.Fori(0, NPIECE // 2) as it:
                for s in range(2):
                    pool.wait_ge(ps2, it * 2 + s + 1)
                    apart(pool, pool_passed)
                    for k in range(SUB):
                        for c in range(K1):
                            pool.indirect_dma_start(
                                out=xs, out_offset=bass.IndirectOffsetOnAxis(ap=posi[:, s, k, c:c + 1], axis=0),
                                in_=xm[:, s, k, :], in_offset=None).then_inc(scat[s], 16)
                for s in range(2):
                    pool.wait_ge(scat[s], (it + 1) * (16 * SUB * K1))
                    pool.sem_inc(scat_ok[s], 1)
            pool.wait_ge(tails, 1)
            for e in range(E1):
                pool.indirect_dma_start(out=xs, out_offset=bass.IndirectOffsetOnAxis(ap=tail[:, e:e + 1], axis=0),
                                        in_=zrow[:, :], in_offset=None).then_inc(tails_in, 16)

            pool.wait_ge(w_hi, 4)
            pool.tensor_tensor(lv[:, :, 0:JC - 1, :], stv[:, :, 0:JC - 1, :], hv[:, :, 0:JC - 1, :].bitcast(F32),
                               op=ALU.subtract).then_inc(w_lo, 1)
            pool.tensor_tensor(lv[0:R1, :, JC - 1, :], stv[0:R1, :, JC - 1, :], hv[0:R1, :, JC - 1, :].bitcast(F32),
                               op=ALU.subtract).then_inc(w_lo, 1)

            pool.wait_ge(gp_r, 1)
            for u in range(4):
                pool.wait_ge(ys_out[u], 16 * (NBLK // 4 + 1))
            def gather(b, p):
                if not isinstance(b, int) or b >= 2:
                    pool.wait_ge(x2_r, 2 * b - 2)
                    apart(pool, pool_passed)
                pool.tensor_copy(gps[:, p, :], gpi[:, ds(b * (2 * K1), 2 * K1)]).then_inc(gps_r, 1)
                pool.wait_ge(gps_r, b + 1)
                apart(pool, pool_passed)
                for u in range(2):
                    for c in range(K1):
                        pool.indirect_dma_start(
                            out=yg[:, 2 * p + u, c, :], out_offset=None, in_=ys,
                            in_offset=bass.IndirectOffsetOnAxis(ap=gps[:, p, u * K1 + c:u * K1 + c + 1], axis=0),
                        ).then_inc(yg_in[2 * p + u], 16)

            own = Tickets(pool, pool_c)
            own.done(pool.memset(identb[:, :], 0.0))
            own.done(pool.memset(mskf[:, :, :], 0.0))
            own.done(pool.memset(ks[:, :, :, :, :].bitcast(F32), 0.0))
            own.done(pool.memset(vp[:, :, :, :, S:S + 1], 1.0))
            own.need(own.n)
            own.done(pool.affine_select(out=identb[:, :], in_=identb[:, :], compare_op=ALU.not_equal, fill=1.0,
                                        base=0, pattern=[[-1, P]], channel_multiplier=1))
            own.done(pool.affine_select(out=mskf[:, 0, :], in_=mskf[:, 0, :], compare_op=ALU.is_ge, fill=-BIG,
                                        base=0, pattern=[[-1, P]], channel_multiplier=1))
            own.done(pool.affine_select(out=mskf[:, 1, :], in_=mskf[:, 1, :], compare_op=ALU.is_ge, fill=-BIG,
                                        base=0, pattern=[[1, P]], channel_multiplier=-1))
            own.done(pool.memset(ks[:, :, :, :, KS:KS + 2].bitcast(F32), 1.0))
            own.need(own.n)
            pool.sem_inc(c_const, 1)

            def p1_pool(b, p):
                pool.wait_ge(c_n, b + 1)
                pool.tensor_tensor(nq[:, 1, :, :], nq[:, 0, :, :], over_tiles(lnw), op=ALU.mult).then_inc(pool_w, 1)
                pool.wait_ge(pool_w, b + 1)
                pool.tensor_tensor(nq[:, 0, :, :], nq[:, 1, :, :], over_tiles(lnb), op=ALU.add).then_inc(c_wb, 1)

            def p2_pool(b, p):
                if not isinstance(b, int) or b >= 2:
                    pool.wait_ge(c_PV, (b - 1) * 4)
                    apart(pool, pool_passed)
                pool.tensor_copy(vp[:, p, :, :, 0:S],
                                 zs[:, p, :, 2 * D:3 * D].rearrange("p u (h s) -> p u h s", h=H)).then_inc(c_vp, 1)

            def parts(c, p, loads):
                pool.wait_ge(w_in[p], loads)
                apart(pool, pool_passed)
                pool.tensor_copy(wh[:, ds(c * WC, WC)], wst[:, p, :]).then_inc(pool_h, 1)
                pool.wait_ge(pool_h, c + 1)
                apart(pool, pool_passed)
                pool.tensor_tensor(wl[:, ds(c * WC, WC)], wst[:, p, :], wh[:, ds(c * WC, WC)].bitcast(F32),
                                   op=ALU.subtract).then_inc(wd_done, 1)

            def pool_turn(i, half, p, E, F, M, P1, G):
                if G:
                    gather(i + 3, 1 - p)
                if M:
                    p2_pool(i + 1, 1 - p)
                if E:
                    parts(i, p, (half + 1) * (16 * WC // D))
                if P1:
                    p1_pool(i + 2, p)

            turns(pool_turn, pool)
            pool.wait_ge(sh_in, 16 * 4)
            for rows_, cols in ((slice(0, P), slice(0, F2)), (slice(0, F2), slice(F2, F2 + D))):
                pool.tensor_copy(shh[rows_, cols], shf[rows_, cols]).then_inc(sh_done, 1)
            pool.wait_ge(sh_done, 2)
            for rows_, cols in ((slice(0, P), slice(0, F2)), (slice(0, F2), slice(F2, F2 + D))):
                pool.tensor_tensor(shl[rows_, cols], shf[rows_, cols], shh[rows_, cols].bitcast(F32),
                                   op=ALU.subtract).then_inc(sh_done, 1)
            pool.wait_ge(c_F6, B + 1)
            pool.memset(selz[:, :, :], 0.0).then_inc(d_const, 1)
            for k in range(2):
                pool.wait_ge(d_const, k + 1)
                pool.affine_select(out=selz[:, :, :], in_=selz[:, :, :], compare_op=ALU.not_equal, fill=1.0,
                                   base=-k * E2, pattern=[[-1, E2], [0, F2]], channel_multiplier=1).then_inc(d_const, 1)

        @block.scalar
        def _(act):
            TABLE = "natural_log_exp_and_others"
            act.preload_act_table_set(TABLE)
            act.wait_ge(consts, 1)

            def rstd_of(ready, stats, s, i):
                act.wait_ge(stats, i)
                own.link(act.activation(lnv[:, s, :], mv[:, s, :, 1], ACT.Ln, bias=eps_c[:, 0:1]))
                act.activation(rstd[:, s, :], lnv[:, s, :], ACT.Exp, scale=-0.5).then_inc(ready, 1)

            def copy_T(dst, ready, made, s, i):
                act.wait_ge(made, i)
                act.activation(dst[:, s, :, :].rearrange("p k d -> p (k d)"), bank[s][:, :], ACT.Copy).then_inc(ready, 1)

            with act.Fori(0, NPIECE // 2) as it:
                act.preload_act_table_set(TABLE)
                own = Tickets(act, act_own, it * ACT_A)
                for s in range(2):
                    rstd_of(rs1, mv1, s, it * 2 + s + 1)
                for s in range(2):
                    copy_T(xnT, tc1, tr1, s, it * 2 + s + 1)
                q = []
                for s in range(2):
                    act.wait_ge(zc1, it * 2 + s + 1)
                    q.append(own.done(act.activation(sp[:, s, 0, :, :], z[:, s, :, 0:D], ACT.Abs)))
                for s in range(2):
                    own.need(q[s])
                    q.append(own.done(act.activation(sp[:, s, 1, :, :], sp[:, s, 0, :, :], ACT.Exp, scale=-1.0)))
                for s in range(2):
                    own.need(q[2 + s])
                    act.activation(sp[:, s, 0, :, :], sp[:, s, 1, :, :], ACT.Ln, bias=1.0).then_inc(sp1, 1)
                for s in range(2):
                    rstd_of(rs2, mv2, s, it * 2 + s + 1)
                for s in range(2):
                    copy_T(xnT, tc2, tr2, s, it * 2 + s + 1)
                for s in range(2):
                    act.wait_ge(df2, it * 2 + s + 1)
                    act.activation(r1[:, s, 4, :], r1[:, s, 3, :], ACT.Exp).then_inc(ex2, 1)
                assert own.n == ACT_A, own.n

            for src_in, src, hi in ((wg_in, stg, wgh), (wu_in, stu, wuh)):
                act.wait_ge(src_in, 16)
                act.activation(hi[:, :], src[:, :], ACT.Copy).then_inc(w_hi, 1)
            act.wait_ge(wd_in, 16 * JC)
            act.activation(hv[:, :, 0:JC - 1, :], stv[:, :, 0:JC - 1, :], ACT.Copy).then_inc(w_hi, 1)
            act.activation(hv[0:R1, :, JC - 1, :], stv[0:R1, :, JC - 1, :], ACT.Copy).then_inc(w_hi, 1)

            def x_hi(b, v):
                act.wait_ge(xT_r, b + 1)
                act.activation(xbh[:, v, :], bank[0][:, 0:D], ACT.Copy).then_inc(xh_r, 1)

            def silu(b, v):
                act.wait_ge(gu_r, b + 1)
                act.activation(sg[:, v, :], bank[4 + v][:, 0:I1], ACT.Silu).then_inc(sg_r, 1)

            def h_hi(b, v):
                act.wait_ge(hT_r, b + 1)
                act.activation(hh[:, v, :], bank[2 + v][:, 0:IP], ACT.Copy).then_inc(hh_r, 1)

            def y_out(b, u, again):
                act.wait_ge(y_r, b + 1)
                if again is not None:
                    act.wait_ge(ys_out[u], again + 16)
                act.activation(yb[:, u, :], bank[1][:, 0:D], ACT.Copy).then_inc(yb_r, 1)

            x_hi(0, 0)
            for b in range(4):
                silu(b, b % 2)
                x_hi(b + 1, (b + 1) % 2)
                if b >= 1:
                    h_hi(b - 1, (b - 1) % 2)
                if b >= 2:
                    y_out(b - 2, b - 2, None)
            with act.Fori(1, NBLK // 4 - 1) as it:
                for u in range(4):
                    b = it * 4 + u
                    silu(b, u % 2)
                    x_hi(b + 1, (u + 1) % 2)
                    h_hi(b - 1, (u - 1) % 2)
                    y_out(b - 2, (u - 2) % 4, (it if u >= 2 else it - 1) * 16)
            for b in range(NBLK - 4, NBLK + 2):
                if b < NBLK:
                    silu(b, b % 2)
                if b + 1 < NBLK:
                    x_hi(b + 1, (b + 1) % 2)
                if b - 1 < NBLK:
                    h_hi(b - 1, (b - 1) % 2)
                y_out(b - 2, (b - 2) % 4, 16 * ((b - 2) // 4))

            act.wait_ge(c_in, 16 * 8)
            act.wait_ge(c_const, 1)
            act.activation(wqh[:, :], wqkv[:, :], ACT.Copy).then_inc(c_w, 1)
            act.activation(idr[:, 1, :], ident[:, :], ACT.Copy).then_inc(c_w, 1)
            act.wait_ge(c_w, 6)

            def act_turn(i, half, p, E, F, M, P1, G):
                if not isinstance(i, int) or i in (-3, B - 3):
                    act.preload_act_table_set(TABLE)

                b1, b2 = i + 1, i + 2

                def exp(g):
                    if E:
                        act.wait_ge(c_S2, i * 4 + g + 1)
                        if g >= 2 or not isinstance(i, int) or i > 0:
                            act.wait_ge(c_PV, i * 4 + g - 1)
                        act.activation(pt[:, g % 2, :, :, :].rearrange("p b j k -> p (b j k)"),
                                       ps[:, 0:3, :].rearrange("p b k -> p (b k)"), ACT.Exp).then_inc(c_P, 1)

                def out_copy(g):
                    if E:
                        act.wait_ge(c_PV, i * 4 + g + 1)
                        act.activation(ot[:, p, g, :], bank[6][:, 0:2 * P], ACT.Copy).then_inc(c_OT, 1)

                def q2_copies(b, c):
                    act.wait_ge(c_T2, 2 * b + c + 1)
                    for j in range(QA):
                        ins = act.activation(qz[rows(j, HW), 2 * c:2 * c + 2, j, :], one_bank(7, rows(j, HW)), ACT.Copy)
                    ins.then_inc(c_q2, 1)

                def z_copy(u):
                    if P1:
                        act.wait_ge(c_z, 2 * b2 + u + 1)
                        act.activation(zs[:, p, u, :], bank[7][:, 0:3 * D], ACT.Copy).then_inc(c_zs, 1)

                if M:
                    act.wait_ge(c_T3, b1 + 1)
                    act.activation(kz[rows(0, KS), :, 0, :], two_banks(3, rows(0, KS)), ACT.Copy)
                if P1:
                    act.wait_ge(c_xT, b2 + 1)
                    act.activation(xch[:, :, :], bank[7][:, 0:2 * P].rearrange("p (u t) -> p u t", u=2),
                                   ACT.Copy).then_inc(c_xh, 1)
                if M:
                    for j in range(1, KA):
                        act.activation(kz[rows(j, KS), :, j, :], two_banks(3, rows(j, KS)), ACT.Copy)
                    low = slice(0, KA * HW)
                    act.activation(kT[low, 1 - p, :, :], two_banks(3, low), ACT.Copy).then_inc(c_kz, 1)
                    act.wait_ge(c_T, b1 + 1)
                    act.activation(qT[:, :, :], two_banks(5, rows(0, P)), ACT.Copy).then_inc(c_qT, 1)
                exp(0)
                z_copy(0)
                if G:
                    act.wait_ge(c_mv, i + 4)
                    act.activation(cln[:, :], cmv[:, :, 1], ACT.Ln, bias=eps_c[:, 0:1]).then_inc(act_c, 1)
                    act.wait_ge(act_c, i + 4)
                    act.activation(crs[:, :], cln[:, :], ACT.Exp, scale=-0.5).then_inc(c_rs, 1)
                exp(1)
                z_copy(1)
                out_copy(0)
                if E:
                    q2_copies(i, 1)
                if P1:
                    act.wait_ge(c_cen, b2 + 1)
                    act.activation(csq[:, :, :], cen[:, :, :], ACT.Square).then_inc(c_sq, 1)
                out_copy(1)
                exp(2)
                if P1:
                    act.wait_ge(c_vs, b2 + 1)
                    act.activation(rql[:, :, :], vsm[:, :, :], ACT.Ln, bias=eps_c[:, 0:1], scale=1.0 / S).then_inc(act_c2, 1)
                    act.wait_ge(act_c2, b2 + 1)
                    act.activation(rq[:, :, :], rql[:, :, :], ACT.Exp, scale=-0.5).then_inc(c_rq, 1)
                out_copy(2)
                if F:
                    act.wait_ge(c_F3, i)
                    act.activation(ooT[:, :, :], bank[7][:, 0:2 * P].rearrange("p (u t) -> p u t", u=2),
                                   ACT.Copy).then_inc(c_F4, 1)
                exp(3)
                if P1:
                    act.wait_ge(c_wb, b2 + 1)
                    for dst, c, o in ((qs, 0, 0), (ks, 1, 0), (qs, 0, S), (ks, 1, 2 * S)):
                        ins = act.activation(dst[:, p, :, :, o:o + S], heads4(nq[:, 0, :, :], c), ACT.Copy)
                        if o == 0 and c == 1:
                            ins.then_inc(c_nh, 1)
                    ins.then_inc(c_dup, 1)
                if M:
                    q2_copies(b1, 0)
                out_copy(3)

            turns(act_turn, act)

            act.wait_ge(d_const, 3)
            act.activation(selr[:, :], selz[:, :, :].rearrange("p e f -> p (e f)"), ACT.Copy).then_inc(d_sel, 1)
            with act.Fori(0, NPIECE // 2) as it:
                act.preload_act_table_set(TABLE)
                for s in range(2):
                    act.wait_ge(d_mv, it * 2 + s + 1)
                    act.activation(lnv[:, s, :], mv[:, s, :, 1], ACT.Ln, bias=eps_c[:, 0:1]).then_inc(act_d, 1)
                    act.wait_ge(act_d, it * 2 + s + 1)
                    act.activation(rstd[:, s, :], lnv[:, s, :], ACT.Exp, scale=-0.5).then_inc(d_rs, 1)
                for s in range(2):
                    copy_T(xnT4, d_Tc, d_T, s, it * 2 + s + 1)
                for s in range(2):
                    act.wait_ge(d_afc, it * 2 + s + 1)
                    act.activation(g4[:, s, 0, :, :], af[:, s, :, :], ACT.Exp, scale=-1.0).then_inc(d_ex, 1)
                for s in range(2):
                    act.wait_ge(d_cT, it * 2 + s + 1)
                    apart(act, act_passed)
                    act.activation(cwT[:, ds((it * 2 + s) * TT, TT)], bank[4 + s][:, :], ACT.Copy).then_inc(d_cw, 1)

            def e_silu(t, u):
                act.wait_ge(u_up, t * NU + u + 1)
                r = slice(0, F2 if u == 0 else P)
                if u == 0:
                    if not (isinstance(t, int) and t == 0):
                        act.wait_ge(u_hl, t * NU - 2)
                    act.activation(h4[r, u % 3, :], bank[u % 3][r, :], ACT.Silu).then_inc(u_sg0, 1)
                else:
                    act.activation(sg4[r, u % 3, :], bank[u % 3][r, :], ACT.Silu).then_inc(u_sg, 1)

            def e_hi(t, u):
                r = slice(0, F2 if u == 0 else P)
                if u == 0:
                    act.wait_ge(u_sg0, t + 1)
                else:
                    act.wait_ge(u_h, t * NP2 + u)
                if u >= 3:
                    act.wait_ge(u_dn, t * NU + u - 2)
                elif not (isinstance(t, int) and t == 0):
                    act.wait_ge(u_dn, (t - 1) * NU + NU + u - 2)
                act.activation(hh4[r, u % 3, :], h4[r, u % 3, :], ACT.Copy).then_inc(u_hh, 1)

            def out_copy4(t, p):
                act.wait_ge(u_dn, (t + 1) * NU)
                act.activation(oT4[:, :], bank[5 + 2 * p][:, :], ACT.Copy).then_inc(u_oT, 1)

            def act_tile(t, p, before):
                for u in range(NU):
                    e_silu(t, u)
                    if u >= 1:
                        e_hi(t, u - 1)
                    elif before is not None:
                        e_hi(before[0], NU - 1)
                    if u == 5 and before is not None:
                        out_copy4(before[0], before[1])

            tiles_of(act, act_tile)
            e_hi(T // TT - 1, NU - 1)
            out_copy4(T // TT - 1, 1)

        @block.vector
        def _(dve):
            dve.wait_ge(x_in, 64)
            dve.wait_ge(consts, 1)
            dve.wait_ge(small_in, 16 * 10)

            def stats(own, s, t0, ready):
                for k in range(SUB):
                    last = own.done(dve.bn_stats(out=st[:, s, k, :], in_=x_res[:, ds(t0 + k, 1), :]))
                own.need(last)
                apart(dve, dve_passed)
                for k in range(SUB):
                    ins = dve.bn_aggr(out=mv[:, s, k, :], in_=st[:, s, k, :])
                ins.then_inc(ready, 1)

            def normed(dst, s, t0, scaled, i, ready):
                dve.wait_ge(scaled, i)
                for k in range(SUB):
                    ins = dve.tensor_scalar(dst[:, s, k:k + 1, :], x_res[:, ds(t0 + k, 1), :], mv[:, s, k, 0:1],
                                            rstd[:, s, k:k + 1], ALU.subtract, ALU.mult)
                ins.then_inc(ready, 1)

            with dve.Fori(0, NPIECE // 2) as it:
                own = Tickets(dve, dve_own, it * DVE_A)
                for s in range(2):
                    stats(own, s, (it * 2 + s) * SUB, mv1)
                for s in range(2):
                    normed(xn, s, (it * 2 + s) * SUB, rs1, it * 2 + s + 1, xn1)
                q = []
                for s in range(2):
                    dve.wait_ge(zz1, it * 2 + s + 1)
                    zv = z[:, s, :, :].rearrange("p (a b) m -> p a (b m)", a=2)
                    for a in range(2):
                        ins = dve.tensor_tensor(zv[:, a, :], bank[2 + 2 * s + a][:, 0:2 * M1],
                                                bias[:, :, :].rearrange("p a m -> p (a m)"), op=ALU.add)
                    ins.then_inc(zc1, 1)
                for s in range(2):
                    dve.wait_ge(zc1, it * 2 + s + 1)
                    q.append(own.done(dve.tensor_tensor(bc[:, s, :, :], z[:, s, :, D:D + N], z[:, s, :, D + N:M1],
                                                        op=ALU.mult)))
                for s in range(2):
                    own.need(q[s])
                    own.done(dve.tensor_reduce(bcs[:, s, :], bc[:, s, :, :], axis=AX.X, op=ALU.add))
                q = []
                for s in range(2):
                    dve.wait_ge(sp1, it * 2 + s + 1)
                    q.append(own.done(dve.scalar_tensor_tensor(
                        sp[:, s, 1, :, :], z[:, s, :, 0:D], 0.0, sp[:, s, 0, :, :], ALU.max, ALU.add)))
                for s in range(2):
                    own.need(q[s])
                    q.append(own.done(dve.tensor_tensor(sp[:, s, 2, :, :], sp[:, s, 1, :, :], xn[:, s, :, :], op=ALU.mult)))
                for s in range(2):
                    own.need(q[2 + s])
                    for k in range(SUB):
                        t = ds((it * 2 + s) * SUB + k, 1)
                        q.append(own.done(dve.scalar_tensor_tensor(
                            x_res[:, t, :], sp[:, s, 2, k:k + 1, :], bcs[:, s, k:k + 1], x_res[:, t, :],
                            ALU.mult, ALU.add)))
                for s in range(2):
                    own.need(q[4 + SUB * (s + 1) - 1])
                    apart(dve, dve_passed)
                    stats(own, s, (it * 2 + s) * SUB, mv2)
                for s in range(2):
                    dve.wait_ge(scat_ok[s], it + 1)
                    normed(xm, s, (it * 2 + s) * SUB, rs2, it * 2 + s + 1, xn2)
                q = []
                for s in range(2):
                    dve.wait_ge(lg2, it * 2 + s + 1)
                    q.append(own.done(dve.tensor_copy(
                        lg[:, s, :, :], bank[2 + 2 * s][:, 0:16 * SUB].rearrange("p (k e) -> p k e", e=16)[:, :, 0:E1])))

                def both(op):
                    was = list(q)
                    for s in range(2):
                        own.need(was[s])
                        q[s] = own.done(op(s))

                def wide(v):
                    return v.unsqueeze(2).broadcast_to([P, SUB, E1])

                def tiles(s):
                    return ds((it * 2 + s) * SUB, SUB)

                for c in range(K1):
                    row = (lambda s: lg[:, s, :, :]) if c == 0 else (lambda s: r9[:, s, 2, :, :])
                    both(lambda s: dve.tensor_reduce(r1[:, s, c, :], row(s), axis=AX.X, op=ALU.max))
                    both(lambda s: dve.tensor_tensor(r9[:, s, 0, :, :], row(s), wide(r1[:, s, c, :]), op=ALU.is_equal))
                    both(lambda s: dve.tensor_tensor(r9[:, s, 1, :, :], r9[:, s, 0, :, :], rev9[:, :, :], op=ALU.mult))
                    both(lambda s: dve.tensor_reduce(r1[:, s, 2, :], r9[:, s, 1, :, :], axis=AX.X, op=ALU.max))
                    both(lambda s: dve.tensor_tensor(pick[:, tiles(s), c, :], r9[:, s, 1, :, :], wide(r1[:, s, 2, :]),
                                                     op=ALU.is_equal))
                    if c == 0:
                        both(lambda s: dve.scalar_tensor_tensor(r9[:, s, 2, :, :], pick[:, tiles(s), c, :], -BIG,
                                                                lg[:, s, :, :], ALU.mult, ALU.add))
                for s in range(2):
                    dve.tensor_tensor(r1[:, s, 3, :], r1[:, s, 1, :], r1[:, s, 0, :], op=ALU.subtract).then_inc(df2, 1)
                for s in range(2):
                    own.need(q[s])
                    dve.tensor_tensor(sel[:, s, :, :], pick[:, tiles(s), 0, :], pick[:, tiles(s), 1, :],
                                      op=ALU.add).then_inc(sl2, 1)
                for s in range(2):
                    dve.wait_ge(ex2, it * 2 + s + 1)
                    q[s] = own.done(dve.tensor_scalar(r1[:, s, 5, :], r1[:, s, 4, :], 1.0, None, ALU.add))
                both(lambda s: dve.reciprocal(r1[:, s, 6, :], r1[:, s, 5, :]))
                both(lambda s: dve.tensor_scalar(wgt[:, tiles(s), 0], r1[:, s, 6, :], 0.0, None, ALU.add))
                both(lambda s: dve.tensor_tensor(wgt[:, tiles(s), 1], r1[:, s, 6, :], r1[:, s, 4, :], op=ALU.mult))
                for s in range(2):
                    dve.wait_ge(rk2, it * 2 + s + 1)
                    own.link(dve.tensor_tensor(
                        r9[:, s, 3, :, :], bank[3 + 2 * s][:, 0:SUB * E1].rearrange("p (k e) -> p k e", e=E1),
                        base[:, :].unsqueeze(1).broadcast_to([P, SUB, E1]), op=ALU.add))
                    own.done(dve.tensor_tensor(base[:, :], bank[3 + 2 * s][:, SUB * E1:(SUB + 1) * E1], base[:, :],
                                               op=ALU.add))
                    own.link(dve.tensor_tensor(
                        r9[:, s, 4, :, :], r9[:, s, 3, :, :],
                        off9[:, :].unsqueeze(1).broadcast_to([P, SUB, E1]), op=ALU.add))
                    for c in range(K1):
                        own.done(dve.tensor_tensor(r9[:, s, c, :, :], r9[:, s, 4, :, :], pick[:, tiles(s), c, :],
                                                   op=ALU.mult))
                    own.need(own.n)
                    for c in range(K1):
                        own.done(dve.tensor_reduce(posf[:, tiles(s), c], r9[:, s, c, :, :], axis=AX.X, op=ALU.add))
                    own.need(own.n)
                    apart(dve, dve_passed)
                    dve.tensor_copy(posi[:, s, :, :], posf[:, tiles(s), :]).then_inc(ps2, 1)
                assert own.n == DVE_A, own.n

            own = Tickets(dve, dve_own, (NPIECE // 2) * DVE_A)
            own.link(dve.tensor_tensor(q9[:, 0, :], base[:, :], off9[:, :], op=ALU.add))
            own.done(dve.tensor_scalar(cnti[:, :], base[:, :], float(P - 1), None, ALU.add))
            own.link(dve.tensor_tensor(q9[:, 1, :], q9[:, 0, :], prow[:, :], op=ALU.add))
            dve.tensor_copy(tail[:, :], q9[:, 1, :]).then_inc(tails, 1)
            own.link(dve.tensor_single_scalar(cnti[:, :], cnti[:, :], 7, ALU.logical_shift_right))
            own.link(dve.tensor_copy(nblk[:, :], cnti[:, :]))
            own.link(dve.tensor_copy(bend[:, 0:1], nblk[:, 0:1]))
            for e in range(1, E1):
                own.link(dve.tensor_tensor(bend[:, e:e + 1], bend[:, e - 1:e], nblk[:, e:e + 1], op=ALU.add))
            own.link(dve.tensor_tensor(bstart[:, :], bend[:, :], nblk[:, :], op=ALU.subtract))
            own.link(dve.scalar_tensor_tensor(q9[:, 2, :], bstart[:, :], -float(P), off9[:, :], ALU.mult, ALU.add))

            def over_e(v):
                return v.unsqueeze(2).broadcast_to([P, NBLK, E1])

            def over_b(v):
                return v.unsqueeze(1).broadcast_to([P, NBLK, E1])

            own.done(dve.tensor_tensor(b9[:, 0, :, :], over_e(iblk[:, :]), over_b(bstart[:, :]), op=ALU.is_ge))
            own.done(dve.tensor_tensor(b9[:, 1, :, :], over_e(iblk[:, :]), over_b(bend[:, :]), op=ALU.is_lt))
            own.need(own.n)
            own.done(dve.tensor_tensor(b9[:, 2, :, :], b9[:, 0, :, :], b9[:, 1, :, :], op=ALU.mult))
            own.need(own.n)
            own.link(dve.tensor_tensor(b9[:, 0, :, :], over_e(iblk[:, :]), over_b(bend[:, :]), op=ALU.is_ge))
            own.done(dve.tensor_reduce(bf[:, 0, :], b9[:, 0, :, :], axis=AX.X, op=ALU.add))
            own.link(dve.tensor_tensor(b9[:, 1, :, :], b9[:, 2, :, :], over_b(q9[:, 2, :]), op=ALU.mult))
            own.done(dve.tensor_reduce(bf[:, 1, :], b9[:, 1, :, :], axis=AX.X, op=ALU.add))
            own.done(dve.tensor_reduce(bf[:, 2, :], b9[:, 2, :, :], axis=AX.X, op=ALU.add))
            own.link(dve.tensor_scalar(bf[:, 0, :], bf[:, 0, :], float(E1 - 1), None, ALU.min))
            own.link(dve.scalar_tensor_tensor(b9[:, 0, 0:NBLK, 0], iblk[:, :], float(P), bf[:, 2, :], ALU.mult, ALU.mult))
            own.link(dve.tensor_tensor(bf[:, 1, :], bf[:, 1, :], b9[:, 0, 0:NBLK, 0], op=ALU.add))
            own.link(dve.tensor_scalar(bf[:, 2, :], bf[:, 2, :], -float((E1 - 1) * REG), float((E1 - 1) * REG),
                                       ALU.mult, ALU.add))
            own.link(dve.tensor_tensor(bf[:, 1, :], bf[:, 1, :], bf[:, 2, :], op=ALU.add))
            own.done(dve.tensor_copy(blk_e[:, :], bf[:, 0, :]))
            dve.tensor_copy(blk_src[:, :], bf[:, 1, :]).then_inc(list_ready, 1)
            pk = pick[:, :, :, :].rearrange("p t c e -> p (t c) e")
            own.link(dve.tensor_tensor(gp9[:, :, :], pk, q9[:, 2, :].unsqueeze(1).broadcast_to([P, NT * K1, E1]),
                                       op=ALU.mult))
            own.link(dve.tensor_reduce(gpf[:, :], gp9[:, :, :], axis=AX.X, op=ALU.add))
            own.link(dve.tensor_tensor(gpf[:, :], posf[:, :, :].rearrange("p t c -> p (t c)"), gpf[:, :], op=ALU.subtract))
            dve.tensor_copy(gpi[:, :], gpf[:, :]).then_inc(gp_r, 1)

            for i, (src, hi, lo) in enumerate(((stg, wgh, wgl), (stu, wuh, wul))):
                dve.wait_ge(w_hi, i + 1)
                dve.tensor_tensor(lo[:, :], src[:, :], hi[:, :].bitcast(F32), op=ALU.subtract).then_inc(w_lo, 1)

            def x_lo(b, v):
                dve.wait_ge(xh_r, b + 1)
                dve.tensor_tensor(xbl[:, v, :], bank[0][:, 0:D], xbh[:, v, :].bitcast(F32),
                                  op=ALU.subtract).then_inc(xl_r, 1)

            def h_of(b, v):
                dve.wait_ge(sg_r, b + 1)
                dve.tensor_tensor(hb[:, v, 0:I1], sg[:, v, :], bank[6 + v][:, 0:I1], op=ALU.mult).then_inc(h_r, 1)

            def h_lo(b, v, first):
                dve.wait_ge(hh_r, b + 1)
                if not first:
                    dve.wait_ge(y_r, b - 1)
                dve.tensor_tensor(hl[:, v, :], bank[2 + v][:, 0:IP], hh[:, v, :].bitcast(F32),
                                  op=ALU.subtract).then_inc(hl_r, 1)

            x_lo(0, 0)
            for b in range(4):
                h_of(b, b % 2)
                x_lo(b + 1, (b + 1) % 2)
                if b >= 1:
                    h_lo(b - 1, (b - 1) % 2, b < 3)
            with dve.Fori(1, NBLK // 4 - 1) as it:
                for u in range(4):
                    b = it * 4 + u
                    h_of(b, u % 2)
                    x_lo(b + 1, (u + 1) % 2)
                    h_lo(b - 1, (u - 1) % 2, False)
            for b in range(NBLK - 4, NBLK + 1):
                if b < NBLK:
                    h_of(b, b % 2)
                if b + 1 < NBLK:
                    x_lo(b + 1, (b + 1) % 2)
                h_lo(b - 1, (b - 1) % 2, False)

            def add_rows(b, p, loads):
                for u in range(2):
                    dve.wait_ge(yg_in[2 * p + u], loads)
                for c in range(K1):
                    for u in range(2):
                        t = ds(2 * b + u, 1)
                        if c == 1:
                            dve.wait_ge(x2_half, 2 * b + u + 1)
                        dve.scalar_tensor_tensor(x_res[:, t, :], yg[:, 2 * p + u, c:c + 1, :], wgt[:, t, c],
                                                 x_res[:, t, :], ALU.mult, ALU.add).then_inc(x2_half if c == 0 else x2_r, 1)

            for u in range(4):
                dve.wait_ge(ys_out[u], 16 * (NBLK // 4 + 1))
            dve.sem_inc(c_F6, 1)
            for zeros in (kz, qz):
                dve.memset(zeros[:, :, :, :].rearrange("p g j t -> p (g j t)").bitcast(F32), 0.0)
            dve.memset(idr[:, 0, :].bitcast(F32), 0.0)
            dve.memset(idr[:, 2, :].bitcast(F32), 0.0)
            dve.memset(qs[:, :, :, :, :].bitcast(F32), 0.0).then_inc(c_w, 1)
            dve.wait_ge(c_in, 16 * 8)
            dve.wait_ge(c_const, 1)
            apart(dve, dve_passed)
            for which in range(2):
                for j in range(4):
                    dve.tensor_copy(msk[:, which, j, :], mskf[:, which, :])
            dve.wait_ge(c_w, 3)
            dve.tensor_tensor(wql[:, :], wqkv[:, :], wqh[:, :].bitcast(F32), op=ALU.subtract).then_inc(c_w, 1)
            scale = 1.0 / float(S) ** 0.5
            for j, (dst, c) in enumerate(((lnw, 0), (lnw, 1), (lnb, 0), (lnb, 1))):
                ins = dve.tensor_scalar(dst[:, c, :, :], ln8[:, j, :].unsqueeze(1).broadcast_to([P, H, S]),
                                        scale if c == 0 else 1.0, None, ALU.mult)
                if j % 2:
                    ins.then_inc(c_w, 1)

            def dve_turn(i, half, p, E, F, M, P1, G):
                b1, b2 = i + 1, i + 2

                def attended(u):
                    if F:
                        dve.wait_ge(c_F1, 2 * i - 1 + u)
                        o = bank[7][:, :].rearrange("p (h w) -> p h w", w=HW)
                        dve.reciprocal(rc[:, u, :], o[:, :, S]).then_inc(dve_cf, 1)
                        dve.wait_ge(dve_cf, 2 * i - 1 + u)
                        dve.tensor_tensor(oo[:, u, :].rearrange("p (h s) -> p h s", h=H), o[:, :, 0:S],
                                          rc[:, u, :].unsqueeze(2).broadcast_to([P, H, S]), op=ALU.mult).then_inc(c_F2, 1)

                def maxima(g):
                    if M:
                        dve.wait_ge(c_S1, b1 * 4 + g + 1)
                        for u, o in ((0, bank[3].rearrange("p (j k) -> p j k", j=4)),
                                     (1, ps[:, 4:6, :].rearrange("p b (j k) -> p (b j) k", j=2))):
                            ins = dve.tensor_reduce(nm[:, u, 4 * g:4 * g + 4], o, axis=AX.X, op=ALU.max, negate=True)
                        ins.then_inc(c_mx, 1)

                def q2_copies(b, c):
                    dve.wait_ge(c_T2, 2 * b + c + 1)
                    for j in range(QA, 4):
                        ins = dve.tensor_copy(qz[rows(j, HW), 2 * c:2 * c + 2, j, :], one_bank(7, rows(j, HW)))
                    ins.then_inc(c_q2d, 1)

                def place_maxima(c):
                    hs = slice(8 * c, 8 * c + 8)
                    dve.wait_ge(c_mx, b1 * 4 + 2 * c + 2)
                    dve.tensor_scalar(nmh[:, :, hs], nm[:, :, hs], 0.0, None, ALU.add).then_inc(dve_nm, 1)
                    dve.wait_ge(dve_nm, b1 * 2 + c + 1)
                    dve.tensor_copy(qs[:, 1 - p, :, hs, KS], nmh[:, :, hs].bitcast(F32))
                    dve.tensor_tensor(qs[:, 1 - p, :, hs, KS + 1], nm[:, :, hs], nmh[:, :, hs].bitcast(F32),
                                      op=ALU.subtract).then_inc(c_nm, 1)

                if M:
                    dve.wait_ge(c_T3, b1 + 1)
                    for j in range(KA, 4):
                        dve.tensor_copy(kz[rows(j, KS), :, j, :], two_banks(3, rows(j, KS)))
                if P1:
                    dve.wait_ge(c_xh, b2 + 1)
                    dve.tensor_tensor(xcl[:, :, :], bank[7][:, 0:2 * P].rearrange("p (u t) -> p u t", u=2),
                                      xch[:, :, :].bitcast(F32), op=ALU.subtract).then_inc(c_xl, 1)
                if M:
                    high = slice(KA * HW, P)
                    dve.tensor_copy(kT[high, 1 - p, :, :], two_banks(3, high)).then_inc(c_kT, 1)
                if G:
                    b3 = i + 3
                    add_rows(b3, 1 - p, (half + 2 + p) * (16 * K1))
                    dve.wait_ge(x2_r, 2 * b3 + 2)
                    apart(dve, dve_passed)
                    ln = Tickets(dve, dve_ln, b3 * 2)
                    for u in range(2):
                        t = ln.done(dve.bn_stats(out=cst[:, u, :], in_=x_res[:, ds(b3 * 2 + u, 1), :]))
                    ln.need(t)
                    apart(dve, dve_passed)
                    for u in range(2):
                        ins = dve.bn_aggr(out=cmv[:, u, :], in_=cst[:, u, :])
                    ins.then_inc(c_mv, 1)
                maxima(0)
                if G:
                    dve.wait_ge(c_rs, b3 + 1)
                    for u in range(2):
                        ins = dve.tensor_scalar(xc[:, u:u + 1, :], x_res[:, ds(b3 * 2 + u, 1), :], cmv[:, u, 0:1],
                                                crs[:, u:u + 1], ALU.subtract, ALU.mult)
                    ins.then_inc(c_xn, 1)
                if P1:
                    own = Tickets(dve, dve_c1, b2)
                    dve.wait_ge(c_zs, b2 * 2 + 2)
                    own.link(dve.tensor_reduce(ms[:, :, :], zs[:, p, :, 0:2 * D].rearrange("p u (g s) -> p u g s", s=S),
                                               axis=AX.X, op=ALU.add))
                    for u in range(2):
                        ins = dve.scalar_tensor_tensor(
                            cen[:, u, :].rearrange("p (g s) -> p g s", s=S),
                            ms[:, u, :].unsqueeze(2).broadcast_to([P, 2 * H, S]), -1.0 / S,
                            zs[:, p, u, 0:2 * D].rearrange("p (g s) -> p g s", s=S), ALU.mult, ALU.add)
                    ins.then_inc(c_cen, 1)
                if E:
                    q2_copies(i, 1)
                if P1:
                    dve.wait_ge(c_sq, b2 + 1)
                    dve.tensor_reduce(vsm[:, :, :], csq[:, :, :].rearrange("p u (g s) -> p u g s", s=S),
                                      axis=AX.X, op=ALU.add).then_inc(c_vs, 1)
                maxima(1)
                if M:
                    place_maxima(0)
                attended(0)
                if P1:
                    dve.wait_ge(c_rq, b2 + 1)
                    if not isinstance(i, int) or i > -2:
                        dve.wait_ge(c_lo, b2)
                    dve.tensor_tensor(nq[:, 0, :, :].rearrange("p u (g s) -> p u g s", s=S),
                                      cen[:, :, :].rearrange("p u (g s) -> p u g s", s=S),
                                      rq[:, :, :].unsqueeze(3).broadcast_to([P, 2, 2 * H, S]), op=ALU.mult).then_inc(c_n, 1)
                attended(1)
                maxima(2)
                if P1:
                    dve.wait_ge(c_nh, b2 + 1)
                    for dst, c, o in ((qs, 0, 2 * S), (ks, 1, S)):
                        ins = dve.tensor_tensor(dst[:, p, :, :, o:o + S], heads4(nq[:, 0, :, :], c),
                                                dst[:, p, :, :, 0:S].bitcast(F32), op=ALU.subtract)
                    ins.then_inc(c_lo, 1)
                if M:
                    q2_copies(b1, 0)
                maxima(3)
                if M:
                    place_maxima(1)
                if F:
                    dve.wait_ge(c_F5, i)
                    t = ds((i - 1) * 2, 2)
                    dve.tensor_tensor(x_res[:, t, :], bank[7][:, 0:2 * D].rearrange("p (u d) -> p u d", u=2),
                                      x_res[:, t, :], op=ALU.add).then_inc(c_F6, 1)

            turns(dve_turn, dve)

            with dve.Fori(0, NPIECE // 2) as it:
                own = Tickets(dve, dve_d, it * DVE_D)
                for s in range(2):
                    stats(own, s, (it * 2 + s) * SUB, d_mv)
                for s in range(2):
                    normed(xm4, s, (it * 2 + s) * SUB, d_rs, it * 2 + s + 1, d_xn)
                for s in range(2):
                    dve.wait_ge(d_Tc, it * 2 + s + 1)
                    tok = ds((it * 2 + s) * TT, TT)
                    apart(dve, dve_passed)
                    own.link(dve.tensor_copy(xh4[:, tok], xnT4[:, s, :, :].rearrange("p k t -> p (k t)")))
                    dve.tensor_tensor(xl4[:, tok], xnT4[:, s, :, :].rearrange("p k t -> p (k t)"),
                                      xh4[:, tok].bitcast(F32), op=ALU.subtract)
                q = []
                for s in range(2):
                    dve.wait_ge(d_af, it * 2 + s + 1)
                    dve.tensor_copy(af[:, s, :, :], bank[2 + s][:, 0:SUB * E2].rearrange("p (k e) -> p k e", e=E2)).then_inc(d_afc, 1)
                for s in range(2):
                    dve.wait_ge(d_afc, it * 2 + s + 1)
                    q.append(own.done(dve.tensor_tensor(bi[:, s, :, :], af[:, s, :, :],
                                                        ebi[:, :].unsqueeze(1).broadcast_to([P, SUB, E2]), op=ALU.add)))
                for s in range(2):
                    own.need(q[s])
                    apart(dve, dve_passed)
                    for k in range(SUB):
                        t = own.done(dve.max(out=m8[:, s, k, :], in_=bi[:, s, k, :]))
                    q[s] = t
                for s in range(2):
                    own.need(q[s])
                    apart(dve, dve_passed)
                    for k in range(SUB):
                        t = own.done(dve.match_replace(out=mr[:, s, k, :], in_to_replace=m8[:, s, k, :],
                                                       in_values=bi[:, s, k, :], imm_value=-BIG))
                    q[s] = t
                both4(lambda s: dve.tensor_tensor(g4[:, s, 1, :, :], mr[:, s, :, :], bi[:, s, :, :], op=ALU.not_equal), q, own)
                for s in range(2):
                    dve.wait_ge(d_ex, it * 2 + s + 1)
                    q[s] = own.done(dve.tensor_scalar(g4[:, s, 2, :, :], g4[:, s, 0, :, :], 1.0, None, ALU.add))
                both4(lambda s: dve.reciprocal(g4[:, s, 3, :, :], g4[:, s, 2, :, :]), q, own)
                both4(lambda s: dve.tensor_tensor(g4[:, s, 4, :, :], g4[:, s, 3, :, :], g4[:, s, 1, :, :], op=ALU.mult), q, own)
                both4(lambda s: dve.tensor_reduce(s4[:, s, 0, :], g4[:, s, 4, :, :], axis=AX.X, op=ALU.add), q, own)
                both4(lambda s: dve.tensor_scalar(s4[:, s, 1, :], s4[:, s, 0, :], 1e-8, None, ALU.add), q, own)
                both4(lambda s: dve.reciprocal(s4[:, s, 2, :], s4[:, s, 1, :]), q, own)
                both4(lambda s: dve.tensor_tensor(g4[:, s, 2, :, :], g4[:, s, 4, :, :],
                                                  s4[:, s, 2, :].unsqueeze(2).broadcast_to([P, SUB, E2]), op=ALU.mult), q, own)
                both4(lambda s: dve.tensor_scalar(cwh[:, s, :, :], g4[:, s, 2, :, :], 0.0, None, ALU.add), q, own)
                for s in range(2):
                    own.need(q[s])
                    apart(dve, dve_passed)
                    dve.tensor_copy(cs[:, s, :, 0:E2], cwh[:, s, :, :].bitcast(F32))
                    dve.tensor_tensor(cs[:, s, :, E2:2 * E2], g4[:, s, 2, :, :], cwh[:, s, :, :].bitcast(F32),
                                      op=ALU.subtract).then_inc(d_cs, 1)
                assert own.n == DVE_D, own.n

            def e_h(t, u):
                dve.wait_ge(u_sg, t * NP2 + u)
                dve.wait_ge(u_cw, t * NP2 + u)
                if u >= 3 or not (isinstance(t, int) and t == 0):
                    dve.wait_ge(u_hl, t * NU + u - 2)
                dve.tensor_tensor(h4[:, u % 3, :], sg4[:, u % 3, :], bank[3 + u % 2][:, :], op=ALU.mult).then_inc(u_h, 1)

            def e_lo(t, u):
                r = slice(0, F2 if u == 0 else P)
                dve.wait_ge(u_hh, t * NU + u + 1)
                dve.tensor_tensor(hl4[r, u % 3, :], h4[r, u % 3, :], hh4[r, u % 3, :].bitcast(F32),
                                  op=ALU.subtract).then_inc(u_hl, 1)

            def result(t, p, stored=0):
                dve.wait_ge(u_T, t + 1)
                if not isinstance(t, int) or t >= 2:
                    dve.wait_ge(o_out[p], stored * 16 + 16)
                dve.tensor_tensor(y4[:, p, :, :], bank[6][:, :].rearrange("p (k d) -> p k d", k=SUB),
                                  x_res[:, ds(t * SUB, SUB), :], op=ALU.add).then_inc(u_y, 1)

            def dve_tile(t, p, before):
                if before is not None:
                    e_lo(before[0], NU - 1)
                for u in range(1, NU):
                    e_h(t, u)
                    e_lo(t, u - 1)
                    if u == 9 and before is not None:
                        result(*before)

            tiles_of(dve, dve_tile)
            e_lo(T // TT - 1, NU - 1)
            result(T // TT - 1, 1, T // TT // 2 - 1)

        @block.tensor
        def _(pe):
            pe.wait_ge(consts, 1)
            pe.wait_ge(small_in, 16 * 10)

            def transposed(src, s, made, i, done):
                pe.wait_ge(made, i)
                for k in range(SUB):
                    ins = pe.transpose(bank[s][:, k * P:(k + 1) * P], src[:, s, k, :], ident[:, :])
                ins.then_inc(done, 1)

            with pe.Fori(0, NPIECE // 2) as it:
                for s in range(2):
                    transposed(xn, s, xn1, it * 2 + s + 1, tr1)
                for s in range(2):
                    pe.wait_ge(tc1, it * 2 + s + 1)
                    for k in range(SUB):
                        ins = pe.matmul(bank[2 + 2 * s + k // 2][:, (k % 2) * M1:(k % 2 + 1) * M1], xnT[:, s, k, :],
                                        w123[:, :], start=True, stop=True)
                    ins.then_inc(zz1, 1)
                for s in range(2):
                    transposed(xm, s, xn2, it * 2 + s + 1, tr2)
                for s in range(2):
                    pe.wait_ge(tc2, it * 2 + s + 1)
                    for k in range(SUB):
                        ins = pe.matmul(bank[2 + 2 * s][:, k * 16:k * 16 + E1], xnT[:, s, k, :], wr_s[:, :],
                                        start=True, stop=True)
                    ins.then_inc(lg2, 1)
                for s in range(2):
                    pe.wait_ge(sl2, it * 2 + s + 1)
                    for k in range(SUB + 1):
                        o = bank[3 + 2 * s][:, k * E1:(k + 1) * E1]
                        for j in range(k):
                            ins = pe.matmul(o, ones[:, :], sel[:, s, j, :], start=j == 0, stop=(k == SUB and j == k - 1))
                        if k < SUB:
                            ins = pe.matmul(o, tri[:, :], sel[:, s, k, :], start=k == 0, stop=True)
                    ins.then_inc(rk2, 1)

            def x_T(b, u, loads):
                pe.wait_ge(xb_in[u], 16 * loads)
                pe.transpose(bank[0][:, 0:P], xb[:, u, :], ident[:, :]).then_inc(xT_r, 1)

            def expert_of(b):
                return pe.value_load(blk_e[0:1, ds(b, 1)], min_val=0, max_val=E1 - 1)

            def up(b, v):
                e = expert_of(b)
                pe.wait_ge(xh_r, b + 1)
                pe.wait_ge(xl_r, b + 1)
                for o, hi, lo in ((bank[4 + v], wgh, wgl), (bank[6 + v], wuh, wul)):
                    w = ds(e * I1, I1)
                    pe.matmul(o[:, 0:I1], xbh[:, v, :], hi[:, w], start=True, stop=False)
                    pe.matmul(o[:, 0:I1], xbh[:, v, :], lo[:, w], start=False, stop=False)
                    ins = pe.matmul(o[:, 0:I1], xbl[:, v, :], hi[:, w], start=False, stop=True)
                ins.then_inc(gu_r, 1)

            def h_T(b, v):
                pe.wait_ge(h_r, b + 1)
                for j in range(JC):
                    ins = pe.transpose(bank[2 + v][:, j * P:(j + 1) * P], hb[:, v, j * P:(j + 1) * P], ident[:, :])
                ins.then_inc(hT_r, 1)

            def down(b, v, first):
                e = expert_of(b)
                pe.wait_ge(hh_r, b + 1)
                pe.wait_ge(hl_r, b + 1)
                if not first:
                    pe.wait_ge(yb_r, b)
                o = bank[1][:, 0:D]
                for j in range(JC):
                    r = min(P, I1 - j * P)
                    w = ds(e * (JC * D) + j * D, D)
                    hhj, hlj = hh[0:r, v, j * P:(j + 1) * P], hl[0:r, v, j * P:(j + 1) * P]
                    pe.matmul(o, hhj, wdh[0:r, w], start=j == 0, stop=False)
                    pe.matmul(o, hhj, wdl[0:r, w], start=False, stop=False)
                    ins = pe.matmul(o, hlj, wdh[0:r, w], start=False, stop=j == JC - 1)
                ins.then_inc(y_r, 1)

            pe.wait_ge(w_hi, 4)
            pe.wait_ge(w_lo, 4)
            pe.wait_ge(list_ready, 1)
            x_T(0, 0, 1)
            for b in range(4):
                up(b, b % 2)
                x_T(b + 1, (b + 1) % 4, (b + 1) // 4 + 1)
                if b >= 1:
                    h_T(b - 1, (b - 1) % 2)
                if b >= 2:
                    down(b - 2, b % 2, b == 2)
            with pe.Fori(1, NBLK // 4 - 1) as it:
                for u in range(4):
                    b = it * 4 + u
                    up(b, u % 2)
                    x_T(b + 1, (u + 1) % 4, it + 1 if u < 3 else it + 2)
                    h_T(b - 1, (u - 1) % 2)
                    down(b - 2, u % 2, False)
            for b in range(NBLK - 4, NBLK + 2):
                if b < NBLK:
                    up(b, b % 2)
                if b + 1 < NBLK:
                    x_T(b + 1, (b + 1) % 4, (b + 1) // 4 + 1)
                if b - 1 < NBLK:
                    h_T(b - 1, (b - 1) % 2)
                down(b - 2, b % 2, False)

            pe.wait_ge(c_in, 16 * 8)
            pe.wait_ge(c_const, 1)
            pe.wait_ge(c_w, 6)

            def pe_turn(i, half, p, E, F, M, P1, G):
                b1, b2 = i + 1, i + 2

                def turned(src, q, first_bank, groups):
                    for g in groups:
                        o = bank[first_bank + (g - groups[0]) // 2][:, (g % 2) * 2 * P:(g % 2 + 1) * 2 * P]
                        for u in range(2):
                            ins = pe.matmul(o, src[:, q, u, 4 * g:4 * g + 4, :].rearrange("p h w -> p (h w)"),
                                            idr[:, 1 - u:3 - u, :].rearrange("p a k -> p (a k)"),
                                            start=u == 0, stop=u == 1)
                    return ins

                def scores_k(g):
                    if E:
                        if g > 0 or not isinstance(i, int) or i > 0:
                            pe.wait_ge(c_P, i * 4 + g)
                        if g % 2 == 0:
                            pe.wait_ge(c_q2, 2 * i + g // 2 + 1)
                            pe.wait_ge(c_q2d, 2 * i + g // 2 + 1)
                        for o, kb, qb in ((bank[0], 0, 0), (bank[1], 0, 1), (bank[2], 1, 1)):
                            if kb == qb:
                                pe.matmul(o, identb[:, :], msk[:, 1, :, :], start=True, stop=False,
                                          skip_group_check=True)
                            ins = pe.matmul(o.rearrange("p (j k) -> p j k", j=4), kT[:, p, g, kb * P:(kb + 1) * P],
                                            qz[:, g, :, qb * P:(qb + 1) * P], start=kb != qb, stop=True,
                                            skip_group_check=True)
                        ins.then_inc(c_S2, 1)

                def scores_q(g):
                    if M:
                        if g > 0:
                            pe.wait_ge(c_mx, b1 * 4 + g)
                        else:
                            pe.wait_ge(c_qT, b1 + 1)
                            pe.wait_ge(c_kz, b1 + 1)
                            pe.wait_ge(c_kT, b1 + 1)
                        pe.matmul(bank[3], identb[:, :], msk[:, 0, :, :], start=True, stop=False, skip_group_check=True)
                        pe.matmul(bank[3].rearrange("p (j k) -> p j k", j=4), qT[:, g, 0:P], kz[:, g, :, 0:P],
                                  start=False, stop=True, skip_group_check=True)
                        for c in range(2):
                            o = bank[4 + c].rearrange("p (j k) -> p j k", j=4)
                            pe.matmul(o[:, 1:4:2, :], identb[:, :], msk[:, 0, 0:2, :], start=True, stop=False,
                                      skip_group_check=True)
                            ins = pe.matmul(bank[4 + c].rearrange("p (j k) -> p j k", j=2), qT[:, g, P:2 * P],
                                            kz[:, g, 2 * c:2 * c + 2, :], start=False, stop=True, skip_group_check=True)
                        ins.then_inc(c_S1, 1)

                def values(g):
                    if E:
                        pe.wait_ge(c_P, i * 4 + g + 1)
                        if g == 0:
                            pe.wait_ge(c_vp, i + 1)
                            if M:
                                pe.wait_ge(c_qT, b1 + 1)
                            else:
                                pe.wait_ge(c_OT, i * 4)
                        else:
                            pe.wait_ge(c_OT, i * 4 + g)
                        for j in range(4):
                            o = bank[6][j * HW:j * HW + S + 1, 0:2 * P]
                            pe.matmul(o.rearrange("p (b k) -> p b k", b=2), vp[:, p, 0, 4 * g + j, :],
                                      pt[:, g % 2, 0:2, j, :], start=True, stop=False, skip_group_check=True)
                            ins = pe.matmul(o[:, P:2 * P], vp[:, p, 1, 4 * g + j, :], pt[:, g % 2, 2, j, :],
                                            start=False, stop=True, skip_group_check=True)
                        ins.then_inc(c_PV, 1)

                def att_T(u):
                    if F:
                        if u == 1:
                            pe.wait_ge(c_F2, 2 * i - 1)
                        elif E:
                            pe.wait_ge(c_q2, 2 * i + 2)
                            pe.wait_ge(c_q2d, 2 * i + 2)
                        else:
                            pe.wait_ge(c_F6, i)
                        if u == 0:
                            pe.wait_ge(c_OT, i * 4)
                        for g in range(4):
                            ins = pe.transpose(bank[7][:, g * P:(g + 1) * P], ot[:, 1 - p, g, u * P:(u + 1) * P], ident[:, :])
                        ins.then_inc(c_F1, 1)

                def qkv(u):
                    if P1:
                        if u:
                            pe.wait_ge(c_zs, 2 * b2 + 1)
                        else:
                            pe.wait_ge(c_xl, b2 + 1)
                        o = bank[7][:, 0:3 * D]
                        pe.matmul(o, xch[:, u, :], wqh[:, :], start=True, stop=False)
                        pe.matmul(o, xch[:, u, :], wql[:, :], start=False, stop=False)
                        pe.matmul(o, xcl[:, u, :], wqh[:, :], start=False, stop=True).then_inc(c_z, 1)

                def with_maxima(q, b, c):
                    pe.wait_ge(c_nm, 2 * b + c + 1)
                    turned(qs, q, 7, (2 * c, 2 * c + 1)).then_inc(c_T2, 1)

                if M:
                    pe.wait_ge(c_dup, b1 + 1)
                    pe.wait_ge(c_lo, b1 + 1)
                    if not isinstance(i, int) or i > -1:
                        pe.wait_ge(c_mx, b1 * 4)
                    turned(ks, 1 - p, 3, range(4)).then_inc(c_T3, 1)
                if P1:
                    pe.wait_ge(c_xn, b2 + 1)
                    if not isinstance(i, int) or i > 0:
                        pe.wait_ge(c_F6, i)
                    elif i > -2:
                        pe.wait_ge(c_zs, 2 * b2)
                    if E:
                        pe.wait_ge(c_q2, 2 * i + 1)
                        pe.wait_ge(c_q2d, 2 * i + 1)
                    for u in range(2):
                        ins = pe.transpose(bank[7][:, u * P:(u + 1) * P], xc[:, u, :], ident[:, :])
                    ins.then_inc(c_xT, 1)
                if M:
                    if not isinstance(i, int) or i > 0:
                        pe.wait_ge(c_OT, i * 4)
                    turned(qs, 1 - p, 5, range(4)).then_inc(c_T, 1)
                scores_k(0)
                qkv(0)
                scores_q(0)
                scores_k(1)
                qkv(1)
                values(0)
                if E:
                    if P1:
                        pe.wait_ge(c_zs, 2 * i + 6)
                    else:
                        pe.wait_ge(c_F6, i)
                    with_maxima(p, i, 1)
                scores_q(1)
                values(1)
                scores_k(2)
                att_T(0)
                values(2)
                att_T(1)
                scores_q(2)
                if F:
                    pe.wait_ge(c_F2, 2 * i)
                    for u in range(2):
                        ins = pe.transpose(bank[7][:, u * P:(u + 1) * P], oo[:, u, :], ident[:, :])
                    ins.then_inc(c_F3, 1)
                scores_k(3)
                if M:
                    if F:
                        pe.wait_ge(c_F4, i)
                    elif E:
                        pe.wait_ge(c_q2, 2 * i + 2)
                        pe.wait_ge(c_q2d, 2 * i + 2)
                    else:
                        pe.wait_ge(c_zs, 2 * i + 6)
                    with_maxima(1 - p, b1, 0)
                scores_q(3)
                values(3)
                if F:
                    if M:
                        pe.wait_ge(c_q2, 2 * b1 + 1)
                        pe.wait_ge(c_q2d, 2 * b1 + 1)
                    pe.wait_ge(c_F4, i)
                    for u in range(2):
                        ins = pe.matmul(bank[7][:, u * D:(u + 1) * D], ooT[:, u, :], wuT[:, :], start=True, stop=True)
                    ins.then_inc(c_F5, 1)

            turns(pe_turn, pe)

            pe.wait_ge(sh_in, 16 * 4)
            with pe.Fori(0, NPIECE // 2) as it:
                for s in range(2):
                    transposed(xm4, s, d_xn, it * 2 + s + 1, d_T)
                for s in range(2):
                    pe.wait_ge(d_Tc, it * 2 + s + 1)
                    for k in range(SUB):
                        ins = pe.matmul(bank[2 + s][:, k * E2:(k + 1) * E2], xnT4[:, s, k, :], cen_s[:, :],
                                        start=True, stop=True)
                    ins.then_inc(d_af, 1)
                for s in range(2):
                    pe.wait_ge(d_cs, it * 2 + s + 1)
                    for k in range(SUB):
                        ins = pe.transpose(bank[4 + s][:, k * P:(k + 1) * P], cs[:, s, k, :], ident[:, :])
                    ins.then_inc(d_cT, 1)

            pe.wait_ge(d_cw, NPIECE)
            pe.wait_ge(d_sel, 1)
            pe.wait_ge(sh_done, 4)
            pe.wait_ge(wd_done, NC)

            def e_up(t, u):
                first = isinstance(t, int) and t == 0
                if u >= 3:
                    pe.wait_ge(u_sg, t * NP2 + u - 3)
                    if u == 3:
                        pe.wait_ge(u_sg0, t + 1)
                elif not first:
                    pe.wait_ge(u_sg, (t - 1) * NP2 + NU + u - 3)
                tok = ds(t * TT, TT)
                if u == 0:
                    o, hi, lo = bank[0][0:F2, :], shh[:, 0:F2], shl[:, 0:F2]
                else:
                    c = slice((u - 1) * P, u * P)
                    o, hi, lo = bank[u % 3][:, :], wh[:, c], wl[:, c]
                pe.matmul(o, hi, xh4[:, tok], start=True, stop=False)
                pe.matmul(o, hi, xl4[:, tok], start=False, stop=False)
                pe.matmul(o, lo, xh4[:, tok], start=False, stop=True).then_inc(u_up, 1)
                if u > 0:
                    if u > 2:
                        pe.wait_ge(u_h, t * NP2 + u - 2)
                    elif not first:
                        pe.wait_ge(u_h, (t - 1) * NP2 + NP2 + u - 2)
                    pe.matmul(bank[3 + u % 2][:, :], selr[:, c], cwT[:, tok], start=True, stop=True).then_inc(u_cw, 1)

            def e_down(t, p, u):
                if u == 0 and not (isinstance(t, int) and t < 2):
                    pe.wait_ge(u_oT, t - 1)
                pe.wait_ge(u_hl, t * NU + u + 1)
                if u == 0:
                    r, hi, lo = slice(0, F2), shh[0:F2, F2:F2 + D], shl[0:F2, F2:F2 + D]
                else:
                    c = slice(E2 * F2 + (u - 1) * D, E2 * F2 + u * D)
                    r, hi, lo = slice(0, P), wh[:, c], wl[:, c]
                o = bank[5 + 2 * p][:, :]
                pe.matmul(o, hi, hh4[r, u % 3, :], start=u == 0, stop=False)
                pe.matmul(o, hi, hl4[r, u % 3, :], start=False, stop=False)
                ins = pe.matmul(o, lo, hh4[r, u % 3, :], start=False, stop=u == NU - 1)
                ins.then_inc(u_dn, 1)

            def out_T(t):
                pe.wait_ge(u_oT, t + 1)
                if not isinstance(t, int) or t >= 1:
                    pe.wait_ge(u_y, t)
                for k in range(SUB):
                    ins = pe.transpose(bank[6][:, k * P:(k + 1) * P], oT4[:, k * P:(k + 1) * P], ident[:, :])
                ins.then_inc(u_T, 1)

            LAG = 3

            def pe_tile(t, p, before):
                for u in range(NU):
                    e_up(t, u)
                    if u >= LAG:
                        e_down(t, p, u - LAG)
                    elif before is not None:
                        e_down(before[0], 1 - p, NU + u - LAG)
                    if u == 7 and before is not None:
                        out_T(before[0])

            tiles_of(pe, pe_tile)
            for u in range(NU - LAG, NU):
                e_down(T // TT - 1, 1, u)
            out_T(T // TT - 1)


_INS = ['L0_attn_x', 'L0_attn_W1', 'L0_attn_b1', 'L0_attn_W2', 'L0_attn_b2', 'L0_attn_W3', 'L0_attn_b3',
        'L0_ffn_Wr', 'L0_ffn_Wg', 'L0_ffn_Wu', 'L0_ffn_Wd', 'L1_attn_Wk', 'L1_attn_Wq', 'L1_attn_Wv', 'L1_attn_Wu',
        'L1_attn_kln_w', 'L1_attn_kln_b', 'L1_attn_qln_w', 'L1_attn_qln_b', 'L1_ffn_centroids', 'L1_ffn_expert_biases',
        'L1_ffn_Ws_up', 'L1_ffn_Ws_down', 'L1_ffn_W_up', 'L1_ffn_W_down']
_TURNED = ('L1_attn_Wk', 'L1_attn_Wq', 'L1_attn_Wv', 'L1_attn_Wu', 'L1_ffn_centroids')
_OUTS = [((16, 256, 128), 'float32')]


def kernel(**inputs):
    import numpy as _np
    import concourse.bacc as _bacc
    from concourse import mybir as _mybir
    from concourse.bass_utils import run_bass_kernel_spmd as _run

    nc = _bacc.Bacc("TRN2", target_bir_lowering=False, num_devices=1)
    arrays, args = {}, []
    for name in _INS:
        a = _np.asarray(inputs[name])
        a = _np.ascontiguousarray(a.T if name in _TURNED else a)
        arrays[f"in_{name}_dram"] = a
        args.append(nc.dram_tensor(f"in_{name}_dram", a.shape, _mybir.dt.from_np(a.dtype), kind="ExternalInput").ap())
    for i, (shape, dtype) in enumerate(_OUTS):
        dt = _mybir.dt.from_np(_np.dtype(dtype))
        args.append(nc.dram_tensor(f"out_{i}_dram", shape, dt, kind="ExternalOutput").ap())
    bass_two_layers(nc, *args)
    r = _run(nc, [arrays], core_ids=[0])
    got = tuple(r.results[0][f"out_{i}_dram"] for i in range(len(_OUTS)))
    return got[0]
```

```python
from contextlib import ExitStack

import concourse.bass as bass
from concourse import mybir

F32 = mybir.dt.float32
F32R = mybir.dt.float32r
BF16 = mybir.dt.bfloat16
I32 = mybir.dt.int32
ALU = mybir.AluOpType
ACT = mybir.ActivationFunctionType
AX = mybir.AxisListType
ds = bass.ds

P = 128
LN_EPS = 1e-5
BIG = 1.0e30


def apart(eng, passed):
    eng.sem_inc(passed, 1)


class Tickets:

    def __init__(self, eng, sem, base=0):
        self.eng, self.sem, self.base, self.n = eng, sem, base, 0

    def done(self, ins):
        ins.then_inc(self.sem, 1)
        self.n += 1
        return self.n

    def need(self, ticket):
        self.eng.wait_ge(self.sem, self.base + ticket)

    def link(self, ins):
        self.need(self.done(ins))


def bass_two_layers(nc, x, W1, b1, W2, b2, W3, b3, Wr, Wg, Wu, Wd, WkT, WqT, WvT, WuT, kln_w, kln_b, qln_w, qln_b,
                    cent, ebias, Ws_up, Ws_down, W_up, W_down, out):
    B, L, D = x.shape
    T = B * L
    NT = T // P
    N = W2.shape[1]
    M1 = D + 2 * N
    E1, _, I1 = Wg.shape
    JC = -(-I1 // P)
    IP = JC * P
    K1 = 2
    SUB = 4
    NPIECE = NT // SUB
    REG = T + P
    NBLK = T * K1 // P + E1 - 1
    NBLK = -(-NBLK // 4) * 4
    assert D == P and NPIECE % 2 == 0

    x_tok = x.rearrange("b (u p) d -> p (b u) d", p=P)
    out_tok = out.rearrange("b (u p) d -> p (b u) d", p=P)

    xs = nc.dram_tensor("xs", [E1 * REG, D], F32).ap()
    ys = nc.dram_tensor("ys", [NBLK * P, D], F32).ap()

    with ExitStack() as ctx:
        def sb(name, shape, dt):
            return ctx.enter_context(nc.sbuf_tensor(name, shape, dt))

        def sem(name):
            return ctx.enter_context(nc.semaphore(name))

        ps = ctx.enter_context(nc.psum_tensor("ps", [P, 8, 512], F32))
        bank = [ps[:, i, :] for i in range(8)]

        x_res = sb("x_res", [P, NT, D], F32)
        ident = sb("ident", [P, P], F32)
        eps_c = sb("eps_c", [P, 1], F32)
        st = sb("st", [P, 2, SUB, 6], F32)
        mv = sb("mv", [P, 2, SUB, 2], F32)
        lnv = sb("lnv", [P, 2, SUB], F32)
        rstd = sb("rstd", [P, 2, SUB], F32)
        wgt = sb("wgt", [P, NT, K1], F32)
        gpi = sb("gpi", [P, NT * K1], I32)
        gps = sb("gps", [P, 2, 2 * K1], I32)
        yg = sb("yg", [P, 4, K1, D], F32)
        first = ExitStack()

        def sb1(name, shape, dt):
            return first.enter_context(nc.sbuf_tensor(name, shape, dt))

        xnT = sb1("xnT", [P, 2, SUB, P], F32)
        xmT = sb1("xmT", [P, 2, SUB, P], F32)
        stb = sb1("stb", [P, 2, SUB, 6], F32)
        mvb = sb1("mvb", [P, 2, SUB, 2], F32)
        lnvb = sb1("lnvb", [P, 2, SUB], F32)
        rstdb = sb1("rstdb", [P, 2, SUB], F32)
        w123 = sb1("w123", [P, M1], F32)
        bias = sb1("bias", [P, 2, M1], F32)
        tri = sb1("tri", [P, P], BF16)
        ones = sb1("ones", [P, P], BF16)
        trif = sb1("trif", [P, P], F32)
        zrow = sb1("zrow", [P, P], F32)
        wr_s = sb1("wr_s", [P, E1], F32)
        rev9 = sb1("rev9", [P, SUB, E1], F32)
        off9 = sb1("off9", [P, E1], F32)
        prow = sb1("prow", [P, E1], F32)
        iblk = sb1("iblk", [P, NBLK], F32)
        xn = sb1("xn", [P, 2, SUB, D], F32)
        xm = sb1("xm", [P, 2, SUB, D], F32)
        xo = sb1("xo", [P, 2, SUB, D], F32)
        bc = sb1("bc", [P, 2, SUB, N], F32)
        bcs = sb1("bcs", [P, 2, SUB], F32)
        lg = sb1("lg", [P, 2, SUB, E1], F32)
        r9 = sb1("r9", [P, 2, 5, SUB, E1], F32)
        r1 = sb1("r1", [P, 2, 8, SUB], F32)
        sel = sb1("sel", [P, 2, SUB, E1], BF16)
        pick = sb1("pick", [P, NT, K1, E1], F32)
        posf = sb1("posf", [P, NT, K1], F32)
        posi = sb1("posi", [P, 2, SUB, K1], I32)
        base = sb1("base", [P, E1], F32)
        stg = sb1("stg", [P, E1 * I1], F32)
        stu = sb1("stu", [P, E1 * I1], F32)
        std = sb1("std", [P, E1 * JC * D], F32)
        wgh = sb1("wgh", [P, E1 * I1], F32R)
        wgl = sb1("wgl", [P, E1 * I1], F32R)
        wuh = sb1("wuh", [P, E1 * I1], F32R)
        wul = sb1("wul", [P, E1 * I1], F32R)
        wd2 = sb1("wd2", [P, E1 * JC, 2, D], F32R)
        cnti = sb1("cnti", [P, E1], I32)
        nblk = sb1("nblk", [P, E1], F32)
        bend = sb1("bend", [P, E1], F32)
        bstart = sb1("bstart", [P, E1], F32)
        q9 = sb1("q9", [P, 3, E1], F32)
        tail = sb1("tail", [P, E1], I32)
        b9 = sb1("b9", [P, 3, NBLK, E1], F32)
        bf = sb1("bf", [P, 3, NBLK], F32)
        blk_src = sb1("blk_src", [P, NBLK], I32)
        blk_e = sb1("blk_e", [P, NBLK], I32)
        gp9 = b9[:, 0, 0:NT * K1, :]
        gpf = sb1("gpf", [P, NT * K1], F32)
        mix = ExitStack()
        z = mix.enter_context(nc.sbuf_tensor("z", [P, 2, SUB, M1], F32))
        sp = mix.enter_context(nc.sbuf_tensor("sp", [P, 2, 3, SUB, D], F32))
        mix.close()
        xb = sb1("xb", [P, 4, D], F32)
        xbh = sb1("xbh", [P, 2, D], F32R)
        xbl = sb1("xbl", [P, 2, D], F32R)
        sg = sb1("sg", [P, 2, I1], F32)
        hb = sb1("hb", [P, 2, IP], F32)
        hh = sb1("hh", [P, 2, IP], F32R)
        hl = sb1("hl", [P, 2, IP], F32R)
        yb = sb1("yb", [P, 4, D], F32)

        first.close()

        E2, F2 = cent.shape[1], W_up.shape[2]
        K2 = 8
        NP2 = E2 * F2 // P
        WC = 512
        TT = 4 * P
        NC = (E2 * F2 + NP2 * D) // WC
        assert NC == B and 2 * F2 == P
        wh = sb("wh", [P, E2 * F2 + NP2 * D], F32R)
        wl = sb("wl", [P, E2 * F2 + NP2 * D], F32R)
        wst = sb("wst", [P, 2, WC], F32)
        shf = sb("shf", [P, F2 + D], F32)
        shh = sb("shh", [P, F2 + D], F32R)
        shl = sb("shl", [P, F2 + D], F32R)
        cen_s = sb("cen_s", [P, E2], F32)
        ebi = sb("ebi", [P, E2], F32)
        attn = ExitStack()

        def sb2(name, shape, dt):
            return attn.enter_context(nc.sbuf_tensor(name, shape, dt))

        H = 16
        S = D // H
        HW = 32
        KA, QA = 2, 2
        KS = 3 * S
        wqkv = sb2("wqkv", [P, 3 * D], F32)
        wqh = sb2("wqh", [P, 3 * D], F32R)
        wql = sb2("wql", [P, 3 * D], F32R)
        wuT = sb2("wuT", [P, D], F32)
        ln8 = sb2("ln8", [P, 4, S], F32)
        lnw = sb2("lnw", [P, 2, H, S], F32)
        lnb = sb2("lnb", [P, 2, H, S], F32)
        identb = sb2("identb", [P, P], BF16)
        idr = sb2("idr", [P, 3, P], F32R)
        mskf = sb2("mskf", [P, 2, P], F32)
        msk = sb2("msk", [P, 2, 4, P], BF16)
        cst = sb2("cst", [P, 2, 6], F32)
        cmv = sb2("cmv", [P, 2, 2], F32)
        cln = sb2("cln", [P, 2], F32)
        crs = sb2("crs", [P, 2], F32)
        xc = sb2("xc", [P, 2, D], F32)
        xch = sb2("xch", [P, 2, P], F32R)
        xcl = sb2("xcl", [P, 2, P], F32R)
        zs = sb2("zs", [P, 2, 2, 3 * D], F32)
        ms = sb2("ms", [P, 2, 2 * H], F32)
        cen = sb2("cen", [P, 2, 2 * D], F32)
        csq = sb2("csq", [P, 2, 2 * D], F32)
        vsm = sb2("vsm", [P, 2, 2 * H], F32)
        rql = sb2("rql", [P, 2, 2 * H], F32)
        rq = sb2("rq", [P, 2, 2 * H], F32)
        nq = sb2("nq", [P, 2, 2, 2 * D], F32)
        qs = sb2("qs", [P, 2, 2, H, HW], F32R)
        ks = sb2("ks", [P, 2, 2, H, HW], F32R)
        vp = sb2("vp", [P, 2, 2, H, S + 1], F32)
        qT = sb2("qT", [P, 4, 2 * P], F32R)
        kT = sb2("kT", [P, 2, 4, 2 * P], F32R)
        kz = sb2("kz", [P, 4, 4, 2 * P], F32R)
        qz = sb2("qz", [P, 4, 4, 2 * P], F32R)
        nm = sb2("nm", [P, 2, H], F32)
        nmh = sb2("nmh", [P, 2, H], F32R)
        pt = sb2("pt", [P, 2, 3, 4, P], F32)
        ot = sb2("ot", [P, 2, 4, 2 * P], F32)
        rc = sb2("rc", [P, 2, H], F32)
        oo = sb2("oo", [P, 2, D], F32)
        ooT = sb2("ooT", [P, 2, P], F32)

        attn.close()

        xh4 = sb("xh4", [P, 2, TT], F32R)
        xl4 = sb("xl4", [P, 2, TT], F32R)
        cwT = sb("cwT", [P, 2, TT], F32R)
        selr = sb("selr", [P, E2, F2], F32R)
        xnT4 = sb("xnT4", [P, SUB, P], F32)
        xm4 = sb("xm4", [P, SUB, D], F32)
        af = sb("af", [P, SUB, E2], F32)
        bi = sb("bi", [P, SUB, E2], F32)
        m8 = sb("m8", [P, SUB, 8], F32)
        mr = sb("mr", [P, SUB, E2], F32)
        g4 = sb("g4", [P, 6, SUB, E2], F32)
        s4 = sb("s4", [P, 3, SUB], F32)
        cwh = sb("cwh", [P, SUB, E2], F32R)
        cs = sb("cs", [P, SUB, 2 * E2], F32)
        sg4 = sb("sg4", [P, 3, TT], F32)
        h4 = sb("h4", [P, 3, TT], F32)
        hh4 = sb("hh4", [P, 3, TT], F32R)
        hl4 = sb("hl4", [P, 3, TT], F32R)
        oT4 = sb("oT4", [P, TT], F32)
        y4 = sb("y4", [P, 2, SUB, D], F32)
        NU = NP2 + 1

        x_in = [sem(f"x_in{i}") for i in range(4)]
        small_in = sem("small_in")
        wg_in, wu_in, wd_in = sem("wg_in"), sem("wu_in"), sem("wd_in")
        w_hi, w_lo = sem("w_hi"), sem("w_lo")
        consts = sem("consts")
        pool_own, dve_own, act_own = sem("pool_own"), sem("dve_own"), sem("act_own")
        dve_passed, pool_passed = sem("dve_passed"), sem("pool_passed")
        mv1, rs1, xn1, tr1, tc1, zz1, zc1, sp1 = (sem(n) for n in (
            "ln1_stats", "ln1_rstd", "ln1_out", "ln1_T", "ln1_T_copied", "mix_z", "mix_z_copied", "mix_softplus"))
        mv2, rs2, xn2, tr2, tc2, lg2, df2, ex2, sl2, rk2, ps2 = (sem(n) for n in (
            "ln2_stats", "ln2_rstd", "ln2_out", "ln2_T", "ln2_T_copied", "r1_logits", "r1_diff", "r1_exp",
            "r1_sel", "r1_rank", "r1_pos"))
        scat = [sem("scat0"), sem("scat1")]
        scat_ok = [sem("scat_ok0"), sem("scat_ok1")]
        tails = sem("tails")
        tails_in = sem("tails_in")
        list_ready = sem("list_ready")
        xb_in = [sem(f"xb_in{u}") for u in range(4)]
        ys_out = [sem(f"ys_out{u}") for u in range(4)]
        xT_r, xh_r, xl_r, gu_r, sg_r, h_r, hT_r, hh_r, hl_r, y_r, yb_r = (sem(n) for n in (
            "blk_xT", "blk_xh", "blk_xl", "blk_gu", "blk_silu", "blk_h", "blk_hT", "blk_hh", "blk_hl", "blk_y", "blk_yb"))
        yg_in = [sem(f"yg_in{u}") for u in range(4)]
        x2_half, x2_r = sem("x2_first_row"), sem("x2_ready")
        gps_r = sem("batch_rows")
        gp_r = sem("gather_rows")
        o_out = [sem("o_out0"), sem("o_out1")]
        w_in = [sem("w_in0"), sem("w_in1")]
        wd_done, sh_in, sh_done, d_const = (sem(n) for n in (
            "w2_parts", "shared_in", "shared_parts", "d_const"))
        act_d, dve_d = sem("act_d"), sem("dve_d")
        dve_s = sem("dve_s")
        d_mv, d_rs, d_xn, d_T, d_Tc, d_hl, d_af, d_afc, d_ex, d_cs, d_cT, d_cw = (sem(n) for n in (
            "ln4_stats", "ln4_rstd", "ln4_out", "ln4_T", "ln4_T_copied", "x4_parts", "r2_logits", "r2_copied", "r2_exp",
            "r2_weights", "r2_T", "r2_done"))
        u_up, u_cw, u_sg, u_h, u_hh, u_hl, u_dn, u_oT, u_y, u_T = (sem(n) for n in (
            "e_up", "e_weight", "e_silu", "e_h", "e_hh", "e_hl", "e_down", "e_outT", "e_y", "e_out_T"))
        c_in, c_const, c_w = sem("c_in"), sem("c_const"), sem("c_w")
        act_c, dve_c1, dve_cf = sem("act_c"), sem("dve_c1"), sem("dve_cf")
        xo_r = sem("rows_copied")
        c_mv, c_rs, c_xn, c_xT, c_xh, c_xl, c_z, c_zs, c_cen, c_sq, c_vs, c_rq, c_n, c_wb, c_nh, c_lo, c_dup, c_vp = (
            sem(n) for n in ("ln3_stats", "ln3_rstd", "ln3_out", "ln3_T", "ln3_T_hi", "ln3_T_lo", "qkv", "qkv_copied",
                             "qk_centred", "qk_squares", "qk_vars", "qk_rstd", "qk_scaled", "qk_affine", "qk_hi", "qk_lo",
                             "qk_spread", "v_spread"))
        c_T, c_qT, c_kT, c_S1, c_mx, c_nm, c_T2, c_q2, c_S2, c_P, c_PV, c_OT, c_F1, c_F2, c_F3, c_F4, c_F5, c_F6 = (
            sem(n) for n in ("qk_T", "q_T_copied", "k_T_copied", "scores_q", "row_max", "max_spread", "q2_T", "q2_T_copied",
                             "scores_k", "probs", "pv", "pv_copied", "att_T", "att_norm", "att_T2", "att_T2_copied",
                             "att_proj", "x3"))

        R1 = I1 - (JC - 1) * P
        QU = E1 * I1 // (NPIECE // 2 - 1)
        QC = E1 * JC // (NPIECE // 2 - 1)
        stv = std[:, :].rearrange("p (e j d) -> p e j d", e=E1, j=JC)
        stc = std[:, :].rearrange("p (c d) -> p c d", d=D)
        wdf = wd2[:, :, :, :].rearrange("p c h d -> p (c h d)")
        ACT_1, ACT_2, DVE_1, DVE_2 = 6, 2, 24, 54
        DVE_S, DVE_D = 4, 19

        c_q2d, c_kz, c_T3 = sem("q2_T_copied_dve"), sem("k_T_spread"), sem("k_T")
        act_own2, dve_own2 = sem("act_own2"), sem("dve_own2")
        dve_ln = sem("dve_ln")
        pool_w, act_c2, dve_nm = sem("pool_w"), sem("act_c2"), sem("dve_nm")
        u_hlp = sem("e_hl_pool")
        pool_h, u_sg0 = sem("pool_h"), sem("e_silu_shared")

        def pieces(eng, turn):
            turn(0, True, False)
            with eng.Fori(1, NPIECE // 2) as k:
                turn(k, True, True)
            turn(NPIECE // 2, False, True)

        def tiles_of(eng, tile):
            last = T // TT - 1
            tile(0, 0, None, True, True)
            tile(1, 1, (0, 0, 0), True, True)
            with eng.Fori(1, (last - 1) // 2) as it:
                tile(it * 2, 0, (it * 2 - 1, 1, it - 1), True, True)
                tile(it * 2 + 1, 1, (it * 2, 0, it), True, True)
            tile(last - 1, 0, (last - 2, 1, last // 2 - 1), True, False)
            tile(last, 1, (last - 1, 0, last // 2), False, False)

        def is_split(eng, t, u):
            if u < 0:
                t, u = t - 1, NU + u
            if u % 2:
                eng.wait_ge(u_hlp, t * (NU // 2) + u // 2 + 1)
            else:
                eng.wait_ge(u_hl, t * (NU - NU // 2) + u // 2 + 1)

        def rows(h, n):
            return slice((h % 4) * HW, (h % 4) * HW + n)

        def one_bank(b, r):
            return bank[b][r, :].rearrange("p (g t) -> p g t", g=2)

        def two_banks(b, r):
            return ps[r, b:b + 2, :].rearrange("p a (g t) -> p (a g) t", g=2)

        def heads4(v, c):
            return v[:, :, c * D:(c + 1) * D].rearrange("p u (h s) -> p u h s", h=H)

        def over_tiles(w):
            return w[:, :, :, :].rearrange("p c h s -> p (c h s)").unsqueeze(1).broadcast_to([P, 2, 2 * D])

        def turns(turn, eng):
            turn(-3, -2, 1, False, False, False, False, True)
            turn(-2, -1, 0, False, False, False, True, True)
            turn(-1, -1, 1, False, False, True, True, True)
            turn(0, 0, 0, True, False, True, True, True)
            with eng.Fori(0, (B - 4) // 2) as it:
                turn(it * 2 + 1, it, 1, True, True, True, True, True)
                turn(it * 2 + 2, it + 1, 0, True, True, True, True, True)
            turn(B - 3, (B - 3) // 2, 1, True, True, True, True, False)
            turn(B - 2, (B - 2) // 2, 0, True, True, True, False, False)
            turn(B - 1, (B - 1) // 2, 1, True, True, False, False, False)
            turn(B, B // 2, 0, False, True, False, False, False)

        block = ctx.enter_context(nc.Block())

        @block.sync
        def _(sp_):
            for i in range(4):
                n = NT // 4
                sp_.dma_start(x_res[:, i * n:(i + 1) * n, :], x_tok[:, i * n:(i + 1) * n, :]).then_inc(x_in[i], 16)
            for o, src in ((0, W1), (D, W2), (D + N, W3)):
                sp_.dma_start(w123[:, o:o + src.shape[1]], src).then_inc(small_in, 16)
            for r in range(2):
                for o, src in ((0, b1), (D, b2), (D + N, b3)):
                    n = src.shape[0]
                    sp_.dma_start(bias[:, r, o:o + n],
                                  src.rearrange("(a n) -> a n", a=1).broadcast_to([P, n])).then_inc(small_in, 16)
            sp_.dma_start(wr_s[:, :], Wr).then_inc(small_in, 16)
            for dst, src, arrived in ((stg, Wg, wg_in), (stu, Wu, wu_in)):
                sp_.dma_start(dst[:, :].rearrange("p (e i) -> p e i", e=E1), src.rearrange("e d i -> d e i")).then_inc(arrived, 16)
            for j in range(JC - 1):
                sp_.dma_start(stv[:, :, j, :], Wd[:, j * P:(j + 1) * P, :].rearrange("e p d -> p e d")).then_inc(wd_in, 16)
            sp_.dma_start(stv[0:R1, :, JC - 1, :],
                          Wd[:, (JC - 1) * P:I1, :].rearrange("e p d -> p e d")).then_inc(wd_in, 16)

            def load_block(b, u):
                src = sp_.value_load(blk_src[0:1, ds(b, 1)], min_val=0, max_val=(E1 - 1) * REG + T)
                sp_.dma_start(xb[:, u, :], xs[ds(src, P), :]).then_inc(xb_in[u], 16)

            for u in range(4):
                sp_.sem_inc(ys_out[u], 16)

            def store_block(b, u):
                sp_.wait_ge(yb_r, b + 1)
                sp_.dma_start(ys[ds(b * P, P), :], yb[:, u, :]).then_inc(ys_out[u], 16)

            sp_.wait_ge(tails, 1)
            for e in range(E1):
                first_row = sp_.value_load(tail[0:1, e:e + 1], min_val=0, max_val=(E1 - 1) * REG + T)
                sp_.dma_start(xs[ds(first_row, P), :], zrow[:, :]).then_inc(tails_in, 16)
            sp_.wait_ge(list_ready, 1)
            for s in range(2):
                sp_.wait_ge(scat[s], 16 * (SUB * K1 * NPIECE // 2))
            sp_.wait_ge(tails_in, 16 * E1)
            for b in range(4):
                load_block(b, b)
            for b in range(4):
                sp_.wait_ge(xT_r, b + 1)
                load_block(b + 4, b)
                if b >= 2:
                    store_block(b - 2, b - 2)
            with sp_.Fori(1, NBLK // 4 - 1) as it:
                for u in range(4):
                    b = it * 4 + u
                    sp_.wait_ge(xT_r, b + 1)
                    load_block(b + 4, u)
                    store_block(b - 2, (u - 2) % 4)
            for b in range(NBLK - 6, NBLK):
                store_block(b, b % 4)
            for u in range(4):
                sp_.wait_ge(ys_out[u], 16 * (NBLK // 4 + 1))
            for j, w in enumerate((WqT, WkT, WvT)):
                sp_.dma_start(wqkv[:, j * D:(j + 1) * D], w).then_inc(c_in, 16)
            sp_.dma_start(wuT[:, :], WuT).then_inc(c_in, 16)
            for j, w in enumerate((qln_w, kln_w, qln_b, kln_b)):
                sp_.dma_start(ln8[:, j, :], w.rearrange("(a n) -> a n", a=1).broadcast_to([P, S])).then_inc(c_in, 16)
            sp_.dma_start(shf[:, 0:F2], Ws_up).then_inc(sh_in, 16)
            sp_.dma_start(shf[0:F2, F2:F2 + D], Ws_down).then_inc(sh_in, 16)
            sp_.dma_start(cen_s[:, :], cent).then_inc(sh_in, 16)
            sp_.dma_start(ebi[:, :], ebias.rearrange("(a n) -> a n", a=1).broadcast_to([P, E2])).then_inc(sh_in, 16)
            PC = WC // D
            for c in range(NC):
                if c >= 2:
                    sp_.wait_ge(wd_done, c - 1)
                for q in range(PC):
                    pair = (c % (NC // 2)) * PC + q
                    dst = wst[:, c % 2, q * D:(q + 1) * D]
                    if c < NC // 2:
                        sp_.dma_start(dst.rearrange("p (two f) -> p two f", two=2),
                                      W_up[2 * pair:2 * pair + 2].rearrange("two d f -> d two f")).then_inc(w_in[c % 2], 16)
                    else:
                        sp_.dma_start(dst, W_down[2 * pair:2 * pair + 2].rearrange("two f d -> (two f) d")).then_inc(w_in[c % 2], 16)
            for p in range(2):
                sp_.sem_inc(o_out[p], 16)
            for t in range(T // TT):
                sp_.wait_ge(u_y, t + 1)
                sp_.dma_start(out_tok[:, t * SUB:(t + 1) * SUB, :], y4[:, t % 2, :, :]).then_inc(o_out[t % 2], 16)
            for p in range(2):
                sp_.wait_ge(o_out[p], 16 * ((T // TT) // 2 + 1))

        @block.gpsimd
        def _(pool):
            own = Tickets(pool, pool_own)
            own.done(pool.memset(ident[:, :], 0.0))
            own.done(pool.memset(trif[:, :], 1.0))
            own.done(pool.memset(eps_c[:, :], LN_EPS))
            own.done(pool.memset(zrow[:, :], 0.0))
            own.done(pool.memset(base[:, :], 0.0))
            own.done(pool.memset(ones[:, :], 1.0))
            for dst, pattern, cm, b0 in ((rev9[:, :, :], [[0, SUB], [-1, E1]], 0, E1), (off9[:, :], [[REG, E1]], 0, 0),
                                         (prow[:, :], [[0, E1]], 1, 0), (iblk[:, :], [[1, NBLK]], 0, 0)):
                own.done(pool.iota(dst, pattern=pattern, base=b0, channel_multiplier=cm,
                                   allow_small_or_imprecise_dtypes=True))
            own.need(own.n)
            own.done(pool.affine_select(out=ident[:, :], in_=ident[:, :], compare_op=ALU.not_equal, fill=1.0,
                                        base=0, pattern=[[-1, P]], channel_multiplier=1))
            own.done(pool.affine_select(out=trif[:, :], in_=trif[:, :], compare_op=ALU.is_gt, fill=0.0,
                                        base=0, pattern=[[1, P]], channel_multiplier=-1))
            own.need(own.n)
            pool.tensor_copy(tri[:, :], trif[:, :]).then_inc(consts, 1)

            for s in range(2):
                pool.sem_inc(scat_ok[s], 1)

            def pool_pieces(it, split):
                if split:
                    part = ds(it * QU, QU)
                    for j, (src, hi, lo) in enumerate(((stg, wgh, wgl), (stu, wuh, wul))):
                        pool.wait_ge(w_hi, it * 3 + 1 + j)
                        pool.tensor_tensor(lo[:, part], src[:, part], hi[:, part].bitcast(F32), op=ALU.subtract).then_inc(w_lo, 1)
                    part = ds(it * QC, QC)
                    pool.wait_ge(w_hi, it * 3 + 3)
                    pool.tensor_tensor(wd2[:, part, 1, :], stc[:, part, :], wd2[:, part, 0, :].bitcast(F32),
                                       op=ALU.subtract).then_inc(w_lo, 1)
                for s in range(2):
                    pool.wait_ge(ps2, it * 2 + s + 1)
                    pool.wait_ge(xo_r, it * 2 + s + 1)
                    apart(pool, pool_passed)
                    for k in range(SUB):
                        for c in range(K1):
                            pool.indirect_dma_start(
                                out=xs, out_offset=bass.IndirectOffsetOnAxis(ap=posi[:, s, k, c:c + 1], axis=0),
                                in_=xo[:, s, k, :], in_offset=None).then_inc(scat[s], 16)
                for s in range(2):
                    pool.wait_ge(scat[s], (it + 1) * (16 * SUB * K1))
                    pool.sem_inc(scat_ok[s], 1)

            with pool.Fori(0, NPIECE // 2 - 1) as it:
                pool_pieces(it, True)
            pool_pieces(NPIECE // 2 - 1, False)
            pool.wait_ge(tails, 1)
            pool.memset(hb[:, :, :], 0.0).then_inc(consts, 1)

            pool.wait_ge(gp_r, 1)
            for u in range(4):
                pool.wait_ge(ys_out[u], 16 * (NBLK // 4 + 1))

            def gather(b, p):
                if not isinstance(b, int) or b >= 2:
                    pool.wait_ge(x2_r, 2 * b - 2)
                    apart(pool, pool_passed)
                pool.tensor_copy(gps[:, p, :], gpi[:, ds(b * (2 * K1), 2 * K1)]).then_inc(gps_r, 1)
                pool.wait_ge(gps_r, b + 1)
                apart(pool, pool_passed)
                for u in range(2):
                    for c in range(K1):
                        pool.indirect_dma_start(
                            out=yg[:, 2 * p + u, c, :], out_offset=None, in_=ys,
                            in_offset=bass.IndirectOffsetOnAxis(ap=gps[:, p, u * K1 + c:u * K1 + c + 1], axis=0),
                        ).then_inc(yg_in[2 * p + u], 16)

            gather(0, 0)

            own = Tickets(pool, pool_own, own.n)
            own.done(pool.memset(identb[:, :], 0.0))
            own.done(pool.memset(mskf[:, :, :], 0.0))
            own.done(pool.memset(ks[:, :, :, :, :].bitcast(F32), 0.0))
            own.done(pool.memset(vp[:, :, :, :, S:S + 1], 1.0))
            own.need(own.n)
            own.done(pool.affine_select(out=identb[:, :], in_=identb[:, :], compare_op=ALU.not_equal, fill=1.0,
                                        base=0, pattern=[[-1, P]], channel_multiplier=1))
            own.done(pool.affine_select(out=mskf[:, 0, :], in_=mskf[:, 0, :], compare_op=ALU.is_ge, fill=-BIG,
                                        base=0, pattern=[[-1, P]], channel_multiplier=1))
            own.done(pool.affine_select(out=mskf[:, 1, :], in_=mskf[:, 1, :], compare_op=ALU.is_ge, fill=-BIG,
                                        base=0, pattern=[[1, P]], channel_multiplier=-1))
            own.done(pool.memset(ks[:, :, :, :, KS:KS + 2].bitcast(F32), 1.0))
            own.need(own.n)
            pool.sem_inc(c_const, 1)

            def p1_pool(b, p):
                pool.wait_ge(c_rq, b + 1)
                pool.tensor_tensor(nq[:, 0, :, :].rearrange("p u (g s) -> p u g s", s=S),
                                   cen[:, :, :].rearrange("p u (g s) -> p u g s", s=S),
                                   rq[:, :, :].unsqueeze(3).broadcast_to([P, 2, 2 * H, S]), op=ALU.mult).then_inc(c_n, 1)
                pool.wait_ge(c_n, b + 1)
                pool.tensor_tensor(nq[:, 1, :, :], nq[:, 0, :, :], over_tiles(lnw), op=ALU.mult).then_inc(pool_w, 1)
                pool.wait_ge(pool_w, b + 1)
                pool.tensor_tensor(nq[:, 0, :, :], nq[:, 1, :, :], over_tiles(lnb), op=ALU.add).then_inc(c_wb, 1)

            def p1_low(b, p):
                pool.wait_ge(c_nh, b + 1)
                for dst, c, o in ((qs, 0, 2 * S), (ks, 1, S)):
                    ins = pool.tensor_tensor(dst[:, p, :, :, o:o + S], heads4(nq[:, 0, :, :], c),
                                             dst[:, p, :, :, 0:S].bitcast(F32), op=ALU.subtract)
                ins.then_inc(c_lo, 1)

            def p2_pool(b, p):
                if not isinstance(b, int) or b >= 2:
                    pool.wait_ge(c_PV, (b - 1) * 4)
                    apart(pool, pool_passed)
                pool.tensor_copy(vp[:, p, :, :, 0:S],
                                 zs[:, p, :, 2 * D:3 * D].rearrange("p u (h s) -> p u h s", h=H)).then_inc(c_vp, 1)

            def parts(c, p, loads):
                pool.wait_ge(w_in[p], loads)
                apart(pool, pool_passed)
                pool.tensor_copy(wh[:, ds(c * WC, WC)], wst[:, p, :]).then_inc(pool_h, 1)
                pool.wait_ge(pool_h, c + 1)
                apart(pool, pool_passed)
                pool.tensor_tensor(wl[:, ds(c * WC, WC)], wst[:, p, :], wh[:, ds(c * WC, WC)].bitcast(F32),
                                   op=ALU.subtract).then_inc(wd_done, 1)

            def pool_turn(i, half, p, E, F, M, P1, G):
                if isinstance(i, int) and i == -3:
                    return
                if G:
                    gather(i + 3, 1 - p)
                if isinstance(i, int) and i == -2:
                    for zeros in (qs[:, :, :, :, :], kz[:, :, :, :], qz[:, :, :, :]):
                        pool.memset(zeros.bitcast(F32), 0.0).then_inc(c_const, 1)
                if M:
                    p2_pool(i + 1, 1 - p)
                if E:
                    parts(i, p, (half + 1) * (16 * WC // D))
                if P1:
                    p1_pool(i + 2, p)
                    p1_low(i + 2, p)

            turns(pool_turn, pool)
            pool.wait_ge(sh_in, 16 * 4)
            for rows_, cols in ((slice(0, P), slice(0, F2)), (slice(0, F2), slice(F2, F2 + D))):
                pool.tensor_copy(shh[rows_, cols], shf[rows_, cols]).then_inc(sh_done, 1)
            pool.wait_ge(sh_done, 2)
            for rows_, cols in ((slice(0, P), slice(0, F2)), (slice(0, F2), slice(F2, F2 + D))):
                pool.tensor_tensor(shl[rows_, cols], shf[rows_, cols], shh[rows_, cols].bitcast(F32),
                                   op=ALU.subtract).then_inc(sh_done, 1)
            pool.wait_ge(c_F6, B + 1)
            sel_f = selr[:, :, :].bitcast(F32)
            pool.memset(sel_f, 0.0).then_inc(d_const, 1)
            for k in range(2):
                pool.wait_ge(d_const, k + 1)
                pool.affine_select(out=selr[:, :, :], in_=sel_f, compare_op=ALU.not_equal, fill=1.0,
                                   base=-k * E2, pattern=[[-1, E2], [0, F2]], channel_multiplier=1).then_inc(d_const, 1)

            def pool_tile(t, p, before, N, S):
                for u in range(1, NU, 2):
                    pool.wait_ge(u_hh, t * NU + u + 1)
                    apart(pool, pool_passed)
                    pool.tensor_tensor(hl4[:, u % 3, :], h4[:, u % 3, :], hh4[:, u % 3, :].bitcast(F32),
                                       op=ALU.subtract).then_inc(u_hlp, 1)

            tiles_of(pool, pool_tile)

        @block.scalar
        def _(act):
            TABLE = "natural_log_exp_and_others"
            act.preload_act_table_set(TABLE)
            act.wait_ge(consts, 1)

            def rstd_of(own, bufs, ready, stats, s, i):
                m, l, r = bufs
                act.wait_ge(stats, i)
                own.link(act.activation(l[:, s, :], m[:, s, :, 1], ACT.Ln, bias=eps_c[:, 0:1]))
                act.activation(r[:, s, :], l[:, s, :], ACT.Exp, scale=-0.5).then_inc(ready, 1)

            def copy_T(dst, first_bank, ready, made, s, i):
                act.wait_ge(made, i)
                act.activation(dst[:, s, :, :].rearrange("p k d -> p (k d)"), bank[first_bank + s][:, :],
                               ACT.Copy).then_inc(ready, 1)

            def act_pieces(k, one, two):
                own1, own2 = Tickets(act, act_own, k * ACT_1), Tickets(act, act_own2, (k - 1) * ACT_2)
                i1, i2 = k * 2 + 1, k * 2 - 1
                if not isinstance(k, int) or k == 0:
                    act.preload_act_table_set(TABLE)
                for s in range(2):
                    if two:
                        rstd_of(own2, (mvb, lnvb, rstdb), rs2, mv2, s, i2 + s)
                    if one:
                        rstd_of(own1, (mv, lnv, rstd), rs1, mv1, s, i1 + s)
                for s in range(2):
                    if one:
                        copy_T(xnT, 0, tc1, tr1, s, i1 + s)
                if one:
                    q = []
                    for s in range(2):
                        act.wait_ge(zc1, i1 + s)
                        q.append(own1.done(act.activation(sp[:, s, 0, :, :], z[:, s, :, 0:D], ACT.Abs)))
                    for s in range(2):
                        own1.need(q[s])
                        q.append(own1.done(act.activation(sp[:, s, 1, :, :], sp[:, s, 0, :, :], ACT.Exp, scale=-1.0)))
                    for s in range(2):
                        own1.need(q[2 + s])
                        act.activation(sp[:, s, 0, :, :], sp[:, s, 1, :, :], ACT.Ln, bias=1.0).then_inc(sp1, 1)
                    assert own1.n == ACT_1, own1.n
                for s in range(2):
                    if two:
                        copy_T(xmT, 6, tc2, tr2, s, i2 + s)
                if one and two:
                    for arrived, n, src, hi in ((wg_in, 1, stg[:, ds((k - 1) * QU, QU)], wgh[:, ds((k - 1) * QU, QU)]),
                                                (wu_in, 1, stu[:, ds((k - 1) * QU, QU)], wuh[:, ds((k - 1) * QU, QU)]),
                                                (wd_in, JC, stc[:, ds((k - 1) * QC, QC), :],
                                                 wd2[:, ds((k - 1) * QC, QC), 0, :])):
                        act.wait_ge(arrived, 16 * n)
                        act.activation(hi, src, ACT.Copy).then_inc(w_hi, 1)
                if two:
                    for s in range(2):
                        act.wait_ge(df2, i2 + s)
                        act.activation(r1[:, s, 4, :], r1[:, s, 3, :], ACT.Exp).then_inc(ex2, 1)
                    for s in range(2):
                        act.wait_ge(scat_ok[s], k)
                        act.activation(xo[:, s, :, :], xm[:, s, :, :], ACT.Copy).then_inc(xo_r, 1)
                    assert own2.n == ACT_2, own2.n

            pieces(act, act_pieces)

            def x_hi(b, v):
                act.wait_ge(xT_r, b + 1)
                act.activation(xbh[:, v, :], bank[0][:, 0:D], ACT.Copy).then_inc(xh_r, 1)

            def silu(b, v):
                act.wait_ge(gu_r, b + 1)
                act.activation(sg[:, v, :], bank[4 + v][:, 0:I1], ACT.Silu).then_inc(sg_r, 1)

            def h_hi(b, v):
                act.wait_ge(hT_r, b + 1)
                act.activation(hh[:, v, :], bank[2 + v][:, 0:IP], ACT.Copy).then_inc(hh_r, 1)

            x_hi(0, 0)
            for b in range(4):
                x_hi(b + 1, (b + 1) % 2)
                silu(b, b % 2)
                if b >= 1:
                    h_hi(b - 1, (b - 1) % 2)
            with act.Fori(1, NBLK // 4 - 1) as it:
                for u in range(4):
                    b = it * 4 + u
                    x_hi(b + 1, (u + 1) % 2)
                    silu(b, u % 2)
                    h_hi(b - 1, (u - 1) % 2)
            for b in range(NBLK - 4, NBLK + 1):
                if b + 1 < NBLK:
                    x_hi(b + 1, (b + 1) % 2)
                if b < NBLK:
                    silu(b, b % 2)
                h_hi(b - 1, (b - 1) % 2)

            act.wait_ge(c_in, 16 * 8)
            act.activation(wqh[:, :], wqkv[:, :], ACT.Copy).then_inc(c_w, 1)
            act.activation(idr[:, 1, :], ident[:, :], ACT.Copy).then_inc(c_w, 1)
            act.wait_ge(c_w, 6)

            def act_turn(i, half, p, E, F, M, P1, G):
                if not isinstance(i, int) or i in (-3, B - 3):
                    act.preload_act_table_set(TABLE)

                b1, b2 = i + 1, i + 2

                def exp(g):
                    if E:
                        act.wait_ge(c_S2, i * 4 + g + 1)
                        if g >= 2 or not isinstance(i, int) or i > 0:
                            act.wait_ge(c_PV, i * 4 + g - 1)
                        act.activation(pt[:, g % 2, :, :, :].rearrange("p b j k -> p (b j k)"),
                                       ps[:, 0:3, :].rearrange("p b k -> p (b k)"), ACT.Exp).then_inc(c_P, 1)

                def out_copy(g):
                    if E:
                        act.wait_ge(c_PV, i * 4 + g + 1)
                        act.activation(ot[:, p, g, :], bank[6][:, 0:2 * P], ACT.Copy).then_inc(c_OT, 1)

                def q2_copies(b, c):
                    act.wait_ge(c_T2, 2 * b + c + 1)
                    for j in range(QA):
                        ins = act.activation(qz[rows(j, HW), 2 * c:2 * c + 2, j, :], one_bank(7, rows(j, HW)), ACT.Copy)
                    ins.then_inc(c_q2, 1)

                def z_copy(u):
                    if P1:
                        act.wait_ge(c_z, 2 * b2 + u + 1)
                        act.activation(zs[:, p, u, :], bank[7][:, 0:3 * D], ACT.Copy).then_inc(c_zs, 1)

                if M:
                    act.wait_ge(c_T3, b1 + 1)
                    act.activation(kz[rows(0, KS), :, 0, :], two_banks(3, rows(0, KS)), ACT.Copy)
                if P1:
                    act.wait_ge(c_xT, b2 + 1)
                    act.activation(xch[:, :, :], bank[7][:, 0:2 * P].rearrange("p (u t) -> p u t", u=2),
                                   ACT.Copy).then_inc(c_xh, 1)
                if M:
                    for j in range(1, KA):
                        act.activation(kz[rows(j, KS), :, j, :], two_banks(3, rows(j, KS)), ACT.Copy)
                    low = slice(0, KA * HW)
                    act.activation(kT[low, 1 - p, :, :], two_banks(3, low), ACT.Copy).then_inc(c_kz, 1)
                    act.wait_ge(c_T, b1 + 1)
                    act.activation(qT[:, :, :], two_banks(5, rows(0, P)), ACT.Copy).then_inc(c_qT, 1)
                exp(0)
                z_copy(0)
                if G:
                    act.wait_ge(c_mv, i + 4)
                    act.activation(cln[:, :], cmv[:, :, 1], ACT.Ln, bias=eps_c[:, 0:1]).then_inc(act_c, 1)
                    act.wait_ge(act_c, i + 4)
                    act.activation(crs[:, :], cln[:, :], ACT.Exp, scale=-0.5).then_inc(c_rs, 1)
                z_copy(1)
                exp(1)
                out_copy(0)
                if E:
                    q2_copies(i, 1)
                if P1:
                    act.wait_ge(c_cen, b2 + 1)
                    act.activation(csq[:, :, :], cen[:, :, :], ACT.Square).then_inc(c_sq, 1)
                out_copy(1)
                exp(2)
                if P1:
                    act.wait_ge(c_vs, b2 + 1)
                    act.activation(rql[:, :, :], vsm[:, :, :], ACT.Ln, bias=eps_c[:, 0:1], scale=1.0 / S).then_inc(act_c2, 1)
                    act.wait_ge(act_c2, b2 + 1)
                    act.activation(rq[:, :, :], rql[:, :, :], ACT.Exp, scale=-0.5).then_inc(c_rq, 1)
                out_copy(2)
                if F:
                    act.wait_ge(c_F3, i)
                    act.activation(ooT[:, :, :], bank[7][:, 0:2 * P].rearrange("p (u t) -> p u t", u=2),
                                   ACT.Copy).then_inc(c_F4, 1)
                exp(3)
                if isinstance(i, int) and i == -2:
                    act.wait_ge(c_const, 4)
                if P1:
                    act.wait_ge(c_wb, b2 + 1)
                    for dst, c, o in ((qs, 0, 0), (ks, 1, 0), (qs, 0, S), (ks, 1, 2 * S)):
                        ins = act.activation(dst[:, p, :, :, o:o + S], heads4(nq[:, 0, :, :], c), ACT.Copy)
                        if o == 0 and c == 1:
                            ins.then_inc(c_nh, 1)
                    ins.then_inc(c_dup, 1)
                if M:
                    q2_copies(b1, 0)
                out_copy(3)

            turns(act_turn, act)

            def x4_rstd(n, p):
                act.wait_ge(d_mv, n + 1)
                act.activation(lnv[:, p, :], mv[:, p, :, 1], ACT.Ln, bias=eps_c[:, 0:1]).then_inc(act_d, 1)
                act.wait_ge(act_d, n + 1)
                act.activation(rstd[:, p, :], lnv[:, p, :], ACT.Exp, scale=-0.5).then_inc(d_rs, 1)

            def x4_T(n, p):
                act.wait_ge(d_T, n + 1)
                act.activation(xnT4[:, :, :].rearrange("p k t -> p (k t)"), bank[6][:, :], ACT.Copy).then_inc(d_Tc, 1)

            def x4_exp(n, p):
                act.wait_ge(d_afc, n + 1)
                act.activation(g4[:, 0, :, :], af[:, :, :], ACT.Exp, scale=-1.0).then_inc(d_ex, 1)

            def x4_weights(n, p):
                act.wait_ge(d_cT, n + 1)
                act.activation(cwT[:, p, :], bank[6][:, :], ACT.Copy).then_inc(d_cw, 1)

            for n in range(2):
                x4_rstd(n, n)
            x4_T(0, 0)
            x4_exp(0, 0)
            x4_weights(0, 0)

            def e_silu(t, u):
                act.wait_ge(u_up, t * NU + u + 1)
                r = slice(0, F2 if u == 0 else P)
                if u == 0:
                    if not (isinstance(t, int) and t == 0):
                        is_split(act, t, -3)
                    act.activation(h4[r, u % 3, :], bank[u % 3][r, :], ACT.Silu).then_inc(u_sg0, 1)
                else:
                    act.activation(sg4[r, u % 3, :], bank[u % 3][r, :], ACT.Silu).then_inc(u_sg, 1)

            def e_hi(t, u):
                r = slice(0, F2 if u == 0 else P)
                if u == 0:
                    act.wait_ge(u_sg0, t + 1)
                else:
                    act.wait_ge(u_h, t * NP2 + u)
                if u >= 3:
                    act.wait_ge(u_dn, t * NU + u - 2)
                elif not (isinstance(t, int) and t == 0):
                    act.wait_ge(u_dn, (t - 1) * NU + NU + u - 2)
                act.activation(hh4[r, u % 3, :], h4[r, u % 3, :], ACT.Copy).then_inc(u_hh, 1)

            def out_copy4(t, p):
                act.wait_ge(u_dn, (t + 1) * NU)
                act.activation(oT4[:, :], bank[5 + 2 * p][:, :], ACT.Copy).then_inc(u_oT, 1)

            def act_tile(t, p, before, N, S):
                for u in range(NU):
                    e_silu(t, u)
                    if u >= 1:
                        e_hi(t, u - 1)
                    elif before is not None:
                        e_hi(before[0], NU - 1)
                    if u == 5 and before is not None:
                        out_copy4(before[0], before[1])
                    if u == 12 and N:
                        x4_T(t + 1, 1 - p)
                    if u == 16 and N:
                        act.preload_act_table_set(TABLE)
                        x4_exp(t + 1, 1 - p)
                        if S:
                            x4_rstd(t + 2, p)
                    if u == 28 and N:
                        x4_weights(t + 1, 1 - p)

            tiles_of(act, act_tile)
            e_hi(T // TT - 1, NU - 1)
            out_copy4(T // TT - 1, 1)

        @block.vector
        def _(dve):
            dve.memset(stv[R1:P, :, JC - 1, :], 0.0)
            dve.wait_ge(x_in[0], 16)
            dve.wait_ge(consts, 1)

            def stats(own, s, t0, ready, bufs=(st, mv)):
                a, m = bufs
                for k in range(SUB):
                    last = own.done(dve.bn_stats(out=a[:, s, k, :], in_=x_res[:, ds(t0 + k, 1), :]))
                own.need(last)
                apart(dve, dve_passed)
                for k in range(SUB):
                    ins = dve.bn_aggr(out=m[:, s, k, :], in_=a[:, s, k, :])
                ins.then_inc(ready, 1)

            def normed(dst, s, t0, m, r, scaled, i, ready):
                dve.wait_ge(scaled, i)
                for k in range(SUB):
                    ins = dve.tensor_scalar(dst[:, s, k:k + 1, :], x_res[:, ds(t0 + k, 1), :], m[:, s, k, 0:1],
                                            r[:, s, k:k + 1], ALU.subtract, ALU.mult)
                ins.then_inc(ready, 1)

            def wide(v):
                return v.unsqueeze(2).broadcast_to([P, SUB, E1])

            def dve_pieces(k, one, two):
                own1, own2 = Tickets(dve, dve_own, k * DVE_1), Tickets(dve, dve_own2, (k - 1) * DVE_2)
                i1, i2 = k * 2 + 1, k * 2 - 1
                q = []

                def first_tile(s, part):
                    return ((k if part == 1 else k - 1) * 2 + s) * SUB

                def tiles(s):
                    return ds(first_tile(s, 2), SUB)

                def both(op):
                    was = list(q)
                    for s in range(2):
                        own2.need(was[s])
                        q[s] = own2.done(op(s))

                def choice(c):
                    row = (lambda s: lg[:, s, :, :]) if c == 0 else (lambda s: r9[:, s, 2, :, :])
                    both(lambda s: dve.tensor_reduce(r1[:, s, c, :], row(s), axis=AX.X, op=ALU.max))
                    both(lambda s: dve.tensor_tensor(r9[:, s, 0, :, :], row(s), wide(r1[:, s, c, :]), op=ALU.is_equal))
                    both(lambda s: dve.tensor_tensor(r9[:, s, 1, :, :], r9[:, s, 0, :, :], rev9[:, :, :], op=ALU.mult))
                    both(lambda s: dve.tensor_reduce(r1[:, s, 2, :], r9[:, s, 1, :, :], axis=AX.X, op=ALU.max))
                    both(lambda s: dve.tensor_tensor(pick[:, tiles(s), c, :], r9[:, s, 1, :, :], wide(r1[:, s, 2, :]),
                                                     op=ALU.is_equal))
                    if c == 0:
                        both(lambda s: dve.scalar_tensor_tensor(r9[:, s, 2, :, :], pick[:, tiles(s), c, :], -BIG,
                                                                lg[:, s, :, :], ALU.mult, ALU.add))

                if two:
                    dve.wait_ge(dve_own, k * DVE_1)
                    apart(dve, dve_passed)
                    for s in range(2):
                        stats(own2, s, first_tile(s, 2), mv2, (stb, mvb))
                if one:
                    for s in range(2):
                        stats(own1, s, first_tile(s, 1), mv1)
                    if isinstance(k, int):
                        for i in range(1, 4):
                            dve.wait_ge(x_in[i], 16)
                if one:
                    for s in range(2):
                        normed(xn, s, first_tile(s, 1), mv, rstd, rs1, i1 + s, xn1)
                if one:
                    q1 = []
                    if isinstance(k, int):
                        dve.wait_ge(small_in, 16 * 10)
                    for s in range(2):
                        dve.wait_ge(zz1, i1 + s)
                        zv = z[:, s, :, :].rearrange("p (a b) m -> p a (b m)", a=2)
                        for a in range(2):
                            ins = dve.tensor_tensor(zv[:, a, :], bank[2 + 2 * s + a][:, 0:2 * M1],
                                                    bias[:, :, :].rearrange("p a m -> p (a m)"), op=ALU.add)
                        ins.then_inc(zc1, 1)
                    for s in range(2):
                        dve.wait_ge(zc1, i1 + s)
                        q1.append(own1.done(dve.tensor_tensor(bc[:, s, :, :], z[:, s, :, D:D + N], z[:, s, :, D + N:M1],
                                                              op=ALU.mult)))
                    for s in range(2):
                        own1.need(q1[s])
                        own1.done(dve.tensor_reduce(bcs[:, s, :], bc[:, s, :, :], axis=AX.X, op=ALU.add))
                if two:
                    for s in range(2):
                        normed(xm, s, first_tile(s, 2), mvb, rstdb, rs2, i2 + s, xn2)
                if two:
                    for s in range(2):
                        dve.wait_ge(lg2, i2 + s)
                        q.append(own2.done(dve.tensor_copy(
                            lg[:, s, :, :], bank[6 + s][:, 0:16 * SUB].rearrange("p (k e) -> p k e", e=16)[:, :, 0:E1])))
                    choice(0)
                if one:
                    q1 = []
                    for s in range(2):
                        dve.wait_ge(sp1, i1 + s)
                        q1.append(own1.done(dve.scalar_tensor_tensor(
                            sp[:, s, 1, :, :], z[:, s, :, 0:D], 0.0, sp[:, s, 0, :, :], ALU.max, ALU.add)))
                    for s in range(2):
                        own1.need(q1[s])
                        q1.append(own1.done(dve.tensor_tensor(sp[:, s, 2, :, :], sp[:, s, 1, :, :], xn[:, s, :, :],
                                                              op=ALU.mult)))
                    for s in range(2):
                        own1.need(q1[2 + s])
                        for j in range(SUB):
                            t = ds(first_tile(s, 1) + j, 1)
                            own1.done(dve.scalar_tensor_tensor(
                                x_res[:, t, :], sp[:, s, 2, j:j + 1, :], bcs[:, s, j:j + 1], x_res[:, t, :],
                                ALU.mult, ALU.add))
                    assert own1.n == DVE_1, own1.n
                if two:
                    choice(1)
                    for s in range(2):
                        dve.tensor_tensor(r1[:, s, 3, :], r1[:, s, 1, :], r1[:, s, 0, :], op=ALU.subtract).then_inc(df2, 1)
                    for s in range(2):
                        own2.need(q[s])
                        dve.tensor_tensor(sel[:, s, :, :], pick[:, tiles(s), 0, :], pick[:, tiles(s), 1, :],
                                          op=ALU.add).then_inc(sl2, 1)
                if two:
                    for s in range(2):
                        dve.wait_ge(ex2, i2 + s)
                        q[s] = own2.done(dve.tensor_scalar(r1[:, s, 5, :], r1[:, s, 4, :], 1.0, None, ALU.add))
                    both(lambda s: dve.reciprocal(r1[:, s, 6, :], r1[:, s, 5, :]))
                    both(lambda s: dve.tensor_scalar(wgt[:, tiles(s), 0], r1[:, s, 6, :], 0.0, None, ALU.add))
                    both(lambda s: dve.tensor_tensor(wgt[:, tiles(s), 1], r1[:, s, 6, :], r1[:, s, 4, :], op=ALU.mult))
                    for s in range(2):
                        dve.wait_ge(rk2, i2 + s)
                        ranks = bank[6 + s][:, 16 * SUB:16 * SUB + (SUB + 1) * E1]
                        own2.link(dve.tensor_tensor(
                            r9[:, s, 3, :, :], ranks[:, 0:SUB * E1].rearrange("p (k e) -> p k e", e=E1),
                            base[:, :].unsqueeze(1).broadcast_to([P, SUB, E1]), op=ALU.add))
                        own2.done(dve.tensor_tensor(base[:, :], ranks[:, SUB * E1:(SUB + 1) * E1], base[:, :], op=ALU.add))
                        own2.link(dve.tensor_tensor(
                            r9[:, s, 4, :, :], r9[:, s, 3, :, :],
                            off9[:, :].unsqueeze(1).broadcast_to([P, SUB, E1]), op=ALU.add))
                        for c in range(K1):
                            own2.done(dve.tensor_tensor(r9[:, s, c, :, :], r9[:, s, 4, :, :], pick[:, tiles(s), c, :],
                                                        op=ALU.mult))
                        own2.need(own2.n)
                        for c in range(K1):
                            own2.done(dve.tensor_reduce(posf[:, tiles(s), c], r9[:, s, c, :, :], axis=AX.X, op=ALU.add))
                        own2.need(own2.n)
                        dve.wait_ge(scat_ok[s], k)
                        apart(dve, dve_passed)
                        dve.tensor_copy(posi[:, s, :, :], posf[:, tiles(s), :]).then_inc(ps2, 1)
                    assert own2.n == DVE_2, own2.n

            pieces(dve, dve_pieces)

            own = Tickets(dve, dve_own2, (NPIECE // 2) * DVE_2)
            own.link(dve.tensor_tensor(q9[:, 0, :], base[:, :], off9[:, :], op=ALU.add))
            own.done(dve.tensor_scalar(cnti[:, :], base[:, :], float(P - 1), None, ALU.add))
            own.link(dve.tensor_tensor(q9[:, 1, :], q9[:, 0, :], prow[:, :], op=ALU.add))
            dve.tensor_copy(tail[:, :], q9[:, 1, :]).then_inc(tails, 1)
            own.link(dve.tensor_single_scalar(cnti[:, :], cnti[:, :], 7, ALU.logical_shift_right))
            own.link(dve.tensor_copy(nblk[:, :], cnti[:, :]))
            own.link(dve.tensor_copy(bend[:, 0:1], nblk[:, 0:1]))
            for e in range(1, E1):
                own.link(dve.tensor_tensor(bend[:, e:e + 1], bend[:, e - 1:e], nblk[:, e:e + 1], op=ALU.add))
            own.link(dve.tensor_tensor(bstart[:, :], bend[:, :], nblk[:, :], op=ALU.subtract))
            own.link(dve.scalar_tensor_tensor(q9[:, 2, :], bstart[:, :], -float(P), off9[:, :], ALU.mult, ALU.add))

            def over_e(v):
                return v.unsqueeze(2).broadcast_to([P, NBLK, E1])

            def over_b(v):
                return v.unsqueeze(1).broadcast_to([P, NBLK, E1])

            own.done(dve.tensor_tensor(b9[:, 0, :, :], over_e(iblk[:, :]), over_b(bstart[:, :]), op=ALU.is_ge))
            own.done(dve.tensor_tensor(b9[:, 1, :, :], over_e(iblk[:, :]), over_b(bend[:, :]), op=ALU.is_lt))
            own.need(own.n)
            own.done(dve.tensor_tensor(b9[:, 2, :, :], b9[:, 0, :, :], b9[:, 1, :, :], op=ALU.mult))
            own.need(own.n)
            own.link(dve.tensor_tensor(b9[:, 0, :, :], over_e(iblk[:, :]), over_b(bend[:, :]), op=ALU.is_ge))
            own.done(dve.tensor_reduce(bf[:, 0, :], b9[:, 0, :, :], axis=AX.X, op=ALU.add))
            own.link(dve.tensor_tensor(b9[:, 1, :, :], b9[:, 2, :, :], over_b(q9[:, 2, :]), op=ALU.mult))
            own.done(dve.tensor_reduce(bf[:, 1, :], b9[:, 1, :, :], axis=AX.X, op=ALU.add))
            own.done(dve.tensor_reduce(bf[:, 2, :], b9[:, 2, :, :], axis=AX.X, op=ALU.add))
            own.link(dve.tensor_scalar(bf[:, 0, :], bf[:, 0, :], float(E1 - 1), None, ALU.min))
            own.link(dve.scalar_tensor_tensor(b9[:, 0, 0:NBLK, 0], iblk[:, :], float(P), bf[:, 2, :], ALU.mult, ALU.mult))
            own.link(dve.tensor_tensor(bf[:, 1, :], bf[:, 1, :], b9[:, 0, 0:NBLK, 0], op=ALU.add))
            own.link(dve.tensor_scalar(bf[:, 2, :], bf[:, 2, :], -float((E1 - 1) * REG), float((E1 - 1) * REG),
                                       ALU.mult, ALU.add))
            own.link(dve.tensor_tensor(bf[:, 1, :], bf[:, 1, :], bf[:, 2, :], op=ALU.add))
            own.done(dve.tensor_copy(blk_e[:, :], bf[:, 0, :]))
            dve.tensor_copy(blk_src[:, :], bf[:, 1, :]).then_inc(list_ready, 1)
            pk = pick[:, :, :, :].rearrange("p t c e -> p (t c) e")
            own.link(dve.tensor_tensor(gp9[:, :, :], pk, q9[:, 2, :].unsqueeze(1).broadcast_to([P, NT * K1, E1]),
                                       op=ALU.mult))
            own.link(dve.tensor_reduce(gpf[:, :], gp9[:, :, :], axis=AX.X, op=ALU.add))
            own.link(dve.tensor_tensor(gpf[:, :], posf[:, :, :].rearrange("p t c -> p (t c)"), gpf[:, :], op=ALU.subtract))
            dve.tensor_copy(gpi[:, :], gpf[:, :]).then_inc(gp_r, 1)

            def x_lo(b, v):
                dve.wait_ge(xh_r, b + 1)
                dve.tensor_tensor(xbl[:, v, :], bank[0][:, 0:D], xbh[:, v, :].bitcast(F32),
                                  op=ALU.subtract).then_inc(xl_r, 1)

            def h_of(b, v):
                dve.wait_ge(sg_r, b + 1)
                dve.tensor_tensor(hb[:, v, 0:I1], sg[:, v, :], bank[6 + v][:, 0:I1], op=ALU.mult).then_inc(h_r, 1)

            def h_lo(b, v, first):
                dve.wait_ge(hh_r, b + 1)
                if not first:
                    dve.wait_ge(y_r, b - 1)
                dve.tensor_tensor(hl[:, v, :], bank[2 + v][:, 0:IP], hh[:, v, :].bitcast(F32),
                                  op=ALU.subtract).then_inc(hl_r, 1)

            def y_out(b, u, again):
                dve.wait_ge(y_r, b + 1)
                if again is not None:
                    dve.wait_ge(ys_out[u], again + 16)
                dve.tensor_reduce(yb[:, u, :], bank[1][:, 0:2 * D].rearrange("p (h d) -> p d h", h=2),
                                  axis=AX.X, op=ALU.add).then_inc(yb_r, 1)

            x_lo(0, 0)
            for b in range(4):
                x_lo(b + 1, (b + 1) % 2)
                h_of(b, b % 2)
                if b >= 1:
                    h_lo(b - 1, (b - 1) % 2, b < 3)
                if b >= 2:
                    y_out(b - 2, b - 2, None)
            with dve.Fori(1, NBLK // 4 - 1) as it:
                for u in range(4):
                    b = it * 4 + u
                    x_lo(b + 1, (u + 1) % 2)
                    h_of(b, u % 2)
                    h_lo(b - 1, (u - 1) % 2, False)
                    y_out(b - 2, (u - 2) % 4, (it if u >= 2 else it - 1) * 16)
            for b in range(NBLK - 4, NBLK + 2):
                if b + 1 < NBLK:
                    x_lo(b + 1, (b + 1) % 2)
                if b < NBLK:
                    h_of(b, b % 2)
                if b - 1 < NBLK:
                    h_lo(b - 1, (b - 1) % 2, False)
                y_out(b - 2, (b - 2) % 4, 16 * ((b - 2) // 4))

            def add_rows(b, p, loads):
                for u in range(2):
                    dve.wait_ge(yg_in[2 * p + u], loads)
                for c in range(K1):
                    for u in range(2):
                        t = ds(2 * b + u, 1)
                        if c == 1:
                            dve.wait_ge(x2_half, 2 * b + u + 1)
                        dve.scalar_tensor_tensor(x_res[:, t, :], yg[:, 2 * p + u, c:c + 1, :], wgt[:, t, c],
                                                 x_res[:, t, :], ALU.mult, ALU.add).then_inc(x2_half if c == 0 else x2_r, 1)

            for u in range(4):
                dve.wait_ge(ys_out[u], 16 * (NBLK // 4 + 1))
            dve.sem_inc(c_F6, 1)
            dve.memset(idr[:, 0, :].bitcast(F32), 0.0)
            dve.memset(idr[:, 2, :].bitcast(F32), 0.0).then_inc(c_w, 1)
            dve.wait_ge(c_in, 16 * 8)
            dve.wait_ge(c_w, 3)
            dve.tensor_tensor(wql[:, :], wqkv[:, :], wqh[:, :].bitcast(F32), op=ALU.subtract).then_inc(c_w, 1)
            scale = 1.0 / float(S) ** 0.5
            for j, (dst, c) in enumerate(((lnw, 0), (lnw, 1), (lnb, 0), (lnb, 1))):
                ins = dve.tensor_scalar(dst[:, c, :, :], ln8[:, j, :].unsqueeze(1).broadcast_to([P, H, S]),
                                        scale if c == 0 else 1.0, None, ALU.mult)
                if j % 2:
                    ins.then_inc(c_w, 1)

            def dve_turn(i, half, p, E, F, M, P1, G):
                b1, b2 = i + 1, i + 2

                def attended(u):
                    if F:
                        dve.wait_ge(c_F1, 2 * i - 1 + u)
                        o = bank[7][:, :].rearrange("p (h w) -> p h w", w=HW)
                        dve.reciprocal(rc[:, u, :], o[:, :, S]).then_inc(dve_cf, 1)
                        dve.wait_ge(dve_cf, 2 * i - 1 + u)
                        dve.tensor_tensor(oo[:, u, :].rearrange("p (h s) -> p h s", h=H), o[:, :, 0:S],
                                          rc[:, u, :].unsqueeze(2).broadcast_to([P, H, S]), op=ALU.mult).then_inc(c_F2, 1)

                def maxima(g):
                    if M:
                        dve.wait_ge(c_S1, b1 * 4 + g + 1)
                        for u, o in ((0, bank[3].rearrange("p (j k) -> p j k", j=4)),
                                     (1, ps[:, 4:6, :].rearrange("p b (j k) -> p (b j) k", j=2))):
                            ins = dve.tensor_reduce(nm[:, u, 4 * g:4 * g + 4], o, axis=AX.X, op=ALU.max, negate=True)
                        ins.then_inc(c_mx, 1)

                def q2_copies(b, c):
                    dve.wait_ge(c_T2, 2 * b + c + 1)
                    for j in range(QA, 4):
                        ins = dve.tensor_copy(qz[rows(j, HW), 2 * c:2 * c + 2, j, :], one_bank(7, rows(j, HW)))
                    ins.then_inc(c_q2d, 1)

                def place_maxima(c):
                    hs = slice(8 * c, 8 * c + 8)
                    dve.wait_ge(c_mx, b1 * 4 + 2 * c + 2)
                    dve.tensor_scalar(nmh[:, :, hs], nm[:, :, hs], 0.0, None, ALU.add).then_inc(dve_nm, 1)
                    dve.wait_ge(dve_nm, b1 * 2 + c + 1)
                    dve.tensor_copy(qs[:, 1 - p, :, hs, KS], nmh[:, :, hs].bitcast(F32))
                    dve.tensor_tensor(qs[:, 1 - p, :, hs, KS + 1], nm[:, :, hs], nmh[:, :, hs].bitcast(F32),
                                      op=ALU.subtract).then_inc(c_nm, 1)

                if M:
                    dve.wait_ge(c_T3, b1 + 1)
                    dve.tensor_copy(kz[rows(KA, KS), :, KA, :], two_banks(3, rows(KA, KS)))
                if isinstance(i, int) and i == -2:
                    dve.wait_ge(c_const, 1)
                    for which in range(2):
                        for j in range(4):
                            ins = dve.tensor_copy(msk[:, which, j, :], mskf[:, which, :])
                    ins.then_inc(c_w, 1)
                if P1:
                    dve.wait_ge(c_xh, b2 + 1)
                    dve.tensor_tensor(xcl[:, :, :], bank[7][:, 0:2 * P].rearrange("p (u t) -> p u t", u=2),
                                      xch[:, :, :].bitcast(F32), op=ALU.subtract).then_inc(c_xl, 1)
                if M:
                    for j in range(KA + 1, 4):
                        dve.tensor_copy(kz[rows(j, KS), :, j, :], two_banks(3, rows(j, KS)))
                    high = slice(KA * HW, P)
                    dve.tensor_copy(kT[high, 1 - p, :, :], two_banks(3, high)).then_inc(c_kT, 1)
                if G:
                    b3 = i + 3
                    add_rows(b3, 1 - p, (half + 2 + p) * (16 * K1))
                    dve.wait_ge(x2_r, 2 * b3 + 2)
                    apart(dve, dve_passed)
                    ln = Tickets(dve, dve_ln, b3 * 2)
                    for u in range(2):
                        t = ln.done(dve.bn_stats(out=cst[:, u, :], in_=x_res[:, ds(b3 * 2 + u, 1), :]))
                    ln.need(t)
                    apart(dve, dve_passed)
                    for u in range(2):
                        ins = dve.bn_aggr(out=cmv[:, u, :], in_=cst[:, u, :])
                    ins.then_inc(c_mv, 1)
                maxima(0)
                if G:
                    dve.wait_ge(c_rs, b3 + 1)
                    for u in range(2):
                        ins = dve.tensor_scalar(xc[:, u:u + 1, :], x_res[:, ds(b3 * 2 + u, 1), :], cmv[:, u, 0:1],
                                                crs[:, u:u + 1], ALU.subtract, ALU.mult)
                    ins.then_inc(c_xn, 1)
                if P1:
                    own = Tickets(dve, dve_c1, b2)
                    dve.wait_ge(c_zs, b2 * 2 + 2)
                    own.link(dve.tensor_reduce(ms[:, :, :], zs[:, p, :, 0:2 * D].rearrange("p u (g s) -> p u g s", s=S),
                                               axis=AX.X, op=ALU.add))
                    for u in range(2):
                        ins = dve.scalar_tensor_tensor(
                            cen[:, u, :].rearrange("p (g s) -> p g s", s=S),
                            ms[:, u, :].unsqueeze(2).broadcast_to([P, 2 * H, S]), -1.0 / S,
                            zs[:, p, u, 0:2 * D].rearrange("p (g s) -> p g s", s=S), ALU.mult, ALU.add)
                    ins.then_inc(c_cen, 1)
                if E:
                    q2_copies(i, 1)
                if P1:
                    dve.wait_ge(c_sq, b2 + 1)
                    dve.tensor_reduce(vsm[:, :, :], csq[:, :, :].rearrange("p u (g s) -> p u g s", s=S),
                                      axis=AX.X, op=ALU.add).then_inc(c_vs, 1)
                maxima(1)
                if M:
                    place_maxima(0)
                attended(0)
                attended(1)
                maxima(2)
                if M:
                    q2_copies(b1, 0)
                maxima(3)
                if M:
                    place_maxima(1)
                if F:
                    dve.wait_ge(c_F5, i)
                    t = ds((i - 1) * 2, 2)
                    dve.tensor_tensor(x_res[:, t, :], bank[7][:, 0:2 * D].rearrange("p (u d) -> p u d", u=2),
                                      x_res[:, t, :], op=ALU.add).then_inc(c_F6, 1)

            turns(dve_turn, dve)

            def x4_stats(n, p):
                own = Tickets(dve, dve_s, n * DVE_S)
                stats(own, p, n * SUB, d_mv)
                assert own.n == DVE_S

            def flat(v):
                return v.rearrange("p k e -> p (k e)")

            def routing(n, p):
                own = Tickets(dve, dve_d, n * DVE_D)

                def norm():
                    dve.wait_ge(d_rs, n + 1)
                    for k in range(SUB):
                        ins = dve.tensor_scalar(xm4[:, k:k + 1, :], x_res[:, ds(n * SUB + k, 1), :], mv[:, p, k, 0:1],
                                                rstd[:, p, k:k + 1], ALU.subtract, ALU.mult)
                    ins.then_inc(d_xn, 1)

                def high():
                    dve.wait_ge(d_Tc, n + 1)
                    apart(dve, dve_passed)
                    own.done(dve.tensor_copy(xh4[:, p, :], flat(xnT4[:, :, :])))

                def low():
                    own.need(1)
                    dve.tensor_tensor(xl4[:, p, :], flat(xnT4[:, :, :]), xh4[:, p, :].bitcast(F32),
                                      op=ALU.subtract).then_inc(d_hl, 1)

                def affinity():
                    dve.wait_ge(d_af, n + 1)
                    dve.tensor_copy(af[:, :, :], bank[6][:, 0:SUB * E2].rearrange("p (k e) -> p k e", e=E2)).then_inc(d_afc, 1)

                def biased():
                    dve.wait_ge(d_afc, n + 1)
                    own.done(dve.tensor_tensor(bi[:, :, :], af[:, :, :],
                                               ebi[:, :].unsqueeze(1).broadcast_to([P, SUB, E2]), op=ALU.add))

                def largest():
                    own.need(own.n)
                    apart(dve, dve_passed)
                    for k in range(SUB):
                        own.done(dve.max(out=m8[:, k, :], in_=bi[:, k, :]))

                def replaced():
                    own.need(own.n)
                    apart(dve, dve_passed)
                    for k in range(SUB):
                        own.done(dve.match_replace(out=mr[:, k, :], in_to_replace=m8[:, k, :], in_values=bi[:, k, :],
                                                   imm_value=-BIG))

                def chosen():
                    own.need(own.n)
                    own.done(dve.tensor_tensor(g4[:, 1, :, :], mr[:, :, :], bi[:, :, :], op=ALU.not_equal))

                def sigmoid():
                    dve.wait_ge(d_ex, n + 1)
                    own.done(dve.tensor_scalar(g4[:, 2, :, :], g4[:, 0, :, :], 1.0, None, ALU.add))

                def then(op):
                    def step():
                        own.need(own.n)
                        own.done(op())
                    return step

                def weights():
                    own.need(own.n)
                    apart(dve, dve_passed)
                    dve.tensor_copy(cs[:, :, 0:E2], cwh[:, :, :].bitcast(F32))
                    dve.tensor_tensor(cs[:, :, E2:2 * E2], g4[:, 5, :, :], cwh[:, :, :].bitcast(F32),
                                      op=ALU.subtract).then_inc(d_cs, 1)
                    assert own.n == DVE_D, own.n

                return [norm, high, low, affinity, biased, largest, replaced, chosen, sigmoid,
                        then(lambda: dve.reciprocal(g4[:, 3, :, :], g4[:, 2, :, :])),
                        then(lambda: dve.tensor_tensor(g4[:, 4, :, :], g4[:, 3, :, :], g4[:, 1, :, :], op=ALU.mult)),
                        then(lambda: dve.tensor_reduce(s4[:, 0, :], g4[:, 4, :, :], axis=AX.X, op=ALU.add)),
                        then(lambda: dve.tensor_scalar(s4[:, 1, :], s4[:, 0, :], 1e-8, None, ALU.add)),
                        then(lambda: dve.reciprocal(s4[:, 2, :], s4[:, 1, :])),
                        then(lambda: dve.tensor_tensor(g4[:, 5, :, :], g4[:, 4, :, :],
                                                       s4[:, 2, :].unsqueeze(2).broadcast_to([P, SUB, E2]), op=ALU.mult)),
                        then(lambda: dve.tensor_scalar(cwh[:, :, :], g4[:, 5, :, :], 0.0, None, ALU.add)),
                        weights]

            STEP_AT = (10, 13, 14, 15, 16, 17, 18, 19, 20, 21, 22, 23, 24, 25, 26, 27, 28)
            for n in range(2):
                x4_stats(n, n)
            for step in routing(0, 0):
                step()

            def e_h(t, u):
                dve.wait_ge(u_sg, t * NP2 + u)
                dve.wait_ge(u_cw, t * NP2 + u)
                if u >= 3 or not (isinstance(t, int) and t == 0):
                    is_split(dve, t, u - 3)
                dve.tensor_tensor(h4[:, u % 3, :], sg4[:, u % 3, :], bank[3 + u % 2][:, :], op=ALU.mult).then_inc(u_h, 1)

            def e_lo(t, u):
                if u % 2:
                    return
                r = slice(0, F2 if u == 0 else P)
                dve.wait_ge(u_hh, t * NU + u + 1)
                dve.tensor_tensor(hl4[r, u % 3, :], h4[r, u % 3, :], hh4[r, u % 3, :].bitcast(F32),
                                  op=ALU.subtract).then_inc(u_hl, 1)

            def result(t, p, stored=0):
                dve.wait_ge(u_T, t + 1)
                if not isinstance(t, int) or t >= 2:
                    dve.wait_ge(o_out[p], stored * 16 + 16)
                dve.tensor_tensor(y4[:, p, :, :], bank[6][:, :].rearrange("p (k d) -> p k d", k=SUB),
                                  x_res[:, ds(t * SUB, SUB), :], op=ALU.add).then_inc(u_y, 1)

            def dve_tile(t, p, before, N, S):
                steps = dict(zip(STEP_AT, routing(t + 1, 1 - p))) if N else {}
                if before is not None:
                    e_lo(before[0], NU - 1)
                for u in range(1, NU):
                    e_h(t, u)
                    e_lo(t, u - 1)
                    if u == 3 and S:
                        x4_stats(t + 2, p)
                    if u == 9 and before is not None:
                        result(*before)
                    if u in steps:
                        steps[u]()

            tiles_of(dve, dve_tile)
            e_lo(T // TT - 1, NU - 1)
            result(T // TT - 1, 1, T // TT // 2 - 1)

        @block.tensor
        def _(pe):
            pe.wait_ge(consts, 1)

            def transposed(src, first_bank, s, made, i, done):
                pe.wait_ge(made, i)
                for k in range(SUB):
                    ins = pe.transpose(bank[first_bank + s][:, k * P:(k + 1) * P], src[:, s, k, :], ident[:, :])
                ins.then_inc(done, 1)

            def pe_pieces(k, one, two):
                i1, i2 = k * 2 + 1, k * 2 - 1
                for s in range(2):
                    if one:
                        transposed(xn, 0, s, xn1, i1 + s, tr1)
                for s in range(2):
                    if one:
                        if isinstance(k, int):
                            pe.wait_ge(small_in, 16 * 10)
                        pe.wait_ge(tc1, i1 + s)
                        for j in range(SUB):
                            ins = pe.matmul(bank[2 + 2 * s + j // 2][:, (j % 2) * M1:(j % 2 + 1) * M1], xnT[:, s, j, :],
                                            w123[:, :], start=True, stop=True)
                        ins.then_inc(zz1, 1)
                for s in range(2):
                    if two:
                        transposed(xm, 6, s, xn2, i2 + s, tr2)
                for s in range(2):
                    if two:
                        pe.wait_ge(tc2, i2 + s)
                        for j in range(SUB):
                            ins = pe.matmul(bank[6 + s][:, j * 16:j * 16 + E1], xmT[:, s, j, :], wr_s[:, :],
                                            start=True, stop=True)
                        ins.then_inc(lg2, 1)
                for s in range(2):
                    if two:
                        pe.wait_ge(sl2, i2 + s)
                        for a in range(SUB + 1):
                            o = bank[6 + s][:, 16 * SUB + a * E1:16 * SUB + (a + 1) * E1]
                            for j in range(a):
                                ins = pe.matmul(o, ones[:, :], sel[:, s, j, :], start=j == 0, stop=(a == SUB and j == a - 1))
                            if a < SUB:
                                ins = pe.matmul(o, tri[:, :], sel[:, s, a, :], start=a == 0, stop=True)
                        ins.then_inc(rk2, 1)

            pieces(pe, pe_pieces)

            def x_T(b, u, loads):
                pe.wait_ge(xb_in[u], 16 * loads)
                if not isinstance(b, int) or b > 0:
                    pe.wait_ge(xl_r, b)
                pe.transpose(bank[0][:, 0:P], xb[:, u, :], ident[:, :]).then_inc(xT_r, 1)

            def expert_of(b):
                return pe.value_load(blk_e[0:1, ds(b, 1)], min_val=0, max_val=E1 - 1)

            kept = [pe.alloc_register(f"expert{v}") for v in range(2)]

            def up(b, v):
                e = expert_of(b)
                if isinstance(b, int):
                    pe.wait_ge(xl_r, b + 1)
                for o, hi, lo in ((bank[4 + v], wgh, wgl), (bank[6 + v], wuh, wul)):
                    w = ds(e * I1, I1)
                    pe.matmul(o[:, 0:I1], xbh[:, v, :], hi[:, w], start=True, stop=False)
                    pe.matmul(o[:, 0:I1], xbh[:, v, :], lo[:, w], start=False, stop=False)
                    ins = pe.matmul(o[:, 0:I1], xbl[:, v, :], hi[:, w], start=False, stop=True)
                ins.then_inc(gu_r, 1)
                return e

            def h_T(b, v):
                pe.wait_ge(h_r, b + 1)
                for j in range(JC):
                    ins = pe.transpose(bank[2 + v][:, j * P:(j + 1) * P], hb[:, v, j * P:(j + 1) * P], ident[:, :])
                ins.then_inc(hT_r, 1)

            def down(b, v, first):
                e = pe.snap(kept[v], min_val=0, max_val=E1 - 1)
                pe.wait_ge(hl_r, b + 1)
                if not first:
                    pe.wait_ge(yb_r, b)
                o = bank[1][:, 0:2 * D]
                for j in range(JC):
                    r = min(P, I1 - j * P)
                    w = wdf[0:r, ds(e * (JC * 2 * D) + j * 2 * D, 2 * D)]
                    pe.matmul(o, hh[0:r, v, j * P:(j + 1) * P], w, start=j == 0, stop=False)
                    ins = pe.matmul(o, hl[0:r, v, j * P:(j + 1) * P], w, start=False, stop=j == JC - 1)
                ins.then_inc(y_r, 1)

            pe.wait_ge(consts, 2)
            pe.wait_ge(w_hi, 3 * (NPIECE // 2 - 1))
            pe.wait_ge(w_lo, 3 * (NPIECE // 2 - 1))
            pe.wait_ge(list_ready, 1)
            x_T(0, 0, 1)
            for b in range(4):
                x_T(b + 1, (b + 1) % 4, (b + 1) // 4 + 1)
                e = up(b, b % 2)
                if b >= 1:
                    h_T(b - 1, (b - 1) % 2)
                if b >= 2:
                    down(b - 2, b % 2, b == 2)
                pe.reg_mov(kept[b % 2], e)
            with pe.Fori(1, NBLK // 4 - 1) as it:
                for u in range(4):
                    b = it * 4 + u
                    x_T(b + 1, (u + 1) % 4, it + 1 if u < 3 else it + 2)
                    e = up(b, u % 2)
                    h_T(b - 1, (u - 1) % 2)
                    down(b - 2, u % 2, False)
                    pe.reg_mov(kept[u % 2], e)
            for b in range(NBLK - 4, NBLK + 2):
                if b + 1 < NBLK:
                    x_T(b + 1, (b + 1) % 4, (b + 1) // 4 + 1)
                if b < NBLK:
                    e = up(b, b % 2)
                if b - 1 < NBLK:
                    h_T(b - 1, (b - 1) % 2)
                down(b - 2, b % 2, False)
                if b < NBLK:
                    pe.reg_mov(kept[b % 2], e)

            pe.wait_ge(c_in, 16 * 8)
            pe.wait_ge(c_w, 6)

            def pe_turn(i, half, p, E, F, M, P1, G):
                b1, b2 = i + 1, i + 2

                def turned(src, q, first_bank, groups):
                    for g in groups:
                        o = bank[first_bank + (g - groups[0]) // 2][:, (g % 2) * 2 * P:(g % 2 + 1) * 2 * P]
                        for u in range(2):
                            ins = pe.matmul(o, src[:, q, u, 4 * g:4 * g + 4, :].rearrange("p h w -> p (h w)"),
                                            idr[:, 1 - u:3 - u, :].rearrange("p a k -> p (a k)"),
                                            start=u == 0, stop=u == 1)
                    return ins

                def scores_k(g):
                    if E:
                        if g > 0 or not isinstance(i, int) or i > 0:
                            pe.wait_ge(c_P, i * 4 + g)
                        if g % 2 == 0:
                            pe.wait_ge(c_q2, 2 * i + g // 2 + 1)
                            pe.wait_ge(c_q2d, 2 * i + g // 2 + 1)
                        for o, kb, qb in ((bank[0], 0, 0), (bank[1], 0, 1), (bank[2], 1, 1)):
                            if kb == qb:
                                pe.matmul(o, identb[:, :], msk[:, 1, :, :], start=True, stop=False,
                                          skip_group_check=True)
                            ins = pe.matmul(o.rearrange("p (j k) -> p j k", j=4), kT[:, p, g, kb * P:(kb + 1) * P],
                                            qz[:, g, :, qb * P:(qb + 1) * P], start=kb != qb, stop=True,
                                            skip_group_check=True)
                        ins.then_inc(c_S2, 1)

                def scores_q(g):
                    if M:
                        if g > 0:
                            pe.wait_ge(c_mx, b1 * 4 + g)
                        else:
                            pe.wait_ge(c_qT, b1 + 1)
                            pe.wait_ge(c_kz, b1 + 1)
                            pe.wait_ge(c_kT, b1 + 1)
                        pe.matmul(bank[3], identb[:, :], msk[:, 0, :, :], start=True, stop=False, skip_group_check=True)
                        pe.matmul(bank[3].rearrange("p (j k) -> p j k", j=4), qT[:, g, 0:P], kz[:, g, :, 0:P],
                                  start=False, stop=True, skip_group_check=True)
                        for c in range(2):
                            o = bank[4 + c].rearrange("p (j k) -> p j k", j=4)
                            pe.matmul(o[:, 1:4:2, :], identb[:, :], msk[:, 0, 0:2, :], start=True, stop=False,
                                      skip_group_check=True)
                            ins = pe.matmul(bank[4 + c].rearrange("p (j k) -> p j k", j=2), qT[:, g, P:2 * P],
                                            kz[:, g, 2 * c:2 * c + 2, :], start=False, stop=True, skip_group_check=True)
                        ins.then_inc(c_S1, 1)

                def values(g):
                    if E:
                        pe.wait_ge(c_P, i * 4 + g + 1)
                        if g == 0:
                            pe.wait_ge(c_vp, i + 1)
                            if M:
                                pe.wait_ge(c_qT, b1 + 1)
                            else:
                                pe.wait_ge(c_OT, i * 4)
                        else:
                            pe.wait_ge(c_OT, i * 4 + g)
                        for j in range(4):
                            o = bank[6][j * HW:j * HW + S + 1, 0:2 * P]
                            pe.matmul(o.rearrange("p (b k) -> p b k", b=2), vp[:, p, 0, 4 * g + j, :],
                                      pt[:, g % 2, 0:2, j, :], start=True, stop=False, skip_group_check=True)
                            ins = pe.matmul(o[:, P:2 * P], vp[:, p, 1, 4 * g + j, :], pt[:, g % 2, 2, j, :],
                                            start=False, stop=True, skip_group_check=True)
                        ins.then_inc(c_PV, 1)

                def att_T(u):
                    if F:
                        if u == 1:
                            pe.wait_ge(c_F2, 2 * i - 1)
                        elif E:
                            pe.wait_ge(c_q2, 2 * i + 2)
                            pe.wait_ge(c_q2d, 2 * i + 2)
                        else:
                            pe.wait_ge(c_F6, i)
                        if u == 0:
                            pe.wait_ge(c_OT, i * 4)
                        for g in range(4):
                            ins = pe.transpose(bank[7][:, g * P:(g + 1) * P], ot[:, 1 - p, g, u * P:(u + 1) * P], ident[:, :])
                        ins.then_inc(c_F1, 1)

                def qkv(u):
                    if P1:
                        if u:
                            pe.wait_ge(c_zs, 2 * b2 + 1)
                        else:
                            pe.wait_ge(c_xl, b2 + 1)
                        o = bank[7][:, 0:3 * D]
                        pe.matmul(o, xch[:, u, :], wqh[:, :], start=True, stop=False)
                        pe.matmul(o, xch[:, u, :], wql[:, :], start=False, stop=False)
                        pe.matmul(o, xcl[:, u, :], wqh[:, :], start=False, stop=True).then_inc(c_z, 1)

                def with_maxima(q, b, c):
                    pe.wait_ge(c_nm, 2 * b + c + 1)
                    turned(qs, q, 7, (2 * c, 2 * c + 1)).then_inc(c_T2, 1)

                if isinstance(i, int) and i == -1:
                    pe.wait_ge(c_const, 1)
                    pe.wait_ge(c_w, 7)
                if M:
                    pe.wait_ge(c_dup, b1 + 1)
                    pe.wait_ge(c_lo, b1 + 1)
                    if not isinstance(i, int) or i > -1:
                        pe.wait_ge(c_mx, b1 * 4)
                    turned(ks, 1 - p, 3, range(4)).then_inc(c_T3, 1)
                if P1:
                    pe.wait_ge(c_xn, b2 + 1)
                    if not isinstance(i, int) or i > 0:
                        pe.wait_ge(c_F6, i)
                    elif i > -2:
                        pe.wait_ge(c_zs, 2 * b2)
                    if E:
                        pe.wait_ge(c_q2, 2 * i + 1)
                        pe.wait_ge(c_q2d, 2 * i + 1)
                    for u in range(2):
                        ins = pe.transpose(bank[7][:, u * P:(u + 1) * P], xc[:, u, :], ident[:, :])
                    ins.then_inc(c_xT, 1)
                if M:
                    if not isinstance(i, int) or i > 0:
                        pe.wait_ge(c_OT, i * 4)
                    turned(qs, 1 - p, 5, range(4)).then_inc(c_T, 1)
                scores_k(0)
                qkv(0)
                scores_q(0)
                scores_k(1)
                qkv(1)
                values(0)
                if E:
                    if P1:
                        pe.wait_ge(c_zs, 2 * i + 6)
                    else:
                        pe.wait_ge(c_F6, i)
                    with_maxima(p, i, 1)
                scores_q(1)
                values(1)
                scores_k(2)
                att_T(0)
                values(2)
                att_T(1)
                scores_q(2)
                if F:
                    pe.wait_ge(c_F2, 2 * i)
                    for u in range(2):
                        ins = pe.transpose(bank[7][:, u * P:(u + 1) * P], oo[:, u, :], ident[:, :])
                    ins.then_inc(c_F3, 1)
                scores_k(3)
                if M:
                    if F:
                        pe.wait_ge(c_F4, i)
                    elif E:
                        pe.wait_ge(c_q2, 2 * i + 2)
                        pe.wait_ge(c_q2d, 2 * i + 2)
                    else:
                        pe.wait_ge(c_zs, 2 * i + 6)
                    with_maxima(1 - p, b1, 0)
                scores_q(3)
                values(3)
                if F:
                    if M:
                        pe.wait_ge(c_q2, 2 * b1 + 1)
                        pe.wait_ge(c_q2d, 2 * b1 + 1)
                    pe.wait_ge(c_F4, i)
                    for u in range(2):
                        ins = pe.matmul(bank[7][:, u * D:(u + 1) * D], ooT[:, u, :], wuT[:, :], start=True, stop=True)
                    ins.then_inc(c_F5, 1)

            turns(pe_turn, pe)

            def x4_turned(n, free):
                pe.wait_ge(d_xn, n + 1)
                if free is not None:
                    pe.wait_ge(u_y, free)
                for k in range(SUB):
                    ins = pe.transpose(bank[6][:, k * P:(k + 1) * P], xm4[:, k, :], ident[:, :])
                ins.then_inc(d_T, 1)

            def x4_logits(n):
                pe.wait_ge(d_Tc, n + 1)
                for k in range(SUB):
                    ins = pe.matmul(bank[6][:, k * E2:(k + 1) * E2], xnT4[:, k, :], cen_s[:, :], start=True, stop=True)
                ins.then_inc(d_af, 1)

            def x4_weights(n):
                pe.wait_ge(d_cs, n + 1)
                for k in range(SUB):
                    ins = pe.transpose(bank[6][:, k * P:(k + 1) * P], cs[:, k, :], ident[:, :])
                ins.then_inc(d_cT, 1)

            pe.wait_ge(sh_in, 16 * 4)
            x4_turned(0, None)
            x4_logits(0)
            x4_weights(0)

            pe.wait_ge(d_const, 3)
            pe.wait_ge(sh_done, 4)
            pe.wait_ge(wd_done, NC)

            def e_up(t, p, u):
                if u == 0:
                    pe.wait_ge(d_hl, t + 1)
                    pe.wait_ge(d_cw, t + 1)
                first = isinstance(t, int) and t == 0
                if u >= 3:
                    pe.wait_ge(u_sg, t * NP2 + u - 3)
                    if u == 3:
                        pe.wait_ge(u_sg0, t + 1)
                elif not first:
                    pe.wait_ge(u_sg, (t - 1) * NP2 + NU + u - 3)
                if u == 0:
                    o, hi, lo = bank[0][0:F2, :], shh[:, 0:F2], shl[:, 0:F2]
                else:
                    c = slice((u - 1) * P, u * P)
                    o, hi, lo = bank[u % 3][:, :], wh[:, c], wl[:, c]
                pe.matmul(o, hi, xh4[:, p, :], start=True, stop=False)
                pe.matmul(o, hi, xl4[:, p, :], start=False, stop=False)
                pe.matmul(o, lo, xh4[:, p, :], start=False, stop=True).then_inc(u_up, 1)
                if u > 0:
                    if u > 2:
                        pe.wait_ge(u_h, t * NP2 + u - 2)
                    elif not first:
                        pe.wait_ge(u_h, (t - 1) * NP2 + NP2 + u - 2)
                    pe.matmul(bank[3 + u % 2][:, :], selr[:, 2 * u - 2:2 * u, :].rearrange("p e f -> p (e f)"), cwT[:, p, :], start=True, stop=True).then_inc(u_cw, 1)

            def e_down(t, p, u):
                if u == 0 and not (isinstance(t, int) and t < 2):
                    pe.wait_ge(u_oT, t - 1)
                is_split(pe, t, u)
                if u == 0:
                    r, hi, lo = slice(0, F2), shh[0:F2, F2:F2 + D], shl[0:F2, F2:F2 + D]
                else:
                    c = slice(E2 * F2 + (u - 1) * D, E2 * F2 + u * D)
                    r, hi, lo = slice(0, P), wh[:, c], wl[:, c]
                o = bank[5 + 2 * p][:, :]
                pe.matmul(o, hi, hh4[r, u % 3, :], start=u == 0, stop=False)
                pe.matmul(o, hi, hl4[r, u % 3, :], start=False, stop=False)
                ins = pe.matmul(o, lo, hh4[r, u % 3, :], start=False, stop=u == NU - 1)
                ins.then_inc(u_dn, 1)

            def out_T(t):
                pe.wait_ge(u_oT, t + 1)
                if isinstance(t, int) and t == T // TT - 1:
                    pe.wait_ge(u_y, t)
                for k in range(SUB):
                    ins = pe.transpose(bank[6][:, k * P:(k + 1) * P], oT4[:, k * P:(k + 1) * P], ident[:, :])
                ins.then_inc(u_T, 1)

            LAG = 3

            def pe_tile(t, p, before, N, S):
                for u in range(NU):
                    e_up(t, p, u)
                    if u >= LAG:
                        e_down(t, p, u - LAG)
                    elif before is not None:
                        e_down(before[0], 1 - p, NU + u - LAG)
                    if u == 7 and before is not None:
                        out_T(before[0])
                    if u == 12 and N:
                        x4_turned(t + 1, t if before is not None else None)
                    if u == 14 and N:
                        x4_logits(t + 1)
                    if u == 30 and N:
                        x4_weights(t + 1)

            tiles_of(pe, pe_tile)
            for u in range(NU - LAG, NU):
                e_down(T // TT - 1, 1, u)
            out_T(T // TT - 1)


_INS = ['L0_attn_x', 'L0_attn_W1', 'L0_attn_b1', 'L0_attn_W2', 'L0_attn_b2', 'L0_attn_W3', 'L0_attn_b3',
        'L0_ffn_Wr', 'L0_ffn_Wg', 'L0_ffn_Wu', 'L0_ffn_Wd', 'L1_attn_Wk', 'L1_attn_Wq', 'L1_attn_Wv', 'L1_attn_Wu',
        'L1_attn_kln_w', 'L1_attn_kln_b', 'L1_attn_qln_w', 'L1_attn_qln_b', 'L1_ffn_centroids', 'L1_ffn_expert_biases',
        'L1_ffn_Ws_up', 'L1_ffn_Ws_down', 'L1_ffn_W_up', 'L1_ffn_W_down']
_TURNED = ('L1_attn_Wk', 'L1_attn_Wq', 'L1_attn_Wv', 'L1_attn_Wu', 'L1_ffn_centroids')
_OUTS = [((16, 256, 128), 'float32')]


def kernel(**inputs):
    import numpy as _np
    import concourse.bacc as _bacc
    from concourse import mybir as _mybir
    from concourse.bass_utils import run_bass_kernel_spmd as _run

    nc = _bacc.Bacc("TRN2", target_bir_lowering=False, num_devices=1)
    arrays, args = {}, []
    for name in _INS:
        a = _np.asarray(inputs[name])
        a = _np.ascontiguousarray(a.T if name in _TURNED else a)
        arrays[f"in_{name}_dram"] = a
        args.append(nc.dram_tensor(f"in_{name}_dram", a.shape, _mybir.dt.from_np(a.dtype), kind="ExternalInput").ap())
    for i, (shape, dtype) in enumerate(_OUTS):
        dt = _mybir.dt.from_np(_np.dtype(dtype))
        args.append(nc.dram_tensor(f"out_{i}_dram", shape, dt, kind="ExternalOutput").ap())
    bass_two_layers(nc, *args)
    r = _run(nc, [arrays], core_ids=[0])
    got = tuple(r.results[0][f"out_{i}_dram"] for i in range(len(_OUTS)))
    return got[0]
```
